# Optimizing a Trainium2 kernel written in Bass

```python
import numpy as np
import jax
import jax.numpy as jnp

def _softmax(x, axis=-1):
    return jax.nn.softmax(x, axis=axis)

def _gelu(x):
    return jax.nn.gelu(x, approximate=True)

def _silu(x):
    return jax.nn.silu(x)

def _sigmoid(x):
    return jax.nn.sigmoid(x)

def _layernorm(x, axis=-1, eps=1e-05):
    m = jnp.mean(x, axis=axis, keepdims=True)
    v = jnp.var(x, axis=axis, keepdims=True)
    return (x - m) / jnp.sqrt(v + eps)

def _scatter_add(tgt, idx, src, axis=0):
    return tgt.at[idx].add(src)

def _segment_sum(src, seg, n):
    return jax.ops.segment_sum(src, seg, n)
kernel_name = 'mk_audio_tower_d2_tok_audfeat512_r4_c654dd'

def setup_inputs(seed: int=0):
    np.random.seed(seed)
    _w = jnp.asarray

    def _rec_inputs():
        import jax
        import jax.numpy as jnp
        _rk = jax.random.key(seed)
        x = 3.78913e-05 + 1.00016 * jax.random.normal(jax.random.fold_in(_rk, 1), (16, 256, 64), jnp.float32)
        return x
    x = _rec_inputs()

    def _L0_tok_setup():
        import jax, jax.numpy as jnp
        import numpy as np
        CONTEXT = 5
        DILATION = 1
        EPS = 1e-05
        key = jax.random.key(seed)
        k1, k2, k3 = jax.random.split(key, 3)
        B, T, D, O = (64, 500, 64, 128)
        x = jax.random.normal(k1, (B, T, D), dtype=jnp.float32)
        K = D * CONTEXT
        W = jax.random.normal(k2, (O, K), dtype=jnp.float32) / np.sqrt(K).astype(np.float32)
        b = jax.random.normal(k3, (O,), dtype=jnp.float32) * 0.01
        gamma = jnp.ones((O,), dtype=jnp.float32)
        beta = jnp.zeros((O,), dtype=jnp.float32)
        return {'x': x, 'W': W, 'b': b, 'gamma': gamma, 'beta': beta}
    _L0_tok_all = _L0_tok_setup()
    _L0_tok_in = {k: v for k, v in _L0_tok_all.items() if k in ('W', 'b', 'gamma', 'beta')}
    del _L0_tok_all

    def _L0_attn_setup():
        import jax, jax.numpy as jnp
        import numpy as np
        EMBED = 128
        HEADS = 8
        HD = EMBED // HEADS // 2
        EXP = 4
        DEPTH = 1
        LAMBDA_INIT = 0.8 - 0.6 * float(np.exp(-0.3 * (DEPTH - 1)))
        EPS = 1e-05

        def layernorm(x, w, b):
            mu = jnp.mean(x, axis=-1, keepdims=True)
            var = jnp.mean(jnp.square(x - mu), axis=-1, keepdims=True)
            return (x - mu) * jax.lax.rsqrt(var + EPS) * w + b

        def rmsnorm(x, w):
            ms = jnp.mean(jnp.square(x), axis=-1, keepdims=True)
            return x * jax.lax.rsqrt(ms + EPS) * w

        def diff_attn(x, Wq, Wk, Wv, Wo, lq1, lk1, lq2, lk2, subln_w):
            B, N, D = x.shape
            q = (x @ Wq.T).reshape(B, N, 2 * HEADS, HD).transpose(0, 2, 1, 3)
            k = (x @ Wk.T).reshape(B, N, 2 * HEADS, HD).transpose(0, 2, 1, 3)
            v = (x @ Wv.T).reshape(B, N, HEADS, 2 * HD).transpose(0, 2, 1, 3)
            q = q * HD ** (-0.5)
            scores = jnp.einsum('bhnd,bhmd->bhnm', q, k)
            attn = jax.nn.softmax(scores, axis=-1)
            attn = attn.reshape(B, HEADS, 2, N, N)
            lam1 = jnp.exp(jnp.sum(lq1 * lk1))
            lam2 = jnp.exp(jnp.sum(lq2 * lk2))
            lam = lam1 - lam2 + LAMBDA_INIT
            attn = attn[:, :, 0] - lam * attn[:, :, 1]
            out = jnp.einsum('bhnm,bhmd->bhnd', attn, v)
            out = rmsnorm(out, subln_w) * (1.0 - LAMBDA_INIT)
            out = out.transpose(0, 2, 1, 3).reshape(B, N, D)
            return out @ Wo.T
        key = jax.random.key(seed)
        ks = jax.random.split(key, 12)
        B, N, D = (8, 256, EMBED)
        s = 0.02
        inp = {'x': jax.random.normal(ks[0], (B, N, D), jnp.float32), 'Wq': jax.random.normal(ks[1], (D, D), jnp.float32) * s, 'Wk': jax.random.normal(ks[2], (D, D), jnp.float32) * s, 'Wv': jax.random.normal(ks[3], (D, D), jnp.float32) * s, 'Wo': jax.random.normal(ks[4], (D, D), jnp.float32) * s, 'lq1': jax.random.normal(ks[5], (HD,), jnp.float32) * 0.1, 'lk1': jax.random.normal(ks[6], (HD,), jnp.float32) * 0.1, 'lq2': jax.random.normal(ks[7], (HD,), jnp.float32) * 0.1, 'lk2': jax.random.normal(ks[8], (HD,), jnp.float32) * 0.1, 'subln_w': jnp.ones((2 * HD,), jnp.float32), 'n1_w': jnp.ones((D,), jnp.float32), 'n1_b': jnp.zeros((D,), jnp.float32), 'n2_w': jnp.ones((D,), jnp.float32), 'n2_b': jnp.zeros((D,), jnp.float32), 'mln1_w': jnp.ones((D,), jnp.float32), 'mln1_b': jnp.zeros((D,), jnp.float32), 'mW1': jax.random.normal(ks[9], (EXP * D, D), jnp.float32) * s, 'mb1': jnp.zeros((EXP * D,), jnp.float32), 'mln2_w': jnp.ones((EXP * D,), jnp.float32), 'mln2_b': jnp.zeros((EXP * D,), jnp.float32), 'mW2': jax.random.normal(ks[10], (D, EXP * D), jnp.float32) * s, 'mb2': jnp.zeros((D,), jnp.float32)}
        return inp
    _L0_attn_all = _L0_attn_setup()
    _L0_attn_in = {k: v for k, v in _L0_attn_all.items() if k in ('Wq', 'Wk', 'Wv', 'Wo', 'lq1', 'lk1', 'lq2', 'lk2', 'subln_w', 'n1_w', 'n1_b', 'n2_w', 'n2_b', 'mln1_w', 'mln1_b', 'mW1', 'mb1', 'mln2_w', 'mln2_b', 'mW2', 'mb2')}
    del _L0_attn_all

    def _L0_ffn_setup():
        import jax, jax.numpy as jnp
        import numpy as np
        EPS = 1e-05
        NUM_HEADS = 8
        TOP_K = 2
        CAP_FACTOR = 2

        def layernorm(x, g, b):
            m = jnp.mean(x, axis=-1, keepdims=True)
            v = jnp.var(x, axis=-1, keepdims=True)
            return (x - m) * jax.lax.rsqrt(v + EPS) * g + b
        key = jax.random.key(seed)
        ks = jax.random.split(key, 16)
        B, S, H, E, F = (2, 512, 128, 64, 512)
        s = 0.02
        return {'x': jax.random.normal(ks[0], (B, S, H), jnp.float32), 'ln1_g': jnp.ones((H,), jnp.float32), 'ln1_b': jnp.zeros((H,), jnp.float32), 'wq': jax.random.normal(ks[1], (H, H), jnp.float32) * s, 'wk': jax.random.normal(ks[2], (H, H), jnp.float32) * s, 'wv': jax.random.normal(ks[3], (H, H), jnp.float32) * s, 'wo': jax.random.normal(ks[4], (H, H), jnp.float32) * s, 'ln2_g': jnp.ones((H,), jnp.float32), 'ln2_b': jnp.zeros((H,), jnp.float32), 'wr': jax.random.normal(ks[5], (H, E), jnp.float32) * s, 'w1': jax.random.normal(ks[6], (E, H, F), jnp.float32) * s, 'b1': jnp.zeros((E, F), jnp.float32), 'w2': jax.random.normal(ks[7], (E, F, H), jnp.float32) * s, 'b2': jnp.zeros((E, H), jnp.float32)}
    _L0_ffn_all = _L0_ffn_setup()
    _L0_ffn_in = {k: v for k, v in _L0_ffn_all.items() if k in ('ln1_g', 'ln1_b', 'wq', 'wk', 'wv', 'wo', 'ln2_g', 'ln2_b', 'wr', 'w1', 'b1', 'w2', 'b2')}
    del _L0_ffn_all

    def _L1_attn_setup():
        import jax, jax.numpy as jnp
        import numpy as np
        B, S, IN, HD, H = (2, 512, 128, 32, 16)
        key = jax.random.key(seed)
        ks = jax.random.split(key, 9)
        sc = 0.02
        return {'x': jax.random.normal(ks[0], (B, S, IN), jnp.float32), 'Wl': jax.random.normal(ks[1], (H, IN, IN), jnp.float32) * sc, 'bl': jax.random.normal(ks[2], (H, IN), jnp.float32) * sc, 'Wq': jax.random.normal(ks[3], (H, IN, HD), jnp.float32) * sc, 'Wk': jax.random.normal(ks[4], (H, IN, HD), jnp.float32) * sc, 'Wv': jax.random.normal(ks[5], (H, IN, HD), jnp.float32) * sc, 'Wo': jax.random.normal(ks[6], (IN, H * HD), jnp.float32) * sc, 'bo': jax.random.normal(ks[7], (IN,), jnp.float32) * sc}
    _L1_attn_all = _L1_attn_setup()
    _L1_attn_in = {k: v for k, v in _L1_attn_all.items() if k in ('Wl', 'bl', 'Wq', 'Wk', 'Wv', 'Wo', 'bo')}
    del _L1_attn_all

    def _L1_ffn_setup():
        import jax, jax.numpy as jnp
        import numpy as np
        B, S, D, F, E, TOP_K = (8, 1024, 128, 256, 16, 2)
        LN_EPS = 1e-05
        key = jax.random.key(seed)
        ks = jax.random.split(key, 5)
        s = 0.02
        x = jax.random.normal(ks[0], (B, S, D), dtype=jnp.float32)
        gate_w = jax.random.normal(ks[1], (D, E), dtype=jnp.float32) * s
        gate_b = jnp.zeros((E,), jnp.float32)
        w1 = jax.random.normal(ks[2], (E, D, F), dtype=jnp.float32) * s
        b1 = jnp.zeros((E, F), jnp.float32)
        w2 = jax.random.normal(ks[3], (E, F, D), dtype=jnp.float32) * s
        b2 = jnp.zeros((E, D), jnp.float32)
        gamma = jnp.ones((E, D), jnp.float32)
        beta = jnp.zeros((E, D), jnp.float32)
        return {'x': x, 'gate_w': gate_w, 'gate_b': gate_b, 'w1': w1, 'b1': b1, 'w2': w2, 'b2': b2, 'gamma': gamma, 'beta': beta}
    _L1_ffn_all = _L1_ffn_setup()
    _L1_ffn_in = {k: v for k, v in _L1_ffn_all.items() if k in ('gate_w', 'gate_b', 'w1', 'b1', 'w2', 'b2', 'gamma', 'beta')}
    del _L1_ffn_all
    return {'x': x, 'L0_tok_W': _L0_tok_in['W'], 'L0_tok_b': _L0_tok_in['b'], 'L0_tok_gamma': _L0_tok_in['gamma'], 'L0_tok_beta': _L0_tok_in['beta'], 'L0_attn_Wq': _L0_attn_in['Wq'], 'L0_attn_Wk': _L0_attn_in['Wk'], 'L0_attn_Wv': _L0_attn_in['Wv'], 'L0_attn_Wo': _L0_attn_in['Wo'], 'L0_attn_lq1': _L0_attn_in['lq1'], 'L0_attn_lk1': _L0_attn_in['lk1'], 'L0_attn_lq2': _L0_attn_in['lq2'], 'L0_attn_lk2': _L0_attn_in['lk2'], 'L0_attn_subln_w': _L0_attn_in['subln_w'], 'L0_attn_n1_w': _L0_attn_in['n1_w'], 'L0_attn_n1_b': _L0_attn_in['n1_b'], 'L0_attn_n2_w': _L0_attn_in['n2_w'], 'L0_attn_n2_b': _L0_attn_in['n2_b'], 'L0_attn_mln1_w': _L0_attn_in['mln1_w'], 'L0_attn_mln1_b': _L0_attn_in['mln1_b'], 'L0_attn_mW1': _L0_attn_in['mW1'], 'L0_attn_mb1': _L0_attn_in['mb1'], 'L0_attn_mln2_w': _L0_attn_in['mln2_w'], 'L0_attn_mln2_b': _L0_attn_in['mln2_b'], 'L0_attn_mW2': _L0_attn_in['mW2'], 'L0_attn_mb2': _L0_attn_in['mb2'], 'L0_ffn_ln1_g': _L0_ffn_in['ln1_g'], 'L0_ffn_ln1_b': _L0_ffn_in['ln1_b'], 'L0_ffn_wq': _L0_ffn_in['wq'], 'L0_ffn_wk': _L0_ffn_in['wk'], 'L0_ffn_wv': _L0_ffn_in['wv'], 'L0_ffn_wo': _L0_ffn_in['wo'], 'L0_ffn_ln2_g': _L0_ffn_in['ln2_g'], 'L0_ffn_ln2_b': _L0_ffn_in['ln2_b'], 'L0_ffn_wr': _L0_ffn_in['wr'], 'L0_ffn_w1': _L0_ffn_in['w1'], 'L0_ffn_b1': _L0_ffn_in['b1'], 'L0_ffn_w2': _L0_ffn_in['w2'], 'L0_ffn_b2': _L0_ffn_in['b2'], 'L1_attn_Wl': _L1_attn_in['Wl'], 'L1_attn_bl': _L1_attn_in['bl'], 'L1_attn_Wq': _L1_attn_in['Wq'], 'L1_attn_Wk': _L1_attn_in['Wk'], 'L1_attn_Wv': _L1_attn_in['Wv'], 'L1_attn_Wo': _L1_attn_in['Wo'], 'L1_attn_bo': _L1_attn_in['bo'], 'L1_ffn_gate_w': _L1_ffn_in['gate_w'], 'L1_ffn_gate_b': _L1_ffn_in['gate_b'], 'L1_ffn_w1': _L1_ffn_in['w1'], 'L1_ffn_b1': _L1_ffn_in['b1'], 'L1_ffn_w2': _L1_ffn_in['w2'], 'L1_ffn_b2': _L1_ffn_in['b2'], 'L1_ffn_gamma': _L1_ffn_in['gamma'], 'L1_ffn_beta': _L1_ffn_in['beta']}

def reference(x, L0_tok_W, L0_tok_b, L0_tok_gamma, L0_tok_beta, L0_attn_Wq, L0_attn_Wk, L0_attn_Wv, L0_attn_Wo, L0_attn_lq1, L0_attn_lk1, L0_attn_lq2, L0_attn_lk2, L0_attn_subln_w, L0_attn_n1_w, L0_attn_n1_b, L0_attn_n2_w, L0_attn_n2_b, L0_attn_mln1_w, L0_attn_mln1_b, L0_attn_mW1, L0_attn_mb1, L0_attn_mln2_w, L0_attn_mln2_b, L0_attn_mW2, L0_attn_mb2, L0_ffn_ln1_g, L0_ffn_ln1_b, L0_ffn_wq, L0_ffn_wk, L0_ffn_wv, L0_ffn_wo, L0_ffn_ln2_g, L0_ffn_ln2_b, L0_ffn_wr, L0_ffn_w1, L0_ffn_b1, L0_ffn_w2, L0_ffn_b2, L1_attn_Wl, L1_attn_bl, L1_attn_Wq, L1_attn_Wk, L1_attn_Wv, L1_attn_Wo, L1_attn_bo, L1_ffn_gate_w, L1_ffn_gate_b, L1_ffn_w1, L1_ffn_b1, L1_ffn_w2, L1_ffn_b2, L1_ffn_gamma, L1_ffn_beta):
    import jax
    import jax.numpy as jnp

    def _L0_tok_ref(x, W, b, gamma, beta):
        import jax, jax.numpy as jnp
        import numpy as np
        CONTEXT = 5
        DILATION = 1
        EPS = 1e-05
        B, T, D = x.shape
        new_T = T - DILATION * (CONTEXT - 1)
        win = jnp.concatenate([x[:, i * DILATION:i * DILATION + new_T, :] for i in range(CONTEXT)], axis=-1)
        y = jnp.einsum('btk,ok->bto', win, W) + b
        y = jax.nn.relu(y)
        mean = jnp.mean(y, axis=(0, 1))
        var = jnp.mean(jnp.square(y - mean), axis=(0, 1))
        y = (y - mean) * jax.lax.rsqrt(var + EPS) * gamma + beta
        return y

    def _L0_attn_ref(x, Wq, Wk, Wv, Wo, lq1, lk1, lq2, lk2, subln_w, n1_w, n1_b, n2_w, n2_b, mln1_w, mln1_b, mW1, mb1, mln2_w, mln2_b, mW2, mb2):
        import jax, jax.numpy as jnp
        import numpy as np
        EMBED = 128
        HEADS = 8
        HD = EMBED // HEADS // 2
        EXP = 4
        DEPTH = 1
        LAMBDA_INIT = 0.8 - 0.6 * float(np.exp(-0.3 * (DEPTH - 1)))
        EPS = 1e-05

        def layernorm(x, w, b):
            mu = jnp.mean(x, axis=-1, keepdims=True)
            var = jnp.mean(jnp.square(x - mu), axis=-1, keepdims=True)
            return (x - mu) * jax.lax.rsqrt(var + EPS) * w + b

        def rmsnorm(x, w):
            ms = jnp.mean(jnp.square(x), axis=-1, keepdims=True)
            return x * jax.lax.rsqrt(ms + EPS) * w

        def diff_attn(x, Wq, Wk, Wv, Wo, lq1, lk1, lq2, lk2, subln_w):
            B, N, D = x.shape
            q = (x @ Wq.T).reshape(B, N, 2 * HEADS, HD).transpose(0, 2, 1, 3)
            k = (x @ Wk.T).reshape(B, N, 2 * HEADS, HD).transpose(0, 2, 1, 3)
            v = (x @ Wv.T).reshape(B, N, HEADS, 2 * HD).transpose(0, 2, 1, 3)
            q = q * HD ** (-0.5)
            scores = jnp.einsum('bhnd,bhmd->bhnm', q, k)
            attn = jax.nn.softmax(scores, axis=-1)
            attn = attn.reshape(B, HEADS, 2, N, N)
            lam1 = jnp.exp(jnp.sum(lq1 * lk1))
            lam2 = jnp.exp(jnp.sum(lq2 * lk2))
            lam = lam1 - lam2 + LAMBDA_INIT
            attn = attn[:, :, 0] - lam * attn[:, :, 1]
            out = jnp.einsum('bhnm,bhmd->bhnd', attn, v)
            out = rmsnorm(out, subln_w) * (1.0 - LAMBDA_INIT)
            out = out.transpose(0, 2, 1, 3).reshape(B, N, D)
            return out @ Wo.T
        x_res = x
        xn = layernorm(x, n1_w, n1_b)
        a = diff_attn(xn, Wq, Wk, Wv, Wo, lq1, lk1, lq2, lk2, subln_w)
        h = layernorm(a, n2_w, n2_b) + x_res
        z = layernorm(h, mln1_w, mln1_b)
        z = jax.nn.gelu(z @ mW1.T + mb1, approximate=False)
        z = layernorm(z, mln2_w, mln2_b)
        z = z @ mW2.T + mb2
        return z + h

    def _L0_ffn_ref(x, ln1_g, ln1_b, wq, wk, wv, wo, ln2_g, ln2_b, wr, w1, b1, w2, b2):
        import jax, jax.numpy as jnp
        import numpy as np
        EPS = 1e-05
        NUM_HEADS = 8
        TOP_K = 2
        CAP_FACTOR = 2

        def layernorm(x, g, b):
            m = jnp.mean(x, axis=-1, keepdims=True)
            v = jnp.var(x, axis=-1, keepdims=True)
            return (x - m) * jax.lax.rsqrt(v + EPS) * g + b
        B, S, H = x.shape
        NH = NUM_HEADS
        dh = H // NH
        x1 = layernorm(x, ln1_g, ln1_b)
        q = (x1 @ wq).reshape(B, S, NH, dh)
        k = (x1 @ wk).reshape(B, S, NH, dh)
        v = (x1 @ wv).reshape(B, S, NH, dh)
        scores = jnp.einsum('bqhd,bkhd->bhqk', q, k) * dh ** (-0.5)
        p = jax.nn.softmax(scores, axis=-1)
        attn_out = jnp.einsum('bhqk,bkhd->bqhd', p, v).reshape(B, S, H) @ wo
        x = x + attn_out
        x2 = layernorm(x, ln2_g, ln2_b).reshape(B * S, H)
        T = B * S
        E = wr.shape[1]
        C = CAP_FACTOR * (T * TOP_K // E)
        probs = jax.nn.softmax(x2 @ wr, axis=-1)
        gate_v, gate_i = jax.lax.top_k(probs, TOP_K)
        gate_v = gate_v / jnp.sum(gate_v, axis=-1, keepdims=True)
        ef = gate_i.reshape(-1)
        gf = gate_v.reshape(-1)
        oh = jax.nn.one_hot(ef, E, dtype=x2.dtype)
        pos = jnp.sum((jnp.cumsum(oh, axis=0) - oh) * oh, axis=1).astype(jnp.int32)
        keep = (pos < C).astype(x2.dtype)
        posc = jnp.minimum(pos, C - 1)
        tok = jnp.repeat(x2, TOP_K, axis=0) * keep[:, None]
        buf = jnp.zeros((E, C, H), x2.dtype).at[ef, posc].add(tok)
        h = jax.nn.gelu(jnp.einsum('ech,ehf->ecf', buf, w1) + b1[:, None, :])
        y = jnp.einsum('ecf,efh->ech', h, w2) + b2[:, None, :]
        ys = y[ef, posc] * (gf * keep)[:, None]
        moe_out = ys.reshape(T, TOP_K, H).sum(axis=1).reshape(B, S, H)
        return x + moe_out

    def _L1_attn_ref(x, Wl, bl, Wq, Wk, Wv, Wo, bo):
        import jax, jax.numpy as jnp
        import numpy as np
        B, S, IN, HD, H = (2, 512, 128, 32, 16)
        b, s, _ = x.shape
        h, _, hd = Wq.shape
        xh = jnp.einsum('bsi,hoi->bhso', x, Wl) + bl[None, :, None, :]
        Q = jnp.einsum('bhsi,hid->bhsd', xh, Wq)
        K = jnp.einsum('bhsi,hid->bhsd', xh, Wk)
        V = jnp.einsum('bhsi,hid->bhsd', xh, Wv)
        scores = jnp.einsum('bhsd,bhtd->bhst', Q, K)
        causal = jnp.triu(jnp.ones((s, s), dtype=bool), k=1)
        scores = jnp.where(causal[None, None], -jnp.inf, scores)
        A = jax.nn.softmax(scores, axis=-1)
        F = jnp.einsum('bhst,bhtd->bhsd', A, V)
        cat = jnp.transpose(F, (0, 2, 1, 3)).reshape(b, s, h * hd)
        return cat @ Wo.T + bo

    def _L1_ffn_ref(x, gate_w, gate_b, w1, b1, w2, b2, gamma, beta):
        import jax, jax.numpy as jnp
        import numpy as np
        B, S, D, F, E, TOP_K = (8, 1024, 128, 256, 16, 2)
        LN_EPS = 1e-05
        b, s, d = x.shape
        e = gate_w.shape[1]
        xf = x.reshape(-1, d)
        scores = xf @ gate_w + gate_b
        topk_s, topk_i = jax.lax.top_k(scores, TOP_K)
        topk_w = jax.nn.softmax(topk_s, axis=1)
        comb = (jax.nn.one_hot(topk_i, e, dtype=xf.dtype) * topk_w[..., None]).sum(1)
        out = jnp.zeros_like(xf)
        for eid in range(e):
            h = jax.nn.gelu(xf @ w1[eid] + b1[eid], approximate=False)
            y = h @ w2[eid] + b2[eid]
            mu = y.mean(axis=-1, keepdims=True)
            var = ((y - mu) ** 2).mean(axis=-1, keepdims=True)
            y = (y - mu) / jnp.sqrt(var + LN_EPS) * gamma[eid] + beta[eid]
            out = out + comb[:, eid:eid + 1] * y
        return out.reshape(b, s, d)
    h = _L0_tok_ref(x, L0_tok_W, L0_tok_b, L0_tok_gamma, L0_tok_beta)
    h = h + _L0_attn_ref(_layernorm(h, axis=-1), L0_attn_Wq, L0_attn_Wk, L0_attn_Wv, L0_attn_Wo, L0_attn_lq1, L0_attn_lk1, L0_attn_lq2, L0_attn_lk2, L0_attn_subln_w, L0_attn_n1_w, L0_attn_n1_b, L0_attn_n2_w, L0_attn_n2_b, L0_attn_mln1_w, L0_attn_mln1_b, L0_attn_mW1, L0_attn_mb1, L0_attn_mln2_w, L0_attn_mln2_b, L0_attn_mW2, L0_attn_mb2)
    h = h + _L0_ffn_ref(_layernorm(h, axis=-1), L0_ffn_ln1_g, L0_ffn_ln1_b, L0_ffn_wq, L0_ffn_wk, L0_ffn_wv, L0_ffn_wo, L0_ffn_ln2_g, L0_ffn_ln2_b, L0_ffn_wr, L0_ffn_w1, L0_ffn_b1, L0_ffn_w2, L0_ffn_b2)
    h = h + _L1_attn_ref(_layernorm(h, axis=-1), L1_attn_Wl, L1_attn_bl, L1_attn_Wq, L1_attn_Wk, L1_attn_Wv, L1_attn_Wo, L1_attn_bo)
    h = h + _L1_ffn_ref(_layernorm(h, axis=-1), L1_ffn_gate_w, L1_ffn_gate_b, L1_ffn_w1, L1_ffn_b1, L1_ffn_w2, L1_ffn_b2, L1_ffn_gamma, L1_ffn_beta)
    return h

_drawn_inputs = setup_inputs


def setup_inputs(seed=0):
    import zlib

    import numpy as np

    out = dict(_drawn_inputs(seed))
    spreads = {'L0_tok_gamma': (1.0, 0.2),
     'L0_tok_beta': (0.0, 0.1),
     'L0_attn_subln_w': (1.0, 0.2),
     'L0_attn_n1_w': (1.0, 0.2),
     'L0_attn_n1_b': (0.0, 0.1),
     'L0_attn_n2_w': (1.0, 0.2),
     'L0_attn_n2_b': (0.0, 0.1),
     'L0_attn_mln1_w': (1.0, 0.2),
     'L0_attn_mln1_b': (0.0, 0.1),
     'L0_attn_mb1': (0.0, 0.1),
     'L0_attn_mln2_w': (1.0, 0.2),
     'L0_attn_mln2_b': (0.0, 0.1),
     'L0_attn_mb2': (0.0, 0.1),
     'L0_ffn_ln1_g': (1.0, 0.6),
     'L0_ffn_ln1_b': (0.0, 0.583),
     'L0_ffn_ln2_g': (1.0, 0.2),
     'L0_ffn_ln2_b': (0.0, 0.315),
     'L0_ffn_b1': (0.0, 0.432),
     'L0_ffn_b2': (0.0, 0.1),
     'L1_ffn_gate_b': (0.0, 0.1),
     'L1_ffn_b1': (0.0, 0.1),
     'L1_ffn_b2': (0.0, 0.1),
     'L1_ffn_gamma': (1.0, 0.2),
     'L1_ffn_beta': (0.0, 0.394)}
    factors = {'L0_tok_b': 2.99,
     'L0_attn_lq1': 8.0,
     'L0_attn_lk1': 6.169,
     'L0_attn_lq2': 5.388,
     'L0_attn_lk2': 4.97,
     'L0_ffn_wq': 8.0,
     'L0_ffn_wk': 8.0,
     'L1_attn_Wl': 3.874,
     'L1_attn_bl': 8.0,
     'L1_attn_Wq': 8.0,
     'L1_attn_Wk': 8.0,
     'L1_attn_Wv': 3.161,
     'L1_attn_Wo': 3.842,
     'L1_attn_bo': 3.45}
    for name, (base, spread) in spreads.items():
        noise = np.random.default_rng([zlib.crc32(name.encode()), seed]).standard_normal(out[name].shape)
        drawn = base * np.exp(spread * noise) if base else spread * noise
        out[name] = jnp.asarray(drawn.astype(out[name].dtype))
    for name, factor in factors.items():
        out[name] = (out[name] * factor).astype(out[name].dtype)
    return out
```

```python
import numpy as np
import concourse.bass as bass
from concourse import mybir
from contextlib import ExitStack

F32 = mybir.dt.float32
BF16 = mybir.dt.bfloat16
U32 = mybir.dt.uint32
I32 = mybir.dt.int32
ALU = mybir.AluOpType
ACT = mybir.ActivationFunctionType
AX = mybir.AxisListType

P = 128
BATCH, FRAMES, CH = 16, 256, 64
CONTEXT = 5
SEQ = FRAMES - (CONTEXT - 1)
WIN = CONTEXT * CH
D = 128
TOK = SEQ // 2
TILES = 4
PAIR = TILES * TOK
ROUNDS = BATCH // 2
N_TOKENS = BATCH * SEQ
EPS = 1e-5
H0, HD0 = 16, 8
V0, VD0 = 8, 16
LAMBDA_INIT = 0.8 - 0.6 * float(np.exp(-0.3 * 0))
MLP = 512
H1, HD1 = 8, 16
E0, F0 = 64, 512
TOP = 2
CAP = 2 * (N_TOKENS * TOP // E0)
H2, HD2 = 16, 32
E1, F1 = 16, 256
EXPERTS_A_ROUND = 4
C_ROUNDS = E0 // EXPERTS_A_ROUND
DROPPED = 1 << 15
MASKED = -1e30
NC_F = MLP // P
ZERO_ROWS = 16

assert CAP == SEQ and LAMBDA_INIT > 0

PHASE_ROUNDS = {"S": 1, "A": ROUNDS, "B": ROUNDS, "C": C_ROUNDS, "D": ROUNDS}


class Signal:

    def __init__(self, sem, growth):
        self.sem, self.growth, self.start = sem, growth, {}
        total = 0
        for phase, rounds in PHASE_ROUNDS.items():
            self.start[phase] = total
            total += rounds * growth.get(phase, 0)

    def value(self, phase, i, n):
        base = self.start[phase] + n
        return i * self.growth.get(phase, 0) + base


def build(nc, T, out):
    with ExitStack() as ctx:
        build_in(nc, T, out, ctx)


def build_in(nc, T, out, ctx):
    def sb(name, shape, dt=F32):
        return ctx.enter_context(nc.sbuf_tensor(name, shape, dt))

    def part(of, at, shape):
        size = int(np.prod(shape[1:]))
        ap = of[0:shape[0], at:at + size]
        if len(shape) == 2:
            return ap
        names = "abc"[:len(shape) - 1]
        return ap.rearrange(f"p ({' '.join(names)}) -> p {' '.join(names)}", **dict(zip(names, shape[1:])))

    def parts(of, at, *shapes):
        found = []
        for shape in shapes:
            found.append(part(of, at, shape))
            at += int(np.prod(shape[1:]))
        assert at <= of.shape[1], at
        return found

    def signal(name, **growth):
        return Signal(ctx.enter_context(nc.semaphore(name)), growth)

    slot_x = nc.dram_tensor("slot_x", [E0 * CAP, D], F32, kind="Internal").ap()
    slot_y = nc.dram_tensor("slot_y", [E0 * CAP, D], F32, kind="Internal").ap()

    psS = [ctx.enter_context(nc.psum_tensor(f"psS{j}", [P, 512], F32)) for j in range(4)]
    psT = [ctx.enter_context(nc.psum_tensor(f"psT{j}", [P, 512], F32)) for j in range(2)]
    psO = ctx.enter_context(nc.psum_tensor("psO", [P, 512], F32))
    psG = ctx.enter_context(nc.psum_tensor("psG", [P, 512], F32))
    psPV = [psO, psG]

    LATE = 7232
    arena = sb("arena", [P, LATE + 2 * E1 * D])
    y_all = sb("y_all", [P, E1 * F1])
    ident = sb("ident", [P, P])
    before = sb("before", [P, P])
    ones = sb("ones", [P, P])
    frac = sb("frac", [P, P])
    causal = sb("causal", [TOK, TOK])
    causal_h = sb("causal_h", [TOK, TOK], BF16)
    ident_h = sb("ident_h", [P, P], BF16)
    eps_t = sb("eps_t", [P, 32])
    mhalf = sb("mhalf", [P, 32])
    iota_i = sb("iota_i", [P, E0], I32)
    iota_f = sb("iota_f", [P, E0])

    colv = {n: sb("c_" + n, [P, 1]) for n in
            ("L0_tok_b", "L0_tok_gamma", "L0_tok_beta", "L0_attn_n1_w", "L0_attn_n1_b", "L0_attn_mln1_w",
             "L0_attn_mln1_b", "L0_ffn_ln1_g", "L0_ffn_ln1_b", "sub_w", "sub_w8")}
    colc = {n: sb("k_" + n, [P, NC_F]) for n in ("L0_attn_mb1", "L0_attn_mln2_w", "L0_attn_mln2_b")}
    rowb = {n: sb("r_" + n, [TOK, T[n].shape[0]]) for n in
            ("L0_attn_n2_w", "L0_attn_n2_b", "L0_ffn_ln2_g", "L0_ffn_ln2_b", "L1_attn_bo", "L1_ffn_gate_b",
             "L0_attn_lq1", "L0_attn_lk1", "L0_attn_lq2", "L0_attn_lk2")}
    beta_e = sb("beta_e", [E1, D])

    zero_t, nat_tok, nat_q, nat_k, nat_v, nat_o, nat_m1, nat_m2, nat_fq, nat_fk, nat_b1, nat_bl, nat_wo1, nat_b11, \
        w2raw, w2w, b2m_row, mb2_row, qkv1 = parts(
            arena, 0, [126, ZERO_ROWS * D], [P, WIN], [P, P], [P, P], [P, P], [P, P], [P, NC_F, P], [P, MLP], [P, D],
            [P, D], [E0, F0], [H2, D], [P, H2 * HD2], [E1, F1], [P, NC_F, D], [P, NC_F, D], [1, D], [1, D],
            [P, 3, H2, HD2])
    nat = {"Wq": nat_q, "Wk": nat_k, "Wv": nat_v, "Wo": nat_o}
    wl = part(y_all, 0, [P, H2, D])
    gamma_b, b2_row1 = parts(arena, LATE, [TOK, E1, D], [1, E1, D])

    w_tok = sb("w_tok", [P, 3, D])
    wq0 = sb("wq0", [P, 4, P])
    wk0 = sb("wk0", [P, 4, P])
    wv0 = sb("wv0", [P, D])
    wo0 = sb("wo0", [P, D])
    w1m = sb("w1m", [P, MLP])
    w2m = sb("w2m", [P, NC_F, D + 1])
    b2m = sb("b2m", [TOK, D])
    neg_lam = sb("neg_lam", [TOK, 1])
    lam_t = sb("lam_t", [TOK, 2, HD0])
    lam_s = sb("lam_s", [TOK, 2])
    lam_e = sb("lam_e", [TOK, 2])
    wq1 = sb("wq1", [P, 2, P])
    wk1 = sb("wk1", [P, 2, P])
    wv1 = sb("wv1", [P, D])
    wo1 = sb("wo1", [P, D])
    wr = sb("wr", [P, E0])
    b1t = sb("b1t", [P, NC_F, E0])
    blt = sb("blt", [P, H2])
    wq2 = sb("wq2", [P, H2 * HD2])
    wk2 = sb("wk2", [P, H2 * HD2])
    wv2 = sb("wv2", [P, H2 * HD2])
    qb2 = sb("qb2", [P, 4])
    kb2 = sb("kb2", [P, 4])
    vb_row = sb("vb_row", [1, H2 * HD2])
    vb2 = sb("vb2", [TOK, H2 * HD2])
    wo2 = sb("wo2", [P, 4, D])
    gate_w = sb("gate_w", [P, E1])
    b1e = sb("b1e", [P, 2, E1])
    w1e = part(y_all, 0, [P, E1, F1])
    w2e = sb("w2e", [P, E1, 2, D])

    y_stats = sb("y_stats", [P, ROUNDS * 6])
    bn_mv = sb("bn_mv", [P, 2])
    bn_e = sb("bn_e", [P, 1])
    bn_r = sb("bn_r", [P, 1])
    bn_s = sb("bn_s", [P, 1])
    bn_m = sb("bn_m", [P, 1])
    bn_c = sb("bn_c", [P, 1])
    hx_all = sb("hx_all", [TOK, ROUNDS * TILES * D])
    gates_all = sb("gates_all", [TOK, ROUNDS * TILES * TOP])
    slots_all = sb("slots_all", [TOK, ROUNDS * TILES * TOP], U32)

    hT = sb("hT", [P, PAIR])
    h = sb("h", [TOK, TILES, D])
    u = sb("u", [TOK, TILES, D])
    n_ = sb("n_", [TOK, TILES, D])
    h1 = sb("h1", [TOK, TILES, D])
    xT = sb("xT", [P, PAIR])
    qT = sb("qT", [P, 4, PAIR])
    kT = sb("kT", [P, 4, PAIR])
    big, sq = qT, kT
    v17 = sb("v17", [TOK, TILES, 8, 17])
    head_rows = sb("head_rows", [P, 4])
    k_head = [sb(f"k_head{j}", [P, SEQ]) for j in range(4)]
    nmax = sb("nmax", [TOK, 4, 2])
    prob = [sb(f"prob{j}", [TOK, 2, SEQ]) for j in range(2)]
    probT = [sb(f"probT{j}", [TOK, 2 * SEQ]) for j in range(2)]
    rden = sb("rden", [TOK, 2, 8])
    o_all = sb("o_all", [TOK, TILES, H2 * HD2])
    xw = o_all[:, :, 0:WIN]
    oc = sb("oc", [TOK, TILES * V0, VD0])
    ocs = sb("ocs", [TOK, TILES * V0, VD0])
    ms = sb("ms", [TOK, TILES * V0])
    ms1 = sb("ms1", [TOK, TILES * V0])
    ms2 = sb("ms2", [TOK, TILES * V0])
    ln_st = sb("ln_st", [TOK, TILES, 6])
    ln_mv = sb("ln_mv", [TOK, TILES, 2])
    ln_e = sb("ln_e", [TOK, TILES])
    ln_r = sb("ln_r", [TOK, TILES])
    mm = sb("mm", [TOK, TILES, 2])
    mm2 = sb("mm2", [TOK, TILES])
    lg = sb("lg", [TOK, TILES, E0])
    mx = sb("mx", [TOK, TILES, 8])
    ix = sb("ix", [TOK, TILES, 8], U32)
    ixf = sb("ixf", [TOK, TILES, TOP])
    dlt = sb("dlt", [TOK, TILES])
    ex = sb("ex", [TOK, TILES])
    den = sb("den", [TOK, TILES])
    gate = sb("gate", [TOK, TILES, TOP])
    hot = sb("hot", [TOK, TILES, TOP, E0])
    hots = sb("hots", [TOK, TILES, E0])
    pos_e = sb("pos_e", [TOK, TILES, E0])
    carry = sb("carry", [TOK, E0])
    pos_h = sb("pos_h", [TOK, TILES, TOP, E0])
    pos = sb("pos", [TOK, TILES * TOP])
    keep = sb("keep", [TOK, TILES * TOP])
    slot_f = sb("slot_f", [TOK, TILES * TOP])
    drop_f = sb("drop_f", [TOK, TILES * TOP])
    slot_s = sb("slot_s", [TOK, TILES * TOP])
    slot_l = sb("slot_l", [TOK, TILES * TOP])
    slot_u = sb("slot_u", [TOK, TILES * TOP], U32)
    x2 = sb("x2", [TOK, TILES, D])
    SETS = EXPERTS_A_ROUND
    SET = 2 * F0 + D + 2 * D
    loads_in_flight = [parts(arena, s * SET, [P, F0], [P, NC_F, D], [1, D], [TOK, 2, D]) for s in range(SETS)]
    we1, we2, be2, xe = zip(*loads_in_flight)
    xeT0, xeT1, ye0, ye1 = parts(arena, SETS * SET, [P, CAP], [P, CAP], [TOK, 2, D], [TOK, 2, D])
    xeT, ye = (xeT0, xeT1), (ye0, ye1)
    he = [x[:, :, 0:CAP] for x in (qT, kT)]
    v33, gy, hm0, hm1, nrm0, nrm1, nrg, acc = parts(
        arena, 0, [TOK, TILES, H2, HD2 + 1], [TOK, TILES * TOP, D], [P, 2, PAIR], [P, 2, PAIR], [TOK, TILES, D],
        [TOK, TILES, D], [TOK, TILES, D], [TOK, TILES, D])
    hm, nrm = (hm0, hm1), (nrm0, nrm1)
    slot_c = sb("slot_c", [TOK, TILES * TOP], U32)
    gate_c = sb("gate_c", [TOK, TILES * TOP])
    hot1 = sb("hot1", [TOK, TILES, TOP, E1])
    comb2 = sb("comb2", [TOK, TILES, TOP, E1])
    comb = sb("comb", [TOK, TILES, E1])
    combT = sb("combT", [E1, PAIR])
    s16 = sb("s16", [TOK, TILES, E1])
    e_st = [sb(f"e_st{s}", [TOK, TILES, 6]) for s in range(2)]
    e_mv = [sb(f"e_mv{s}", [TOK, TILES, 2]) for s in range(2)]
    e_e = sb("e_e", [TOK, TILES])
    e_r = sb("e_r", [TOK, TILES])
    e_s = [sb(f"e_s{s}", [TOK, TILES]) for s in range(2)]

    LN_B, LN_D = 7, 2
    FM_B, FM_D = 6, 2
    HEADS_B, HEADS_D = 2 * (H0 + H1), 2 * H2
    loaded = signal("loaded", S=0)
    loaded_e = signal("loaded_e", S=0)
    const_made = signal("const_made", S=0)
    prep_psum = signal("prep_psum", S=0)
    prep_done = signal("prep_done", S=0)
    prep_pool = signal("prep_pool", S=0)
    prep_act = signal("prep_act", S=0)
    cleared = signal("cleared", S=0)
    dve_link = signal("dve_link", S=0)
    ready = signal("ready", S=0)

    win_in = signal("win_in", A=16 * TILES)
    win_psum = signal("win_psum", A=3)
    win_T = signal("win_T", A=3)
    conv_psum = signal("conv_psum", A=1)
    y_ready = signal("y_ready", A=1)
    y_counted = signal("y_counted", A=1)
    bn_link = signal("bn_link")
    bn_pool = signal("bn_pool")
    bn_ready = signal("bn_ready")

    round_done = signal("round_done", B=1, D=1)
    hT_ready = signal("hT_ready", B=1)
    h_psum = signal("h_psum", B=1)
    ln_in = signal("ln_in", B=LN_B, D=LN_D)
    ln_stats = signal("ln_stats", B=LN_B, D=LN_D)
    ln_aggr = signal("ln_aggr", B=LN_B, D=LN_D)
    ln_eps = signal("ln_eps", B=LN_B, D=LN_D)
    ln_rstd = signal("ln_rstd", B=LN_B, D=LN_D)
    ln_out = signal("ln_out", B=LN_B, D=LN_D)
    fm_psum = signal("fm_psum", B=FM_B, D=FM_D)
    fm_ready = signal("fm_ready", B=FM_B, D=FM_D)
    q_psum = signal("q_psum", B=4 + 2, D=4)
    q_ready = signal("q_ready", B=4 + 2, D=4)
    k_psum = signal("k_psum", B=4 + 2, D=4)
    k_ready = signal("k_ready", B=4 + 2, D=4)
    v_psum = signal("v_psum", B=2, D=4)
    v_ready = signal("v_ready", B=2, D=4)
    scored = signal("scored", B=HEADS_B, D=HEADS_D)
    k_masked = signal("k_masked", B=HEADS_B, D=HEADS_D)
    maxed = signal("maxed", B=HEADS_B, D=HEADS_D)
    probs = signal("probs", B=HEADS_B, D=HEADS_D)
    turned = signal("turned", B=HEADS_B, D=HEADS_D)
    taken = [signal(f"taken{j}", B=HEADS_B // 2, D=HEADS_D // 2) for j in range(2)]
    mixed = signal("mixed", B=HEADS_B, D=HEADS_D)
    recip = signal("recip", B=HEADS_B // 4, D=HEADS_D // 4)
    normed = signal("normed", B=HEADS_B // 4, D=HEADS_D // 4)
    chain = signal("chain", B=29, D=14)
    diff_ms = signal("diff_ms", B=1)
    diff_e = signal("diff_e", B=1)
    diff_r = signal("diff_r", B=1)
    diff_out = signal("diff_out", B=1)
    proj_psum = signal("proj_psum", B=2, D=1)
    up_psum = signal("up_psum", B=4)
    up_act = signal("up_act", B=4)
    up_sq = signal("up_sq", B=4)
    down_psum = signal("down_psum", B=1)
    down_var = signal("down_var", B=1)
    down_e = signal("down_e", B=1)
    down_r = signal("down_r", B=1)
    x2_ready = signal("x2_ready", B=1)
    route_psum = signal("route_psum", B=1)
    top_diff = signal("top_diff", B=1, D=1)
    top_exp = signal("top_exp", B=1, D=1)
    hot_ready = signal("hot_ready", B=1)
    rank_psum = signal("rank_psum", B=1)
    slots_ready = signal("slots_ready", B=1)
    scattered = signal("scattered", B=16 * TILES * TOP)

    N = EXPERTS_A_ROUND
    ew_in = [signal(f"ew_in{s}", C=16 * 4) for s in range(N)]
    xe_psum = [signal(f"xe_psum{s}", C=N // 2) for s in range(2)]
    xe_T = [signal(f"xe_T{s}", C=N // 2) for s in range(2)]
    eu_psum = [signal(f"eu_psum{s}", C=N) for s in range(2)]
    eu_act = [signal(f"eu_act{s}", C=N) for s in range(2)]
    ed_psum = [signal(f"ed_psum{s}", C=1) for s in range(N)]
    ye_ready = [signal(f"ye_ready{s}", C=N // 2) for s in range(2)]
    ye_out = [signal(f"ye_out{s}", C=16 * N // 2) for s in range(2)]

    idx_ready = signal("idx_ready", D=1)
    gathered = signal("gathered", D=16 * TILES * TOP)
    cat_psum = signal("cat_psum", D=4)
    cat_T = signal("cat_T", D=4)
    gate_psum = signal("gate_psum", D=1)
    comb_ready = signal("comb_ready", D=1)
    combT_psum = signal("combT_psum", D=1)
    combT_ready = signal("combT_ready", D=1)
    beta_psum = signal("beta_psum", D=1)
    acc_ready = signal("acc_ready", D=1)
    mu_psum = signal("mu_psum", D=2 * E1)
    mu_act = signal("mu_act", D=2 * E1)
    md_psum = signal("md_psum", D=E1)
    me_stats = signal("me_stats", D=E1)
    me_var = signal("me_var", D=E1)
    me_e = signal("me_e", D=E1)
    me_r = signal("me_r", D=E1)
    me_scale = signal("me_scale", D=E1)
    me_norm = signal("me_norm", D=E1)
    me_g = signal("me_g", D=E1)
    me_acc = signal("me_acc", D=E1)
    stored = signal("stored", D=16)

    due = {}

    def hold(eng, sig, phase, i, n):
        eng.wait_ge(sig.sem, sig.value(phase, i, n))

    def hold_apart(eng, sig, phase, i, n):
        name = str(eng.engine)
        if name not in due:
            due[name] = eng.alloc_register(f"due_{len(due)}")
        eng.reg_mov(due[name], sig.value(phase, i, n))
        eng.wait_ge(ready.sem, 1)
        eng.wait_ge(sig.sem, due[name])

    def bc(ap, axis, shape):
        return ap.unsqueeze(axis).broadcast_to(shape)

    tile = lambda t: slice(t * TOK, (t + 1) * TOK)

    def column(name):
        return T[name].rearrange("(p o) -> p o", o=1)

    loads = [(nat_tok[:, :], T["L0_tok_W"])]
    loads += [(nat[n][:, :], T["L0_attn_" + n]) for n in ("Wq", "Wk", "Wv", "Wo")]
    loads += [(colv[n][:, :], column(n)) for n in colv if n in T]
    loads += [(colv["sub_w"][j * VD0:(j + 1) * VD0, :], column("L0_attn_subln_w")) for j in range(V0)]
    loads += [(colc[n][:, c:c + 1], T[n][c * P:(c + 1) * P].rearrange("(p o) -> p o", o=1))
              for n in colc for c in range(NC_F)]
    loads += [(rowb[n][:, :], T[n].partition_broadcast(TOK)) for n in rowb]
    loads += [
        (mb2_row[:, :], T["L0_attn_mb2"].rearrange("(o d) -> o d", o=1)),
        (nat_m1[:, :, :], T["L0_attn_mW1"].rearrange("(c p) d -> p c d", p=P)),
        (nat_m2[:, :], T["L0_attn_mW2"]),
        (nat_fq[:, :], T["L0_ffn_wq"]), (nat_fk[:, :], T["L0_ffn_wk"]),
        (wv1[:, :], T["L0_ffn_wv"]), (wo1[:, :], T["L0_ffn_wo"]), (wr[:, :], T["L0_ffn_wr"]),
        (nat_b1[:, :], T["L0_ffn_b1"]), (nat_bl[:, :], T["L1_attn_bl"]), (nat_wo1[:, :], T["L1_attn_Wo"]),
        (nat_b11[:, :], T["L1_ffn_b1"]), (wl[:, :, :], T["L1_attn_Wl"].rearrange("h o i -> o h i")),
        (qkv1[:, 0, :, :], T["L1_attn_Wq"].rearrange("h i d -> i h d")),
        (qkv1[:, 1, :, :], T["L1_attn_Wk"].rearrange("h i d -> i h d")),
        (qkv1[:, 2, :, :], T["L1_attn_Wv"].rearrange("h i d -> i h d")),
        (gate_w[:, :], T["L1_ffn_gate_w"]),
    ]
    expert_loads = [
        (w1e[:, :, :], T["L1_ffn_w1"].rearrange("e d f -> d e f")),
        (w2e[:, :, :, :].rearrange("p e c d -> p (e c) d"), T["L1_ffn_w2"].rearrange("e (c p) d -> p (e c) d", p=P)),
        (gamma_b[:, :, :].rearrange("p e d -> p (e d)"), T["L1_ffn_gamma"].rearrange("e d -> (e d)").partition_broadcast(TOK)),
        (beta_e[:, :], T["L1_ffn_beta"]),
        (b2_row1[:, :, :].rearrange("o e d -> o (e d)"), T["L1_ffn_b2"].rearrange("(o e) d -> o (e d)", o=1)),
    ]

    def heads(ap, n, hd):
        return ap.rearrange("p (n d) -> p n d", d=hd)

    turns = [(nat_tok[:, 0:128], w_tok[:, 0, :], None), (nat_tok[:, 128:256], w_tok[:, 1, :], None),
             (nat_tok[:, 256:320], w_tok[0:64, 2, :], None)]
    for n, w in (("Wq", wq0), ("Wk", wk0)):
        turns.append((nat[n][:, :], w[:, :, :].rearrange("p g (j s) -> p (g j) s", s=32)[:, :, 0:HD0], HD0))
    turns += [(nat["Wv"][:, :], wv0[:, :], None), (nat["Wo"][:, :], wo0[:, :], None)]
    for c in range(NC_F):
        turns.append((nat_m1[:, c, :], w1m[:, c * P:(c + 1) * P], None))
        turns.append((nat_m2[:, c * P:(c + 1) * P], w2raw[:, c, :], None))
        turns.append((nat_wo1[:, c * P:(c + 1) * P], wo2[:, c, :], None))
        turns.append((nat_b1[:, c * P:(c + 1) * P], b1t[:, c, :], None))
    turns.append((nat_bl[:, :], blt[:, :], None))
    for c in range(2):
        turns.append((nat_b11[:, c * P:(c + 1) * P], b1e[:, c, :], None))
    RING = 4
    N_TURNS = len(turns)
    STEP_MEAN, STEP_B2, STEP_B2B, STEP_QKV, STEP_QB, STEP_KB, STEP_VB, STEP_VBB = (
        N_TURNS + 1, N_TURNS + 2, N_TURNS + 3, N_TURNS + 4, N_TURNS + 4 + H2, N_TURNS + 5 + H2,
        N_TURNS + 6 + H2, N_TURNS + 7 + H2)

    def take_turned(eng, copy, phase, i, off, m, causal_):
        hold(eng, turned, phase, i, off + m + 1)
        if m >= 2:
            hold(eng, mixed, phase, i, off + m - 1)
        if causal_:
            copy(eng, probT[m % 2][:, 0:SEQ], psT[m % 2][0:TOK, 0:SEQ])
            copy(eng, probT[m % 2][:, SEQ + TOK:2 * SEQ], psT[m % 2][0:TOK, SEQ + TOK:2 * SEQ]).then_inc(taken[m % 2].sem, 1)
        else:
            copy(eng, probT[m % 2][:, :], psT[m % 2][0:TOK, 0:2 * SEQ]).then_inc(taken[m % 2].sem, 1)

    def gates(dve, v, phase, i, link):
        hold(dve, top_exp, phase, i, 1)
        link(phase, i, v.tensor_scalar(den[:, :], ex[:, :], 1.0, None, ALU.add))
        link(phase, i, v.reciprocal(gate[:, :, 0], den[:, :]))
        link(phase, i, v.tensor_tensor(gate[:, :, 1], ex[:, :], gate[:, :, 0], ALU.mult))

    CONSTS = 3 + 3 + 6 + 1 + 4 + 1
    CLEARS = E0 * CAP // (126 * ZERO_ROWS)

    block = ctx.enter_context(nc.Block())

    @block.sync
    def _(sp):
        for dst, src in loads:
            sp.dma_start(dst, src, allow_slow_non_contiguous=True).then_inc(loaded.sem, 16)
        sp.wait_ge(const_made.sem, CONSTS)
        rows = slot_x.rearrange("(n p r) d -> n p (r d)", p=126, r=ZERO_ROWS)
        for n in range(rows.shape[0]):
            sp.dma_start(rows[n], zero_t[:, :]).then_inc(cleared.sem, 16)
        with sp.Fori(0, ROUNDS) as i:
            hold_apart(sp, win_psum, "A", i, 0)
            for b in range(2):
                for half in range(2):
                    src = bass.AP(T["x"].tensor, (i * 2 + b) * (FRAMES * CH) + half * TOK * CH,
                                  [[CH, TOK], [1, WIN]])
                    sp.dma_start(xw[:, 2 * b + half, :], src).then_inc(win_in.sem, 16)

        sp.wait_ge(scattered.sem, scattered.value("C", 0, 0))
        sp.wait_ge(round_done.sem, round_done.value("C", 0, 0))
        with sp.Fori(0, C_ROUNDS) as i:
            for s in range(N):
                e = i * N + s
                hold_apart(sp, ed_psum[s], "C", i, 0)
                sp.dma_start(xe[s][:, :, :], bass.AP(slot_x.tensor, e * (CAP * D), [[D, TOK], [TOK * D, 2], [1, D]])).then_inc(ew_in[s].sem, 16)
                sp.dma_start(we1[s][:, :], bass.AP(T["L0_ffn_w1"].tensor, e * (D * F0), [[F0, P], [1, F0]])).then_inc(ew_in[s].sem, 16)
                sp.dma_start(we2[s][:, :, :], bass.AP(T["L0_ffn_w2"].tensor, e * (D * F0), [[D, P], [P * D, NC_F], [1, D]])).then_inc(ew_in[s].sem, 16)
                sp.dma_start(be2[s][:, :], bass.AP(T["L0_ffn_b2"].tensor, e * D, [[D, 1], [1, D]])).then_inc(ew_in[s].sem, 16)

        for dst, src in expert_loads:
            sp.dma_start(dst, src, allow_slow_non_contiguous=True).then_inc(loaded_e.sem, 16)

        with sp.Fori(0, ROUNDS) as i:
            hold_apart(sp, me_acc, "D", i, E1)
            sp.dma_start(bass.AP(out.tensor, i * (PAIR * D), [[D, TOK], [TOK * D, TILES], [1, D]]),
                         acc[:, :, :]).then_inc(stored.sem, 16)
        sp.wait_ge(stored.sem, 16 * ROUNDS)

    @block.gpsimd
    def _(pool):
        g = nc.gpsimd
        g.memset(ident[:, :], 0.0).then_inc(const_made.sem, 1)
        g.memset(before[:, :], 1.0).then_inc(const_made.sem, 1)
        g.memset(causal[:, :], 0.0).then_inc(const_made.sem, 1)
        pool.wait_ge(const_made.sem, 3)
        g.affine_select(out=ident[:, :], in_=ident[:, :], compare_op=ALU.not_equal, fill=1.0, base=0,
                        pattern=[[-1, P]], channel_multiplier=1).then_inc(const_made.sem, 1)
        g.affine_select(out=before[:, :], in_=before[:, :], compare_op=ALU.is_gt, fill=0.0, base=0,
                        pattern=[[1, P]], channel_multiplier=-1).then_inc(const_made.sem, 1)
        g.affine_select(out=causal[:, :], in_=causal[:, :], compare_op=ALU.is_ge, fill=MASKED, base=0,
                        pattern=[[-1, TOK]], channel_multiplier=1).then_inc(const_made.sem, 1)
        g.memset(ones[:, :], 1.0).then_inc(const_made.sem, 1)
        g.memset(frac[:, :], 1.0 / MLP).then_inc(const_made.sem, 1)
        g.memset(eps_t[:, :], EPS).then_inc(const_made.sem, 1)
        g.memset(mhalf[:, :], -0.5).then_inc(const_made.sem, 1)
        g.memset(zero_t[:, :], 0.0).then_inc(const_made.sem, 1)
        g.memset(carry[:, :], 0.0).then_inc(const_made.sem, 1)
        g.iota(iota_i[:, :], pattern=[[1, E0]], base=0, channel_multiplier=0).then_inc(const_made.sem, 1)
        for w in (wq0, wk0, wq1, wk1):
            g.memset(w[:, :, :], 0.0).then_inc(const_made.sem, 1)
        g.memset(v17[:, :, :, VD0:VD0 + 1], 1.0).then_inc(const_made.sem, 1)

        pool.wait_ge(bn_link.sem, 1)
        g.tensor_tensor(bn_e[:, :], bn_mv[:, 1:2], eps_t[:, 0:1], ALU.add).then_inc(bn_pool.sem, 1)
        pool.wait_ge(bn_pool.sem, 1)
        g.tensor_tensor(bn_r[:, :], bn_e[:, :], mhalf[:, 0:1], ALU.pow).then_inc(bn_pool.sem, 1)

        def rstd(phase, i, k, n, src, e_sig, mid, r_sig, dst, given):
            hold_apart(pool, given, phase, i, k + 1)
            g.tensor_tensor(mid, src, eps_t[0:TOK, 0:n], ALU.add).then_inc(e_sig.sem, 1)
            hold_apart(pool, e_sig, phase, i, k + 1)
            g.tensor_tensor(dst, mid, mhalf[0:TOK, 0:n], ALU.pow).then_inc(r_sig.sem, 1)

        def norm(phase, i, k):
            rstd(phase, i, k, TILES, ln_mv[:, :, 1], ln_eps, ln_e[:, :], ln_rstd, ln_r[:, :], ln_aggr)

        with pool.Fori(0, ROUNDS) as i:
            norm("B", i, 0)
            norm("B", i, 1)
            rstd("B", i, 0, TILES * V0, ms1[:, :], diff_e, ms2[:, :], diff_r, ms[:, :], diff_ms)
            norm("B", i, 2)
            norm("B", i, 3)
            rstd("B", i, 0, TILES, mm2[:, :], down_e, ln_e[:, :], down_r, ln_r[:, :], down_var)
            for k in range(4, LN_B):
                norm("B", i, k)
            pool.wait_ge(cleared.sem, 16 * CLEARS)
            hold_apart(pool, slots_ready, "B", i, 1)
            for t in range(TILES):
                for k in range(TOP):
                    c = t * TOP + k
                    g.indirect_dma_start(out=slot_x, out_offset=bass.IndirectOffsetOnAxis(ap=slot_u[:, c:c + 1], axis=0),
                                         in_=x2[:, t, :], in_offset=None, bounds_check=E0 * CAP - 1,
                                         oob_is_err=False).then_inc(scattered.sem, 16)

        with pool.Fori(0, C_ROUNDS) as i:
            for s in range(N):
                p, q = s % 2, s // 2
                hold_apart(pool, ye_ready[p], "C", i, q + 1)
                g.dma_start(bass.AP(slot_y.tensor, (i * N + s) * (CAP * D), [[D, TOK], [TOK * D, 2], [1, D]]),
                            ye[p][:, :, :]).then_inc(ye_out[p].sem, 16)
        for p in range(2):
            pool.wait_ge(ye_out[p].sem, 16 * E0 // 2)

        with pool.Fori(0, ROUNDS) as i:
            hold_apart(pool, idx_ready, "D", i, 1)
            for c in range(TILES * TOP):
                g.indirect_dma_start(out=gy[:, c, :], out_offset=None, in_=slot_y,
                                     in_offset=bass.IndirectOffsetOnAxis(ap=slot_c[:, c:c + 1], axis=0),
                                     bounds_check=E0 * CAP - 1, oob_is_err=False).then_inc(gathered.sem, 16)
            norm("D", i, 0)
            norm("D", i, 1)

            def scale(e):
                s = e % 2
                rstd("D", i, e, TILES, e_mv[s][:, :, 1], me_e, e_e[:, :], me_r, e_r[:, :], me_var)
                hold_apart(pool, me_r, "D", i, e + 1)
                g.tensor_tensor(e_s[s][:, :], e_r[:, :], comb[:, :, e], ALU.mult).then_inc(me_scale.sem, 1)

            scale(0)
            for e in range(E1):
                if e + 1 < E1:
                    scale(e + 1)
                hold_apart(pool, me_norm, "D", i, e + 1)
                g.tensor_tensor(nrg[:, :, :], nrm[e % 2][:, :, :], bc(gamma_b[:, e, :], 1, [TOK, TILES, D]),
                                ALU.mult).then_inc(me_g.sem, 1)
                hold_apart(pool, me_g, "D", i, e + 1)
                g.tensor_tensor(acc[:, :, :], acc[:, :, :], nrg[:, :, :], ALU.add).then_inc(me_acc.sem, 1)
                hold_apart(pool, me_acc, "D", i, e + 1)

    @block.scalar
    def _(act):
        a = nc.scalar
        act.wait_ge(prep_done.sem, STEP_VBB)
        a.activation(lam_e[:, :], lam_s[:, :], ACT.Exp).then_inc(prep_act.sem, 1)
        act.wait_ge(ready.sem, 1)

        with act.Fori(0, ROUNDS) as i:
            hold_apart(act, conv_psum, "A", i, 1)
            a.activation(y_all[:, bass.ds(i * PAIR, PAIR)], psG[:, 0:PAIR], ACT.Relu,
                         bias=colv["L0_tok_b"][:, :]).then_inc(y_ready.sem, 1)

        def feature_major(phase, i, k, weight, bias):
            hold(act, fm_psum, phase, i, k + 1)
            more = {}
            if weight is not None:
                more["scale"] = weight[:, :]
            if bias is not None:
                more["bias"] = bias[:, :]
            a.activation(xT[:, :], psG[:, 0:PAIR], ACT.Identity, **more).then_inc(fm_ready.sem, 1)

        def queries(phase, i, k, groups, scale, bias):
            for g in range(groups):
                hold(act, q_psum, phase, i, k + g + 1)
                more = {"bias": bias[:, g:g + 1]} if bias is not None else {}
                a.activation(qT[:, g, :], psS[g][:, 0:PAIR], ACT.Identity, scale=scale, **more).then_inc(q_ready.sem, 1)

        def attention(phase, i, off, steps, causal_):
            for m in range(steps + 1):
                if m < steps:
                    hold(act, maxed, phase, i, off + m + 1)
                    if m >= 2:
                        hold(act, turned, phase, i, off + m - 1)
                    for t in range(2):
                        keys = TOK if causal_ and t == 0 else SEQ
                        last = a.activation(prob[m % 2][:, t, 0:keys], psS[m % 4][0:TOK, t * 256:t * 256 + keys],
                                            ACT.Exp, bias=nmax[:, m % 4, t:t + 1])
                    last.then_inc(probs.sem, 1)
                if m >= 1 and (m - 1) % 2 == 1:
                    take(act, phase, i, off, m - 1, causal_)

        def take_copy(eng, dst, src):
            return nc.scalar.copy(dst, src) if eng is act else nc.vector.tensor_copy(dst, src)

        def take(eng, phase, i, off, m, causal_):
            take_turned(eng, take_copy, phase, i, off, m, causal_)

        act.wait_ge(bn_ready.sem, 1)
        with act.Fori(0, ROUNDS) as i:
            hold_apart(act, round_done, "B", i, 0)
            a.activation(hT[:, :], y_all[:, bass.ds(i * PAIR, PAIR)], ACT.Identity,
                         bias=bn_c[:, :], scale=bn_s[:, :]).then_inc(hT_ready.sem, 1)
            feature_major("B", i, 0, colv["L0_attn_n1_w"], colv["L0_attn_n1_b"])
            queries("B", i, 0, 4, HD0 ** -0.5, None)
            attention("B", i, 0, 2 * H0, False)
            feature_major("B", i, 1, colv["sub_w8"], None)
            feature_major("B", i, 2, colv["L0_attn_mln1_w"], colv["L0_attn_mln1_b"])
            for c in range(NC_F):
                hold(act, up_psum, "B", i, c + 1)
                a.activation(big[:, c, :], psS[c][:, 0:PAIR], ACT.Gelu,
                             bias=colc["L0_attn_mb1"][:, c:c + 1]).then_inc(up_act.sem, 1)
            feature_major("B", i, 3, colv["L0_ffn_ln1_g"], colv["L0_ffn_ln1_b"])
            queries("B", i, 4, 2, HD1 ** -0.5, None)
            attention("B", i, 2 * H0, 2 * H1, False)
            feature_major("B", i, 4, None, None)
            feature_major("B", i, 5, None, None)
            hold(act, top_diff, "B", i, 1)
            a.activation(ex[:, :], dlt[:, :], ACT.Exp).then_inc(top_exp.sem, 1)

        with act.Fori(0, C_ROUNDS) as i:
            for s in range(N):
                p, q = s % 2, s // 2
                if q:
                    hold(act, ed_psum[s - 2], "C", i, 1)
                else:
                    hold(act, ed_psum[s + N - 2], "C", i, 0)
                for half in range(2):
                    hold_apart(act, eu_psum[p], "C", i, 2 * q + half + 1)
                    for c in (2 * half, 2 * half + 1):
                        last = a.activation(he[p][:, c, :], psS[2 * p + half][:, (c % 2) * 256:(c % 2) * 256 + CAP], ACT.Gelu_apprx_tanh,
                                            bias=b1t[:, c, bass.ds(i * N + s, 1)])
                    last.then_inc(eu_act[p].sem, 1)

        with act.Fori(0, ROUNDS) as i:
            feature_major("D", i, 0, None, None)
            queries("D", i, 0, 4, 1.0, qb2)
            attention("D", i, 0, 2 * H2, True)
            for c in range(4):
                hold(act, cat_psum, "D", i, c + 1)
                a.copy(big[:, c, :], psS[c][:, 0:PAIR]).then_inc(cat_T.sem, 1)
            feature_major("D", i, 1, None, None)
            hold(act, top_diff, "D", i, 1)
            a.activation(ex[:, :], dlt[:, :], ACT.Exp).then_inc(top_exp.sem, 1)
            for e in range(E1):
                s = e % 2
                for c in range(2):
                    hold(act, mu_psum, "D", i, 2 * e + c + 1)
                    if e >= 2 and c == 0:
                        hold(act, md_psum, "D", i, e - 1)
                    a.activation(hm[s][:, c, :], psS[2 * s + c][:, 0:PAIR], ACT.Gelu,
                                 bias=b1e[:, c, e:e + 1]).then_inc(mu_act.sem, 1)

    @block.vector
    def _(dve):
        v = nc.vector
        count = [0]

        def step(ins):
            count[0] += 1
            ins.then_inc(dve_link.sem, 1)
            dve.wait_ge(dve_link.sem, count[0])

        dve.wait_ge(const_made.sem, CONSTS)
        dve.wait_ge(loaded.sem, 16 * len(loads))
        v.tensor_copy(iota_f[:, :], iota_i[:, :])
        v.tensor_reduce(head_rows[:, :], ident[:, :].rearrange("p (j r) -> p j r", j=4), AX.X, ALU.add)
        v.tensor_copy(ident_h[:, :], ident[:, :])
        v.tensor_copy(causal_h[:, :], causal[:, :])
        v.memset(w2m[:, :, D:D + 1], 1.0 / MLP)
        v.tensor_scalar(colv["sub_w8"][:, :], colv["sub_w"][:, :], 1.0 - LAMBDA_INIT, None, ALU.mult)
        for w, src in ((wq1, nat_fq), (wk1, nat_fk)):
            v.tensor_copy(w[:, :, :].rearrange("p g (j s) -> p (g j) s", s=32)[:, :, 0:HD1], heads(src[:, :], H1, HD1))
        for j, (x, y) in enumerate((("lq1", "lk1"), ("lq2", "lk2"))):
            step(v.tensor_tensor(lam_t[:, j, :], rowb["L0_attn_" + x][:, :], rowb["L0_attn_" + y][:, :], ALU.mult))
        v.tensor_reduce(lam_s[:, :], lam_t[:, :, :], AX.X, ALU.add)
        for k, (src, dst, hd) in enumerate(turns):
            dve.wait_ge(prep_psum.sem, k + 1)
            rows, cols = src.shape[1], src.shape[0]
            ps = psS[k % RING][0:rows, 0:cols]
            v.tensor_copy(dst, ps if hd is None else heads(ps, cols // hd, hd)).then_inc(prep_done.sem, 1)
        dve.wait_ge(prep_done.sem, N_TURNS)
        for c in range(NC_F):
            last = v.tensor_scalar(w2w[:, c, :], w2raw[:, c, :], colc["L0_attn_mln2_w"][:, c:c + 1], None, ALU.mult)
        last.then_inc(prep_pool.sem, 1)
        dve.wait_ge(prep_psum.sem, STEP_MEAN)
        dve.wait_ge(prep_pool.sem, 1)
        v.tensor_tensor(w2m[:, :, 0:D], w2w[:, :, :], bc(psS[0][:, 0:D], 1, [P, NC_F, D]), ALU.subtract).then_inc(prep_done.sem, 1)
        dve.wait_ge(prep_psum.sem, STEP_B2)
        v.tensor_tensor(b2m_row[:, :], psS[1][0:1, 0:D], mb2_row[:, :], ALU.add).then_inc(prep_done.sem, 1)
        dve.wait_ge(prep_psum.sem, STEP_B2B)
        v.tensor_copy(b2m[:, :], psS[2][0:TOK, 0:D]).then_inc(prep_done.sem, 1)
        for n in range(H2):
            dve.wait_ge(prep_psum.sem, STEP_QKV + n)
            for x, w in enumerate((wq2, wk2, wv2)):
                last = v.tensor_copy(w[:, n * HD2:(n + 1) * HD2], psS[n % RING][:, x * HD2:(x + 1) * HD2])
            last.then_inc(prep_done.sem, 1)
        for k, dst in ((STEP_QB, qb2), (STEP_KB, kb2)):
            dve.wait_ge(prep_psum.sem, k + 0)
            v.tensor_copy(dst[:, :], psT[0 if dst is qb2 else 1][:, 0:4]).then_inc(prep_done.sem, 1)
        dve.wait_ge(prep_psum.sem, STEP_VB)
        v.tensor_copy(vb_row[:, :], psO[0:1, :]).then_inc(prep_done.sem, 1)
        dve.wait_ge(prep_psum.sem, STEP_VBB)
        v.tensor_copy(vb2[:, :], psG[0:TOK, :]).then_inc(prep_done.sem, 1)
        dve.wait_ge(prep_act.sem, 1)
        step(v.tensor_tensor(lam_s[:, 0:1], lam_e[:, 1:2], lam_e[:, 0:1], ALU.subtract))
        v.tensor_scalar(neg_lam[:, :], lam_s[:, 0:1], -LAMBDA_INIT, None, ALU.add).then_inc(ready.sem, 1)

        with dve.Fori(0, ROUNDS) as i:
            for c in range(3):
                rows = P if c < 2 else WIN - 2 * P
                hold(dve, win_psum, "A", i, c + 1)
                if c == 0:
                    hold(dve, conv_psum, "A", i, 0)
                v.tensor_copy(big[0:rows, c, :], psS[c][0:rows, 0:PAIR]).then_inc(win_T.sem, 1)
            hold_apart(dve, y_ready, "A", i, 1)
            v.bn_stats(y_stats[:, bass.ds(i * 6, 6)], y_all[:, bass.ds(i * PAIR, PAIR)]).then_inc(y_counted.sem, 1)
        dve.wait_ge(y_counted.sem, ROUNDS)
        v.bn_aggr(bn_mv[:, :], y_stats[:, :]).then_inc(bn_link.sem, 1)
        dve.wait_ge(bn_pool.sem, 2)
        v.tensor_tensor(bn_s[:, :], bn_r[:, :], colv["L0_tok_gamma"][:, :], ALU.mult).then_inc(bn_link.sem, 1)
        dve.wait_ge(bn_link.sem, 2)
        v.tensor_tensor(bn_m[:, :], bn_mv[:, 0:1], bn_s[:, :], ALU.mult).then_inc(bn_link.sem, 1)
        dve.wait_ge(bn_link.sem, 3)
        v.tensor_tensor(bn_c[:, :], colv["L0_tok_beta"][:, :], bn_m[:, :], ALU.subtract).then_inc(bn_ready.sem, 1)

        done = [0]

        def link(phase, i, ins):
            done[0] += 1
            ins.then_inc(chain.sem, 1)
            hold_apart(dve, chain, phase, i, done[0])

        def chain_ends(phase):
            assert done[0] == chain.growth[phase], (phase, done[0])
            done[0] = 0

        def norm(phase, i, k, src, dst):
            for t in range(TILES):
                last = v.bn_stats(ln_st[:, t, :], src[t])
            last.then_inc(ln_stats.sem, 1)
            hold_apart(dve, ln_stats, phase, i, k + 1)
            for t in range(TILES):
                last = v.bn_aggr(ln_mv[:, t, :], ln_st[:, t, :])
            last.then_inc(ln_aggr.sem, 1)
            hold(dve, ln_rstd, phase, i, k + 1)
            for t in range(TILES):
                last = v.tensor_scalar(dst[:, t, :], src[t], ln_mv[:, t, 0:1], ln_r[:, t:t + 1], ALU.subtract, ALU.mult)
            last.then_inc(ln_out.sem, 1)
            hold(dve, ln_out, phase, i, k + 1)

        def tiles(x):
            return [x[:, t, :] for t in range(TILES)]

        def keys(phase, i, k, groups, bias):
            for g in range(groups):
                hold(dve, k_psum, phase, i, k + g + 1)
                src = psS[g][:, 0:PAIR]
                ins = v.tensor_copy(kT[:, g, :], src) if bias is None else v.tensor_scalar(kT[:, g, :], src, bias[:, g:g + 1], None, ALU.add)
                ins.then_inc(k_ready.sem, 1)

        def attention(phase, i, off, H, vd, o, causal_, k_ready_n):
            steps = 2 * H
            group0 = off // 4

            def mask(m):
                b, n = m // H, m % H
                if m >= 4:
                    hold(dve, scored, phase, i, off + m - 3)
                v.tensor_scalar(k_head[m % 4][:, :], kT[:, n // 4, b * SEQ:(b + 1) * SEQ], head_rows[:, n % 4:n % 4 + 1], None,
                                ALU.mult).then_inc(k_masked.sem, 1)

            def maximum(m):
                hold(dve, scored, phase, i, off + m + 1)
                s = psS[m % 4]
                if causal_:
                    v.tensor_reduce(nmax[:, m % 4, 0:1], s[0:TOK, 0:TOK], AX.X, ALU.max, negate=True)
                    v.tensor_reduce(nmax[:, m % 4, 1:2], s[0:TOK, 256:256 + SEQ], AX.X, ALU.max, negate=True).then_inc(maxed.sem, 1)
                else:
                    v.tensor_reduce(nmax[:, m % 4, :], s[0:TOK, :].rearrange("p (t k) -> p t k", t=2)[:, :, 0:SEQ],
                                    AX.X, ALU.max, negate=True).then_inc(maxed.sem, 1)

            def divide(m):
                gr = m // 4
                hold(dve, mixed, phase, i, off + m + 1)
                ps = psPV[gr % 2][0:TOK, 0:8 * (vd + 1)].rearrange("p (n t d) -> p n t d", n=4, t=2)
                rd = rden[:, gr % 2, :].rearrange("p (n t) -> p n t", n=4)
                v.reciprocal(rd, ps[:, :, :, vd]).then_inc(recip.sem, 1)
                hold(dve, recip, phase, i, group0 + gr + 1)
                b, n0 = m // H, m % H - 3
                dst = o[:, 2 * b:2 * b + 2, n0 * vd:(n0 + 4) * vd].rearrange("p t (n d) -> p n t d", n=4)
                v.tensor_tensor(dst, ps[:, :, :, 0:vd], bc(rd, 3, [TOK, 4, 2, vd]), ALU.mult).then_inc(normed.sem, 1)

            hold(dve, k_ready, phase, i, k_ready_n)
            for m in range(4):
                mask(m)
            maximum(0)
            maximum(1)
            for m in range(steps):
                if m + 4 < steps:
                    mask(m + 4)
                if m + 2 < steps:
                    maximum(m + 2)
                if m % 2 == 0:
                    take_turned(dve, lambda eng, dst, src: v.tensor_copy(dst, src), phase, i, off, m, causal_)
                if m >= 1 and (m - 1) % 4 == 3:
                    divide(m - 1)
            divide(steps - 1)

        with dve.Fori(0, ROUNDS) as i:
            done[0] = 0
            hold(dve, h_psum, "B", i, 1)
            link("B", i, v.tensor_copy(h[:, :, :], psG[0:TOK, :].rearrange("p (t d) -> p t d", t=TILES)))
            norm("B", i, 0, tiles(h), u)
            norm("B", i, 1, tiles(u), n_)
            keys("B", i, 0, 4, None)
            hold(dve, v_psum, "B", i, 1)
            v.tensor_copy(v17[:, :, :, 0:VD0], psG[0:TOK, :].rearrange("p (t n d) -> p t n d", t=TILES, d=VD0)).then_inc(v_ready.sem, 1)
            o0 = o_all[:, :, 0:H0 * VD0]
            attention("B", i, 0, H0, VD0, o_all, False, 4)
            hold(dve, normed, "B", i, 2 * H0 // 4)
            for t in range(TILES):
                pair = o_all[:, t, 0:H0 * VD0].rearrange("p (n two d) -> p n two d", two=2, d=VD0)
                last = v.scalar_tensor_tensor(oc[:, t * V0:(t + 1) * V0, :], pair[:, :, 1, :], neg_lam[:, :], pair[:, :, 0, :], ALU.mult, ALU.add)
            link("B", i, last)
            link("B", i, v.tensor_tensor(ocs[:, :, :], oc[:, :, :], oc[:, :, :], ALU.mult))
            link("B", i, v.tensor_reduce(ms[:, :], ocs[:, :, :], AX.X, ALU.add))
            v.tensor_scalar(ms1[:, :], ms[:, :], 1.0 / VD0, None, ALU.mult).then_inc(diff_ms.sem, 1)
            hold(dve, diff_r, "B", i, 1)
            v.tensor_tensor(n_[:, :, :].rearrange("p t (n d) -> p (t n) d", d=VD0), oc[:, :, :], bc(ms[:, :], 2, [TOK, TILES * V0, VD0]),
                            ALU.mult).then_inc(diff_out.sem, 1)
            hold(dve, proj_psum, "B", i, 1)
            norm("B", i, 2, [psS[0][0:TOK, t * D:(t + 1) * D] for t in range(TILES)], n_)
            row = lambda n: bc(rowb[n][:, :], 1, [TOK, TILES, D])
            link("B", i, v.tensor_tensor(n_[:, :, :], n_[:, :, :], row("L0_attn_n2_w"), ALU.mult))
            link("B", i, v.tensor_tensor(n_[:, :, :], n_[:, :, :], row("L0_attn_n2_b"), ALU.add))
            link("B", i, v.tensor_tensor(h1[:, :, :], n_[:, :, :], u[:, :, :], ALU.add))
            norm("B", i, 3, tiles(h1), n_)
            link("B", i, v.tensor_tensor(h[:, :, :], h[:, :, :], h1[:, :, :], ALU.add))
            link("B", i, v.tensor_tensor(h[:, :, :], h[:, :, :], bc(b2m[:, :], 1, [TOK, TILES, D]), ALU.add))
            for c in range(NC_F):
                hold(dve, up_act, "B", i, c + 1)
                v.tensor_tensor(sq[:, c, :], big[:, c, :], big[:, c, :], ALU.mult).then_inc(up_sq.sem, 1)
            hold(dve, down_psum, "B", i, 1)
            for j in range(2):
                last = v.tensor_copy(mm[:, 2 * j:2 * j + 2, :], psT[j][0:TOK, 0:2 * (D + 2)].rearrange("p (t d) -> p t d", t=2)[:, :, D:D + 2])
            link("B", i, last)
            link("B", i, v.tensor_tensor(mm2[:, :], mm[:, :, 0], mm[:, :, 0], ALU.mult))
            v.tensor_tensor(mm2[:, :], mm[:, :, 1], mm2[:, :], ALU.subtract).then_inc(down_var.sem, 1)
            hold(dve, down_r, "B", i, 1)
            for t in range(TILES):
                at = (t % 2) * (D + 2)
                last = v.scalar_tensor_tensor(h[:, t, :], psT[t // 2][0:TOK, at:at + D], ln_r[:, t:t + 1], h[:, t, :], ALU.mult, ALU.add)
            link("B", i, last)
            norm("B", i, 4, tiles(h), u)
            norm("B", i, 5, tiles(u), n_)
            keys("B", i, 4, 2, None)
            hold(dve, v_psum, "B", i, 2)
            v.tensor_copy(v17[:, :, :, 0:HD1], psG[0:TOK, :].rearrange("p (t n d) -> p t n d", t=TILES, d=HD1)).then_inc(v_ready.sem, 1)
            attention("B", i, 2 * H0, H1, HD1, n_, False, 6)
            hold(dve, proj_psum, "B", i, 2)
            link("B", i, v.tensor_tensor(u[:, :, :], u[:, :, :], psS[0][0:TOK, :].rearrange("p (t d) -> p t d", t=TILES), ALU.add))
            norm("B", i, 6, tiles(u), n_)
            link("B", i, v.tensor_tensor(n_[:, :, :], n_[:, :, :], row("L0_ffn_ln2_g"), ALU.mult))
            hold(dve, scattered, "B", i, 0)
            v.tensor_tensor(x2[:, :, :], n_[:, :, :], row("L0_ffn_ln2_b"), ALU.add).then_inc(x2_ready.sem, 1)
            hold_apart(dve, x2_ready, "B", i, 1)
            v.tensor_tensor(hx_all[:, bass.ds(i * (TILES * D), TILES * D)], h[:, :, :].rearrange("p t d -> p (t d)"),
                            u[:, :, :].rearrange("p t d -> p (t d)"), ALU.add)
            hold(dve, route_psum, "B", i, 1)
            link("B", i, v.tensor_copy(lg[:, :, :], psS[1][0:TOK, 0:TILES * E0].rearrange("p (t e) -> p t e", t=TILES)))
            for t in range(TILES):
                last = v.max(mx[:, t, :], lg[:, t, :])
            link("B", i, last)
            v.tensor_tensor(dlt[:, :], mx[:, :, 1], mx[:, :, 0], ALU.subtract).then_inc(top_diff.sem, 1)
            for t in range(TILES):
                last = v.max_index(ix[:, t, :], mx[:, t, :], lg[:, t, :])
            link("B", i, last)
            link("B", i, v.tensor_copy(ixf[:, :, :], ix[:, :, 0:TOP]))
            pairs = [TOK, TILES * TOP, E0]
            ix8 = ixf[:, :, :].rearrange("p t k -> p (t k)")
            link("B", i, v.tensor_tensor(hot[:, :, :, :].rearrange("p t k e -> p (t k) e"), bc(iota_f[0:TOK, :], 1, pairs), bc(ix8, 2, pairs), ALU.is_equal))
            v.tensor_tensor(hots[:, :, :], hot[:, :, 0, :], hot[:, :, 1, :], ALU.add).then_inc(hot_ready.sem, 1)
            gates(dve, v, "B", i, link)
            hold(dve, rank_psum, "B", i, 1)
            link("B", i, v.tensor_tensor(pos_e[:, :, :], psT[0][0:TOK, 0:TILES * E0].rearrange("p (t e) -> p t e", t=TILES),
                                         bc(carry[0:TOK, :], 1, [TOK, TILES, E0]), ALU.add))
            v.tensor_tensor(carry[:, :], carry[:, :], psT[1][0:TOK, 0:E0], ALU.add)
            link("B", i, v.tensor_tensor(pos_h[:, :, :, :], hot[:, :, :, :], bc(pos_e[:, :, :], 2, [TOK, TILES, TOP, E0]), ALU.mult))
            link("B", i, v.tensor_reduce(pos[:, :], pos_h[:, :, :, :].rearrange("p t k e -> p (t k) e"), AX.X, ALU.add))
            v.tensor_scalar(slot_l[:, :], ix8, float(CAP), float(CAP - 1), ALU.mult, ALU.add)
            v.tensor_scalar(keep[:, :], pos[:, :], float(CAP), None, ALU.is_lt)
            link("B", i, v.scalar_tensor_tensor(slot_f[:, :], ix8, float(CAP), pos[:, :], ALU.mult, ALU.add))
            link("B", i, v.tensor_scalar(drop_f[:, :], keep[:, :], -float(DROPPED), float(DROPPED), ALU.mult, ALU.add))
            link("B", i, v.tensor_tensor(slot_s[:, :], slot_f[:, :], drop_f[:, :], ALU.add))
            v.tensor_copy(slot_u[:, :], slot_s[:, :]).then_inc(slots_ready.sem, 1)
            link("B", i, v.tensor_tensor(slot_l[:, :], slot_f[:, :], slot_l[:, :], ALU.min))
            v.tensor_copy(slots_all[:, bass.ds(i * (TILES * TOP), TILES * TOP)], slot_l[:, :])
            v.tensor_tensor(gates_all[:, bass.ds(i * (TILES * TOP), TILES * TOP)], gate[:, :, :].rearrange("p t k -> p (t k)"),
                            keep[:, :], ALU.mult).then_inc(round_done.sem, 1)
            chain_ends("B")

        def rows_turned(i, s):
            p, q = s % 2, s // 2
            hold(dve, xe_psum[p], "C", i, q + 1)
            v.tensor_copy(xeT[p][:, :], (psG, psO)[p][:, 0:CAP]).then_inc(xe_T[p].sem, 1)

        def expert_steps(i, ahead):
            for s in range(N):
                if s + 2 < N or ahead:
                    rows_turned(i, s + 2)
                p, q = s % 2, s // 2
                hold(dve, ed_psum[s], "C", i, 1)
                hold(dve, ye_out[p], "C", i, 16 * q)
                v.tensor_copy(ye[p][:, :, :], psT[p][0:TOK, 0:2 * D].rearrange("p (t d) -> p t d", t=2)).then_inc(ye_ready[p].sem, 1)

        rows_turned(0, 0)
        rows_turned(0, 1)
        with dve.Fori(0, C_ROUNDS - 1) as i:
            expert_steps(i, True)
        expert_steps(C_ROUNDS - 1, False)

        v.memset(v33[:, :, :, HD2:HD2 + 1], 1.0)
        with dve.Fori(0, ROUNDS) as i:
            hold_apart(dve, round_done, "D", i, 0)
            v.tensor_copy(slot_c[:, :], slots_all[:, bass.ds(i * (TILES * TOP), TILES * TOP)]).then_inc(idx_ready.sem, 1)
            v.tensor_copy(gate_c[:, :], gates_all[:, bass.ds(i * (TILES * TOP), TILES * TOP)])
            link("D", i, v.tensor_copy(h[:, :, :].rearrange("p t d -> p (t d)"), hx_all[:, bass.ds(i * (TILES * D), TILES * D)]))
            hold(dve, gathered, "D", i, 16 * TILES * TOP)
            for k in range(TOP):
                for t in range(TILES):
                    c = t * TOP + k
                    last = v.scalar_tensor_tensor(h[:, t, :], gy[:, c, :], gate_c[:, c:c + 1], h[:, t, :], ALU.mult, ALU.add)
                link("D", i, last)
            norm("D", i, 0, tiles(h), u)
            keys("D", i, 0, 4, kb2)
            for t in range(TILES):
                hold(dve, v_psum, "D", i, t + 1)
                v.tensor_tensor(v33[:, t, :, 0:HD2], [psT[0], psT[1], psO, psG][t][0:TOK, :].rearrange("p (n d) -> p n d", d=HD2),
                                vb2[:, :].rearrange("p (n d) -> p n d", d=HD2), ALU.add).then_inc(v_ready.sem, 1)
            attention("D", i, 0, H2, HD2, o_all, True, 4)
            hold(dve, proj_psum, "D", i, 1)
            link("D", i, v.tensor_tensor(h[:, :, :], h[:, :, :], psG[0:TOK, :].rearrange("p (t d) -> p t d", t=TILES), ALU.add))
            link("D", i, v.tensor_tensor(h[:, :, :], h[:, :, :], bc(rowb["L1_attn_bo"][:, :], 1, [TOK, TILES, D]), ALU.add))
            norm("D", i, 1, tiles(h), u)
            hold(dve, gate_psum, "D", i, 1)
            link("D", i, v.tensor_tensor(s16[:, :, :], psT[0][0:TOK, 0:TILES * E1].rearrange("p (t e) -> p t e", t=TILES),
                                         bc(rowb["L1_ffn_gate_b"][:, :], 1, [TOK, TILES, E1]), ALU.add))
            for t in range(TILES):
                last = v.max(mx[:, t, :], s16[:, t, :])
            link("D", i, last)
            v.tensor_tensor(dlt[:, :], mx[:, :, 1], mx[:, :, 0], ALU.subtract).then_inc(top_diff.sem, 1)
            for t in range(TILES):
                last = v.max_index(ix[:, t, :], mx[:, t, :], s16[:, t, :])
            link("D", i, last)
            link("D", i, v.tensor_copy(ixf[:, :, :], ix[:, :, 0:TOP]))
            pairs = [TOK, TILES * TOP, E1]
            link("D", i, v.tensor_tensor(hot1[:, :, :, :].rearrange("p t k e -> p (t k) e"), bc(iota_f[0:TOK, 0:E1], 1, pairs),
                                         bc(ixf[:, :, :].rearrange("p t k -> p (t k)"), 2, pairs), ALU.is_equal))
            gates(dve, v, "D", i, link)
            link("D", i, v.tensor_tensor(comb2[:, :, :, :].rearrange("p t k e -> p (t k) e"), hot1[:, :, :, :].rearrange("p t k e -> p (t k) e"),
                                         bc(gate[:, :, :].rearrange("p t k -> p (t k)"), 2, pairs), ALU.mult))
            v.tensor_tensor(comb[:, :, :], comb2[:, :, 0, :], comb2[:, :, 1, :], ALU.add).then_inc(comb_ready.sem, 1)
            hold(dve, combT_psum, "D", i, 1)
            v.tensor_copy(combT[:, :], psT[1][0:E1, 0:PAIR]).then_inc(combT_ready.sem, 1)
            hold(dve, beta_psum, "D", i, 1)
            hold(dve, stored, "D", i, 0)
            v.tensor_tensor(acc[:, :, :], h[:, :, :], psG[0:TOK, :].rearrange("p (t d) -> p t d", t=TILES), ALU.add).then_inc(acc_ready.sem, 1)

            def stats(e):
                s = e % 2
                if e >= 2:
                    hold(dve, me_scale, "D", i, e - 1)
                hold(dve, md_psum, "D", i, e + 1)
                for t in range(TILES):
                    last = v.bn_stats(e_st[s][:, t, :], psT[s][0:TOK, t * D:(t + 1) * D])
                last.then_inc(me_stats.sem, 1)
                hold_apart(dve, me_stats, "D", i, e + 1)
                for t in range(TILES):
                    last = v.bn_aggr(e_mv[s][:, t, :], e_st[s][:, t, :])
                last.then_inc(me_var.sem, 1)

            stats(0)
            for e in range(E1):
                s = e % 2
                if e + 1 < E1:
                    stats(e + 1)
                hold(dve, me_scale, "D", i, e + 1)
                if e >= 2:
                    hold(dve, me_g, "D", i, e - 1)
                for t in range(TILES):
                    last = v.tensor_scalar(nrm[s][:, t, :], psT[s][0:TOK, t * D:(t + 1) * D], e_mv[s][:, t, 0:1], e_s[s][:, t:t + 1],
                                           ALU.subtract, ALU.mult)
                last.then_inc(me_norm.sem, 1)
            hold(dve, me_acc, "D", i, E1)
            v.tensor_copy(ex[:, :], dlt[:, :]).then_inc(round_done.sem, 1)
            chain_ends("D")

    @block.tensor
    def _(pe):
        mmul = nc.tensor.matmul
        pe.wait_ge(const_made.sem, CONSTS)
        pe.wait_ge(loaded.sem, 16 * len(loads))
        for k, (src, dst, hd) in enumerate(turns):
            rows, cols = src.shape[1], src.shape[0]
            if k >= RING:
                pe.wait_ge(prep_done.sem, k - RING + 1)
            nc.tensor.transpose(psS[k % RING][0:rows, 0:cols], src, ident[0:cols, 0:cols]).then_inc(prep_psum.sem, 1)
        pe.wait_ge(prep_done.sem, N_TURNS)
        pe.wait_ge(prep_pool.sem, 1)
        for c in range(NC_F):
            last = mmul(psS[0][:, 0:D], frac[:, :], w2w[:, c, :], start=c == 0, stop=c == NC_F - 1)
        last.then_inc(prep_psum.sem, 1)
        for c in range(NC_F):
            last = mmul(psS[1][0:1, 0:D], colc["L0_attn_mln2_b"][:, c:c + 1], w2raw[:, c, :], start=c == 0, stop=c == NC_F - 1)
        last.then_inc(prep_psum.sem, 1)
        pe.wait_ge(prep_done.sem, STEP_B2)
        mmul(psS[2][0:TOK, 0:D], ones[0:1, 0:TOK], b2m_row[:, :], start=True, stop=True).then_inc(prep_psum.sem, 1)
        for n in range(H2):
            pe.wait_ge(prep_done.sem, max(STEP_B2B, STEP_QKV + n - RING))
            for x in range(3):
                last = mmul(psS[n % RING][:, x * HD2:(x + 1) * HD2], wl[:, n, :], qkv1[:, x, n, :], start=True, stop=True)
            last.then_inc(prep_psum.sem, 1)
        for x, ps in ((0, psT[0]), (1, psT[1])):
            for n in range(H2):
                j, g = n % 4, n // 4
                last = mmul(ps[32 * j:32 * j + 32, g:g + 1], qkv1[:, x, n, :], blt[:, n:n + 1], start=True, stop=True)
            last.then_inc(prep_psum.sem, 1)
        for n in range(H2):
            last = mmul(psO[0:1, n * HD2:(n + 1) * HD2], blt[:, n:n + 1], qkv1[:, 2, n, :], start=True, stop=True)
        last.then_inc(prep_psum.sem, 1)
        pe.wait_ge(prep_done.sem, STEP_VB)
        mmul(psG[0:TOK, :], ones[0:1, 0:TOK], vb_row[:, :], start=True, stop=True).then_inc(prep_psum.sem, 1)
        pe.wait_ge(ready.sem, 1)

        with pe.Fori(0, ROUNDS) as i:
            hold(pe, win_in, "A", i, 16 * TILES)
            hold(pe, win_T, "A", i, 0)
            for c in range(3):
                cols = P if c < 2 else WIN - 2 * P
                for t in range(TILES):
                    last = nc.tensor.transpose(psS[c][0:cols, tile(t)], xw[:, t, c * P:c * P + cols], ident[0:TOK, 0:TOK])
                last.then_inc(win_psum.sem, 1)
            hold(pe, win_T, "A", i, 3)
            hold(pe, y_ready, "A", i, 0)
            for c in range(3):
                rows = P if c < 2 else WIN - 2 * P
                last = mmul(psG[:, 0:PAIR], w_tok[0:rows, c, :], big[0:rows, c, :], start=c == 0, stop=c == 2)
            last.then_inc(conv_psum.sem, 1)

        def turn_to_features(phase, i, src):
            for t in range(TILES):
                last = nc.tensor.transpose(psG[:, tile(t)], src[:, t, :], ident[0:TOK, 0:TOK])
            last.then_inc(fm_psum.sem, 1)

        def project(phase, i, k, groups, wq, wk, v_tiles):
            for g in range(groups):
                mmul(psS[g][:, 0:PAIR], wq[g], xT[:, :], start=True, stop=True).then_inc(q_psum.sem, 1)
            v_tiles()
            for g in range(groups):
                hold(pe, q_ready, phase, i, k + g + 1)
                mmul(psS[g][:, 0:PAIR], wk[g], xT[:, :], start=True, stop=True).then_inc(k_psum.sem, 1)

        def attention(phase, i, off, H, hd, vd, v_of, causal_, heads_a_value):
            steps = 2 * H

            def scores(m):
                b, n = m // H, m % H
                j, g = n % 4, n // 4
                hold(pe, k_masked, phase, i, off + m + 1)
                if m >= 4:
                    hold(pe, probs, phase, i, off + m - 3)
                for t in range(2):
                    keys = TOK if causal_ and t == 0 else SEQ
                    at = t * 256
                    last = mmul(psS[j][0:TOK, at:at + keys], qT[:, g, tile(2 * b + t)], k_head[m % 4][:, 0:keys],
                                start=True, stop=not causal_)
                    if causal_:
                        last = mmul(psS[j][0:TOK, at + t * TOK:at + (t + 1) * TOK], ident_h[0:TOK, 0:TOK], causal_h[:, :], start=False, stop=True)
                last.then_inc(scored.sem, 1)

            def turn(m):
                hold(pe, probs, phase, i, off + m + 1)
                if m >= 2:
                    hold(pe, taken[m % 2], phase, i, (off + m) // 2)
                for c in range(2):
                    for t in range(2):
                        if causal_ and t < c:
                            continue
                        last = nc.tensor.transpose(psT[m % 2][0:TOK, c * SEQ + t * TOK:c * SEQ + (t + 1) * TOK],
                                                   prob[m % 2][:, t, c * TOK:(c + 1) * TOK], ident[0:TOK, 0:TOK])
                last.then_inc(turned.sem, 1)

            def mix(m):
                b, n = m // H, m % H
                hold(pe, taken[m % 2], phase, i, (off + m) // 2 + 1)
                if m % 4 == 0 and m >= 8:
                    hold(pe, normed, phase, i, (off + m) // 4 - 1)
                for t in range(2):
                    last_c = 0 if causal_ and t == 0 else 1
                    at = ((n % 4) * 2 + t) * (vd + 1)
                    for c in range(last_c + 1):
                        last = mmul(psPV[(m // 4) % 2][0:TOK, at:at + vd + 1], probT[m % 2][:, c * SEQ + t * TOK:c * SEQ + (t + 1) * TOK],
                                    v_of(2 * b + c, n // heads_a_value), start=c == 0, stop=c == last_c)
                last.then_inc(mixed.sem, 1)

            for m in range(3):
                scores(m)
            for m in range(steps):
                if m + 3 < steps:
                    scores(m + 3)
                turn(m)
                if m:
                    mix(m - 1)
            mix(steps - 1)

        def v_small(phase, i, k, w):
            for t in range(TILES):
                last = mmul(psG[0:TOK, t * D:(t + 1) * D], xT[:, tile(t)], w[:, :], start=True, stop=True)
            last.then_inc(v_psum.sem, 1)

        def out_projection(w):
            for t in range(TILES):
                last = mmul(psS[0][0:TOK, t * D:(t + 1) * D], xT[:, tile(t)], w[:, :], start=True, stop=True)
            last.then_inc(proj_psum.sem, 1)

        with pe.Fori(0, ROUNDS) as i:
            hold(pe, round_done, "B", i, 0)
            hold(pe, hT_ready, "B", i, 1)
            for t in range(TILES):
                last = nc.tensor.transpose(psG[0:TOK, t * D:(t + 1) * D], hT[:, tile(t)], ident[:, :])
            last.then_inc(h_psum.sem, 1)
            hold(pe, ln_out, "B", i, 2)
            turn_to_features("B", i, n_)
            hold(pe, fm_ready, "B", i, 1)
            project("B", i, 0, 4, [wq0[:, g, :] for g in range(4)], [wk0[:, g, :] for g in range(4)], lambda: v_small("B", i, 1, wv0))
            hold(pe, k_ready, "B", i, 4)
            hold(pe, v_ready, "B", i, 1)
            attention("B", i, 0, H0, HD0, VD0, lambda t, n: v17[:, t, n, :], False, H0 // V0)
            hold(pe, diff_out, "B", i, 1)
            turn_to_features("B", i, n_)
            hold(pe, fm_ready, "B", i, 2)
            out_projection(wo0)
            hold(pe, ln_out, "B", i, 4)
            turn_to_features("B", i, n_)
            hold(pe, fm_ready, "B", i, 3)
            for c in range(NC_F):
                mmul(psS[c][:, 0:PAIR], w1m[:, c * P:(c + 1) * P], xT[:, :], start=True, stop=True).then_inc(up_psum.sem, 1)
            hold(pe, up_act, "B", i, NC_F)
            for t in range(TILES):
                at = (t % 2) * (D + 2)
                for c in range(NC_F):
                    mmul(psT[t // 2][0:TOK, at:at + D + 1], big[:, c, tile(t)], w2m[:, c, :], start=c == 0, stop=c == NC_F - 1)
                if t == 0:
                    hold(pe, up_sq, "B", i, NC_F)
                for c in range(NC_F):
                    last = mmul(psT[t // 2][0:TOK, at + D + 1:at + D + 2], sq[:, c, tile(t)], frac[:, 0:1], start=c == 0, stop=c == NC_F - 1)
            last.then_inc(down_psum.sem, 1)
            hold(pe, ln_out, "B", i, 6)
            turn_to_features("B", i, n_)
            hold(pe, fm_ready, "B", i, 4)
            project("B", i, 4, 2, [wq1[:, g, :] for g in range(2)], [wk1[:, g, :] for g in range(2)], lambda: v_small("B", i, 2, wv1))
            hold(pe, k_ready, "B", i, 6)
            hold(pe, v_ready, "B", i, 2)
            attention("B", i, 2 * H0, H1, HD1, HD1, lambda t, n: v17[:, t, n, :], False, 1)
            hold(pe, normed, "B", i, HEADS_B // 4)
            turn_to_features("B", i, n_)
            hold(pe, fm_ready, "B", i, 5)
            out_projection(wo1)
            hold(pe, x2_ready, "B", i, 1)
            turn_to_features("B", i, x2)
            hold(pe, fm_ready, "B", i, 6)
            for t in range(TILES):
                last = mmul(psS[1][0:TOK, t * E0:(t + 1) * E0], xT[:, tile(t)], wr[:, :], start=True, stop=True)
            last.then_inc(route_psum.sem, 1)
            hold(pe, hot_ready, "B", i, 1)
            for t in range(TILES):
                for t2 in range(t + 1):
                    lhs = before if t2 == t else ones
                    mmul(psT[0][0:TOK, t * E0:(t + 1) * E0], lhs[0:TOK, 0:TOK], hots[:, t2, :], start=t2 == 0, stop=t2 == t)
            for t in range(TILES):
                last = mmul(psT[1][0:TOK, 0:E0], ones[0:TOK, 0:TOK], hots[:, t, :], start=t == 0, stop=t == TILES - 1)
            last.then_inc(rank_psum.sem, 1)

        pe.wait_ge(round_done.sem, round_done.value("C", 0, 0))

        def rows_to_features(i, s):
            p, q = s % 2, s // 2
            if s < N:
                hold(pe, ew_in[s], "C", i, 16 * 4)
            else:
                hold(pe, ew_in[s - N], "C", i, 2 * 16 * 4)
            hold(pe, xe_T[p], "C", i, q)
            for t in range(2):
                last = nc.tensor.transpose((psG, psO)[p][:, tile(t)], xe[s % N][:, t, :], ident[0:TOK, 0:TOK])
            last.then_inc(xe_psum[p].sem, 1)

        def expert_up(i, s):
            p, q = s % 2, s // 2
            hold(pe, xe_T[p], "C", i, q + 1)
            for half in range(2):
                hold(pe, eu_act[p], "C", i, 2 * q)
                for c in (2 * half, 2 * half + 1):
                    last = mmul(psS[2 * p + half][:, (c % 2) * 256:(c % 2) * 256 + CAP], we1[s % N][:, c * P:(c + 1) * P], xeT[p][:, :],
                                start=True, stop=True)
                last.then_inc(eu_psum[p].sem, 1)

        def expert_down(i, s):
            p, q = s % 2, s // 2
            hold(pe, eu_act[p], "C", i, 2 * q + 2)
            hold(pe, ye_ready[p], "C", i, q)
            for t in range(2):
                for c in range(NC_F):
                    mmul(psT[p][0:TOK, t * D:(t + 1) * D], he[p][:, c, tile(t)], we2[s][:, c, :], start=c == 0, stop=False)
                last = mmul(psT[p][0:TOK, t * D:(t + 1) * D], ones[0:1, 0:TOK], be2[s][:, :], start=False, stop=True)
            last.then_inc(ed_psum[s].sem, 1)

        def expert_round(i, ahead):
            for s in range(N):
                if s + 2 < N or ahead:
                    rows_to_features(i, s + 2)
                if s + 1 < N or ahead:
                    expert_up(i, s + 1)
                expert_down(i, s)

        rows_to_features(0, 0)
        rows_to_features(0, 1)
        expert_up(0, 0)
        with pe.Fori(0, C_ROUNDS - 1) as i:
            expert_round(i, True)
        expert_round(C_ROUNDS - 1, False)

        with pe.Fori(0, ROUNDS) as i:
            hold(pe, round_done, "D", i, 0)
            hold(pe, ln_out, "D", i, 1)
            turn_to_features("D", i, u)
            hold(pe, fm_ready, "D", i, 1)

            def v_wide():
                for t, ps in enumerate((psT[0], psT[1], psO, psG)):
                    mmul(ps[0:TOK, :], xT[:, tile(t)], wv2[:, :], start=True, stop=True).then_inc(v_psum.sem, 1)

            project("D", i, 0, 4, [wq2[:, g * P:(g + 1) * P] for g in range(4)], [wk2[:, g * P:(g + 1) * P] for g in range(4)], v_wide)
            hold(pe, k_ready, "D", i, 4)
            hold(pe, v_ready, "D", i, 4)
            attention("D", i, 0, H2, HD2, HD2, lambda t, n: v33[:, t, n, :], True, 1)
            hold(pe, normed, "D", i, HEADS_D // 4)
            for c in range(4):
                for t in range(TILES):
                    last = nc.tensor.transpose(psS[c][:, tile(t)], o_all[:, t, c * P:(c + 1) * P], ident[0:TOK, 0:TOK])
                last.then_inc(cat_psum.sem, 1)
            hold(pe, cat_T, "D", i, 4)
            for t in range(TILES):
                for c in range(4):
                    last = mmul(psG[0:TOK, t * D:(t + 1) * D], big[:, c, tile(t)], wo2[:, c, :], start=c == 0, stop=c == 3)
            last.then_inc(proj_psum.sem, 1)
            hold(pe, ln_out, "D", i, 2)
            turn_to_features("D", i, u)
            hold(pe, fm_ready, "D", i, 2)
            for t in range(TILES):
                last = mmul(psT[0][0:TOK, t * E1:(t + 1) * E1], xT[:, tile(t)], gate_w[:, :], start=True, stop=True)
            last.then_inc(gate_psum.sem, 1)
            hold(pe, comb_ready, "D", i, 1)
            pe.wait_ge(loaded_e.sem, 16 * len(expert_loads))
            for t in range(TILES):
                last = nc.tensor.transpose(psT[1][0:E1, tile(t)], comb[:, t, :], ident[0:TOK, 0:TOK])
            last.then_inc(combT_psum.sem, 1)
            hold(pe, combT_ready, "D", i, 1)
            for t in range(TILES):
                last = mmul(psG[0:TOK, t * D:(t + 1) * D], combT[:, tile(t)], beta_e[:, :], start=True, stop=True)
            last.then_inc(beta_psum.sem, 1)

            def up(e):
                s = e % 2
                for c in range(2):
                    if e >= 2:
                        hold(pe, mu_act, "D", i, 2 * (e - 2) + c + 1)
                    mmul(psS[2 * s + c][:, 0:PAIR], w1e[:, e, c * P:(c + 1) * P], xT[:, :], start=True, stop=True).then_inc(mu_psum.sem, 1)

            def down(e):
                s = e % 2
                hold(pe, mu_act, "D", i, 2 * e + 2)
                if e >= 2:
                    hold(pe, me_norm, "D", i, e - 1)
                for t in range(TILES):
                    for c in range(2):
                        mmul(psT[s][0:TOK, t * D:(t + 1) * D], hm[s][:, c, tile(t)], w2e[:, e, c, :], start=c == 0, stop=False)
                    last = mmul(psT[s][0:TOK, t * D:(t + 1) * D], ones[0:1, 0:TOK], b2_row1[:, e, :], start=False, stop=True)
                last.then_inc(md_psum.sem, 1)

            up(0)
            for e in range(E1):
                if e + 1 < E1:
                    up(e + 1)
                down(e)


_OUT = (BATCH, SEQ, D)


def kernel(**inputs):
    import numpy as _np
    import concourse.bacc as _bacc
    from concourse import mybir as _mybir
    from concourse.bass_utils import run_bass_kernel_spmd as _run

    nc = _bacc.Bacc("TRN2", target_bir_lowering=False, num_devices=1)
    arrays, handles = {}, {}
    for name, value in inputs.items():
        a = _np.ascontiguousarray(value)
        arrays["in_" + name] = a
        handles[name] = nc.dram_tensor("in_" + name, a.shape, _mybir.dt.from_np(a.dtype), kind="ExternalInput").ap()
    result = nc.dram_tensor("result", _OUT, _mybir.dt.float32, kind="ExternalOutput").ap()
    build(nc, handles, result)
    r = _run(nc, [arrays], core_ids=[0])
    return r.results[0]["result"]
```

```python
import numpy as np
import concourse.bass as bass
from concourse import mybir
from contextlib import ExitStack

F32 = mybir.dt.float32
BF16 = mybir.dt.bfloat16
U32 = mybir.dt.uint32
I32 = mybir.dt.int32
ALU = mybir.AluOpType
ACT = mybir.ActivationFunctionType
AX = mybir.AxisListType

P = 128
BATCH, FRAMES, CH = 16, 256, 64
CONTEXT = 5
SEQ = FRAMES - (CONTEXT - 1)
WIN = CONTEXT * CH
D = 128
TOK = SEQ // 2
TILES = 4
PAIR = TILES * TOK
ROUNDS = BATCH // 2
N_TOKENS = BATCH * SEQ
EPS = 1e-5
H0, HD0 = 16, 8
V0, VD0 = 8, 16
LAMBDA_INIT = 0.8 - 0.6 * float(np.exp(-0.3 * 0))
MLP = 512
H1, HD1 = 8, 16
E0, F0 = 64, 512
TOP = 2
CAP = 2 * (N_TOKENS * TOP // E0)
H2, HD2 = 16, 32
E1, F1 = 16, 256
EXPERTS_A_ROUND = 4
TAIL_LINKS = 17
C_ROUNDS = E0 // EXPERTS_A_ROUND
DROPPED = 1 << 15
MASKED = -1e30
NC_F = MLP // P
SPLIT = 3
ZERO_ROWS = 16

assert CAP == SEQ and LAMBDA_INIT > 0

PHASE_ROUNDS = {"S": 1, "A": ROUNDS, "B": ROUNDS, "C": C_ROUNDS, "P": 1, "D": ROUNDS}


class Signal:

    def __init__(self, sem, growth):
        self.sem, self.growth, self.start = sem, growth, {}
        total = 0
        for phase, rounds in PHASE_ROUNDS.items():
            self.start[phase] = total
            total += rounds * growth.get(phase, 0)

    def value(self, phase, i, n):
        base = self.start[phase] + n
        return i * self.growth.get(phase, 0) + base


def build(nc, T, out):
    with ExitStack() as ctx:
        build_in(nc, T, out, ctx)


def build_in(nc, T, out, ctx):
    def sb(name, shape, dt=F32):
        return ctx.enter_context(nc.sbuf_tensor(name, shape, dt))

    def part(of, at, shape):
        size = int(np.prod(shape[1:]))
        ap = of[0:shape[0], at:at + size]
        if len(shape) == 2:
            return ap
        names = "abc"[:len(shape) - 1]
        return ap.rearrange(f"p ({' '.join(names)}) -> p {' '.join(names)}", **dict(zip(names, shape[1:])))

    def parts(of, at, *shapes):
        found = []
        for shape in shapes:
            found.append(part(of, at, shape))
            at += int(np.prod(shape[1:]))
        assert at <= of.shape[1], at
        return found

    def signal(name, **growth):
        return Signal(ctx.enter_context(nc.semaphore(name)), growth)

    slot_x = nc.dram_tensor("slot_x", [E0 * CAP, D], F32, kind="Internal").ap()
    slot_y = nc.dram_tensor("slot_y", [E0 * CAP, D], F32, kind="Internal").ap()

    psS = [ctx.enter_context(nc.psum_tensor(f"psS{j}", [P, 512], F32)) for j in range(4)]
    psT = [ctx.enter_context(nc.psum_tensor(f"psT{j}", [P, 512], F32)) for j in range(2)]
    psO = ctx.enter_context(nc.psum_tensor("psO", [P, 512], F32))
    psG = ctx.enter_context(nc.psum_tensor("psG", [P, 512], F32))
    psPV = [psO, psG]
    ps_down = [psT[0], psT[1], psO]

    LATE = 7232
    arena = sb("arena", [P, LATE + 2 * E1 * D])
    y_all = sb("y_all", [P, E1 * F1])
    ident = sb("ident", [P, P])
    before = sb("before", [P, P])
    ones = sb("ones", [P, P])
    frac = sb("frac", [P, P])
    causal = sb("causal", [TOK, TOK])
    causal_h = sb("causal_h", [TOK, TOK], BF16)
    ident_h = sb("ident_h", [P, P], BF16)
    eps_t = sb("eps_t", [P, 32])
    mhalf = sb("mhalf", [P, 32])
    iota_i = sb("iota_i", [P, E0], I32)
    iota_f = sb("iota_f", [P, E0])

    colv = {n: sb("c_" + n, [P, 1]) for n in
            ("L0_tok_b", "L0_tok_gamma", "L0_tok_beta", "L0_attn_n1_w", "L0_attn_n1_b", "L0_attn_mln1_w",
             "L0_attn_mln1_b", "L0_ffn_ln1_g", "L0_ffn_ln1_b", "sub_w", "sub_w8")}
    colc = {n: sb("k_" + n, [P, NC_F]) for n in ("L0_attn_mb1", "L0_attn_mln2_w", "L0_attn_mln2_b")}
    rowb = {n: sb("r_" + n, [TOK, T[n].shape[0]]) for n in
            ("L0_attn_n2_w", "L0_attn_n2_b", "L0_ffn_ln2_g", "L0_ffn_ln2_b", "L1_attn_bo", "L1_ffn_gate_b",
             "L0_attn_lq1", "L0_attn_lk1", "L0_attn_lq2", "L0_attn_lk2")}
    beta_e = sb("beta_e", [E1, D])

    zero_t, nat_tok, nat_q, nat_k, nat_v, nat_o, nat_m1, nat_m2, nat_fq, nat_fk, nat_b1, nat_bl, nat_wo1, nat_b11, \
        w2raw, w2w, b2m_row, mb2_row, qkv1 = parts(
            arena, 0, [126, ZERO_ROWS * D], [P, WIN], [P, P], [P, P], [P, P], [P, P], [P, NC_F, P], [P, MLP], [P, D],
            [P, D], [E0, F0], [H2, D], [P, H2 * HD2], [E1, F1], [P, NC_F, D], [P, NC_F, D], [1, D], [1, D],
            [P, 3, H2, HD2])
    nat = {"Wq": nat_q, "Wk": nat_k, "Wv": nat_v, "Wo": nat_o}
    wl = part(y_all, 0, [P, H2, D])
    gamma_b, b2_rows = parts(arena, LATE, [TOK, E1, D], [SPLIT, E1, D])

    w_tok = sb("w_tok", [P, 3, D])
    wq0 = sb("wq0", [P, 4, P])
    wk0 = sb("wk0", [P, 4, P])
    wv0 = sb("wv0", [P, D])
    wo0 = sb("wo0", [P, D])
    w1m = sb("w1m", [P, MLP])
    w2m = sb("w2m", [P, NC_F, D + 1])
    b2m = sb("b2m", [TOK, D])
    neg_lam = sb("neg_lam", [TOK, 1])
    lam_t = sb("lam_t", [TOK, 2, HD0])
    lam_s = sb("lam_s", [TOK, 2])
    lam_e = sb("lam_e", [TOK, 2])
    wq1 = sb("wq1", [P, 2, P])
    wk1 = sb("wk1", [P, 2, P])
    wv1 = sb("wv1", [P, D])
    wo1 = sb("wo1", [P, D])
    wr = sb("wr", [P, E0])
    b1t = sb("b1t", [P, NC_F, E0])
    blt = sb("blt", [P, H2])
    wq2 = sb("wq2", [P, H2 * HD2])
    wk2 = sb("wk2", [P, H2 * HD2])
    wv2 = sb("wv2", [P, H2 * HD2])
    qb2 = sb("qb2", [P, 4])
    kb2 = sb("kb2", [P, 4])
    vb_row = sb("vb_row", [1, H2 * HD2])
    vb2 = sb("vb2", [TOK, H2 * HD2])
    wo2 = sb("wo2", [P, 4, D])
    gate_w = sb("gate_w", [P, E1])
    b1e = sb("b1e", [P, 2, E1])
    w1e = part(y_all, 0, [P, E1, F1])
    w2e = sb("w2e", [P, E1, 2, D])

    ones_h = sb("ones_h", [SPLIT, TOK], BF16)
    b2_split = sb("b2_split", [SPLIT, E1, D], BF16)
    b2_part = sb("b2_part", [SPLIT, E1 // 2, D], BF16)

    y_stats = sb("y_stats", [P, ROUNDS * 6])
    bn_mv = sb("bn_mv", [P, 2])
    bn_e = sb("bn_e", [P, 1])
    bn_r = sb("bn_r", [P, 1])
    bn_s = sb("bn_s", [P, 1])
    bn_m = sb("bn_m", [P, 1])
    bn_c = sb("bn_c", [P, 1])
    hx_all = sb("hx_all", [TOK, ROUNDS * TILES * D])
    gates_all = sb("gates_all", [TOK, ROUNDS * TILES * TOP])
    slots_all = sb("slots_all", [TOK, (ROUNDS + 1) * TILES * TOP], U32)

    hT = sb("hT", [P, PAIR])
    h = sb("h", [TOK, TILES, D])
    u = sb("u", [TOK, TILES, D])
    n_ = sb("n_", [TOK, TILES, D])
    h1 = sb("h1", [TOK, TILES, D])
    xT = sb("xT", [P, PAIR])
    qT = sb("qT", [P, 4, PAIR])
    kT = sb("kT", [P, 4, PAIR])
    b2_left = [x[0:SPLIT, :, :].rearrange("p a b -> p (a b)")[:, 0:E1 // 2 * D].rearrange("p (e d) -> p e d", d=D) for x in (qT, kT)]
    big, sq = qT, kT
    v17 = sb("v17", [TOK, TILES, 8, 17])
    head_rows = sb("head_rows", [P, 4])
    k_head = [sb(f"k_head{j}", [P, SEQ]) for j in range(4)]
    nmax = sb("nmax", [TOK, 4, 2])
    prob = [sb(f"prob{j}", [TOK, 2, SEQ]) for j in range(2)]
    probT = [sb(f"probT{j}", [TOK, 2 * SEQ]) for j in range(2)]
    rden = sb("rden", [TOK, 2, 8])
    o_all = sb("o_all", [TOK, TILES, H2 * HD2])
    xw = o_all[:, :, 0:WIN]
    oc = sb("oc", [TOK, TILES * V0, VD0])
    ocs = sb("ocs", [TOK, TILES * V0, VD0])
    ms = sb("ms", [TOK, TILES * V0])
    ms1 = sb("ms1", [TOK, TILES * V0])
    ms2 = sb("ms2", [TOK, TILES * V0])
    again_v = sb("again_v", [TOK, TILES])
    again_w = sb("again_w", [TOK, TILES])
    again_e = sb("again_e", [TOK, TILES])
    again_r = sb("again_r", [TOK, TILES])
    ln_st = sb("ln_st", [TOK, TILES, 6])
    ln_mv = sb("ln_mv", [TOK, TILES, 2])
    ln_e = sb("ln_e", [TOK, TILES])
    ln_r = sb("ln_r", [TOK, TILES])
    mm = sb("mm", [TOK, TILES, 2])
    mm2 = sb("mm2", [TOK, TILES])
    lg = sb("lg", [TOK, TILES, E0])
    mx = sb("mx", [TOK, TILES, 8])
    ix = sb("ix", [TOK, TILES, 8], U32)
    ixf = sb("ixf", [TOK, TILES, TOP])
    dlt = sb("dlt", [TOK, TILES])
    ex = sb("ex", [TOK, TILES])
    den = sb("den", [TOK, TILES])
    gate = sb("gate", [TOK, TILES, TOP])
    hot = sb("hot", [TOK, TILES, TOP, E0])
    hots = sb("hots", [TOK, TILES, E0])
    pos_e = sb("pos_e", [TOK, TILES, E0])
    carry = sb("carry", [TOK, E0])
    pos_h = sb("pos_h", [TOK, TILES, TOP, E0])
    pos = sb("pos", [TOK, TILES * TOP])
    keep = sb("keep", [TOK, TILES * TOP])
    slot_f = sb("slot_f", [TOK, TILES * TOP])
    drop_f = sb("drop_f", [TOK, TILES * TOP])
    slot_s = sb("slot_s", [TOK, TILES * TOP])
    slot_l = sb("slot_l", [TOK, TILES * TOP])
    slot_u = sb("slot_u", [TOK, TILES * TOP], U32)
    x2 = sb("x2", [TOK, TILES, D])
    q1, k1, v17m, hm_, um_, om = parts(arena, ZERO_ROWS * D, [P, 2, PAIR], [P, 2, PAIR], [TOK, TILES, 8, 17],
                                       [TOK, TILES, D], [TOK, TILES, D], [TOK, TILES, D])
    SETS = EXPERTS_A_ROUND
    SET = 2 * F0 + D + 2 * D
    loads_in_flight = [parts(arena, s * SET, [P, F0], [P, NC_F, D], [1, D], [TOK, 2, D]) for s in range(SETS)]
    we1, we2, be2, xe = zip(*loads_in_flight)
    xeT0, xeT1, ye0, ye1 = parts(arena, SETS * SET, [P, CAP], [P, CAP], [TOK, 2, D], [TOK, 2, D])
    xeT, ye = (xeT0, xeT1), (ye0, ye1)
    he = [x[:, :, 0:CAP] for x in (qT, kT)]
    v33, gy, hm_both, nrm0, nrm1, acc = parts(
        arena, 0, [TOK, TILES, H2, HD2 + 1], [TOK, TILES * TOP, D], [P, 4, PAIR], [TOK, TILES, D],
        [TOK, TILES, D], [TOK, TILES, D])
    cat_b = hm_both
    hm, nrm = (hm_both[:, 0:2, :], hm_both[:, 2:4, :]), (nrm0, nrm1)
    slot_c = sb("slot_c", [TOK, TILES * TOP], U32)
    gate_c = sb("gate_c", [TOK, TILES * TOP])
    hot1 = sb("hot1", [TOK, TILES, TOP, E1])
    comb2 = sb("comb2", [TOK, TILES, TOP, E1])
    comb = sb("comb", [TOK, TILES, E1])
    combT = sb("combT", [E1, PAIR])
    s16 = sb("s16", [TOK, TILES, E1])
    e_st = [sb(f"e_st{s}", [TOK, TILES, 6]) for s in range(2)]
    e_mv = [sb(f"e_mv{s}", [TOK, TILES, 2]) for s in range(2)]
    e_e = sb("e_e", [TOK, TILES])
    e_r = sb("e_r", [TOK, TILES])
    e_s = [sb(f"e_s{s}", [TOK, TILES]) for s in range(2)]

    LN_B, LN_D = 4, 2
    FM_B, FM_D = 4, 2
    HEADS_B, HEADS_D = 2 * (H0 + H1), 2 * H2
    loaded = signal("loaded", S=0)
    loaded_e = signal("loaded_e", S=0)
    const_made = signal("const_made", S=0)
    prep_psum = signal("prep_psum", S=0)
    prep_done = signal("prep_done", S=0)
    prep_pool = signal("prep_pool", S=0)
    prep_act = signal("prep_act", S=0)
    cleared = signal("cleared", S=0)
    dve_link = signal("dve_link", S=0)
    ready = signal("ready", S=0)

    win_in = signal("win_in", A=16 * TILES)
    win_psum = signal("win_psum", A=3)
    win_T = signal("win_T", A=3)
    conv_psum = signal("conv_psum", A=1)
    y_ready = signal("y_ready", A=1)
    y_counted = signal("y_counted", A=1)
    bn_link = signal("bn_link")
    bn_pool = signal("bn_pool")
    bn_ready = signal("bn_ready")

    round_done = signal("round_done", B=1)
    hT_ready = signal("hT_ready", B=1)
    h_psum = signal("h_psum", B=1)
    h_ready = signal("h_ready", B=1)
    ln_stats = signal("ln_stats", B=LN_B, D=LN_D)
    ln_aggr = signal("ln_aggr", B=LN_B, D=LN_D)
    ln_eps = signal("ln_eps", B=LN_B, D=LN_D)
    ln_rstd = signal("ln_rstd", B=LN_B, D=LN_D)
    ln_out = signal("ln_out", B=LN_B, D=LN_D)
    again_link = signal("again_link", B=2 * 3)
    again_rstd = signal("again_rstd", B=2)
    again_out = signal("again_out", B=2)
    fm_psum = signal("fm_psum", B=FM_B, D=FM_D)
    fm_ready = signal("fm_ready", B=FM_B, D=FM_D)
    q_psum = signal("q_psum", B=4 + 2, D=4)
    q_ready = signal("q_ready", B=4 + 2, D=4)
    k_psum = signal("k_psum", B=4 + 2, D=4)
    k_ready = signal("k_ready", B=4 + 2, D=4)
    v_psum = signal("v_psum", B=2, D=4)
    v_ready = signal("v_ready", B=2, D=4)
    scored = signal("scored", B=HEADS_B, D=HEADS_D)
    k_masked = signal("k_masked", B=HEADS_B, D=HEADS_D)
    maxed = signal("maxed", B=HEADS_B, D=HEADS_D)
    probs = signal("probs", B=HEADS_B, D=HEADS_D)
    turned = signal("turned", B=HEADS_B, D=HEADS_D)
    taken = [signal(f"taken{j}", B=HEADS_B // 2, D=HEADS_D // 2) for j in range(2)]
    mixed = signal("mixed", B=HEADS_B, D=HEADS_D)
    recip = signal("recip", B=HEADS_B // 4, D=HEADS_D // 4)
    normed = signal("normed", B=HEADS_B // 4, D=HEADS_D // 4)
    chain = signal("chain", B=11, D=11)
    diff_ms = signal("diff_ms", B=1)
    diff_e = signal("diff_e", B=1)
    diff_r = signal("diff_r", B=1)
    diff_out = signal("diff_out", B=1)
    proj_psum = signal("proj_psum", B=1, D=1)
    up_psum = signal("up_psum", B=4)
    up_act = signal("up_act", B=4)
    up_sq = signal("up_sq", B=4)
    down_psum = signal("down_psum", B=1)
    down_var = signal("down_var", B=1)
    down_e = signal("down_e", B=1)
    down_r = signal("down_r", B=1)
    x2_ready = signal("x2_ready", B=1)
    tail_fm_psum = signal("tail_fm_psum", B=2)
    tail_fm_ready = signal("tail_fm_ready", B=2)
    tail_proj = signal("tail_proj", B=1)
    tail_chain = signal("tail_chain", B=TAIL_LINKS)
    tail_stats = signal("tail_stats", B=1)
    tail_aggr = signal("tail_aggr", B=1)
    tail_eps = signal("tail_eps", B=1)
    tail_rstd = signal("tail_rstd", B=1)
    tail_out = signal("tail_out", B=1)
    route_psum = signal("route_psum", B=1)
    top_diff = signal("top_diff", B=1, D=1)
    top_exp = signal("top_exp", B=1, D=1)
    hot_ready = signal("hot_ready", B=1)
    rank_psum = signal("rank_psum", B=1)
    slots_ready = signal("slots_ready", B=1)
    scattered = signal("scattered", B=16 * TILES * TOP)

    N = EXPERTS_A_ROUND
    ew_in = [signal(f"ew_in{s}", C=16 * 4) for s in range(N)]
    xe_psum = [signal(f"xe_psum{s}", C=N // 2) for s in range(2)]
    xe_T = [signal(f"xe_T{s}", C=N // 2) for s in range(2)]
    eu_psum = [signal(f"eu_psum{s}", C=N) for s in range(2)]
    eu_act = [signal(f"eu_act{s}", C=N) for s in range(2)]
    ed_psum = [signal(f"ed_psum{s}", C=1) for s in range(N)]
    ye_ready = [signal(f"ye_ready{s}", C=N // 2) for s in range(2)]
    ye_out = [signal(f"ye_out{s}", C=16 * N // 2) for s in range(2)]

    b2_link = signal("b2_link")
    idx_ready = signal("idx_ready", P=1, D=1)
    gathered = signal("gathered", P=16 * TILES * TOP, D=16 * TILES * TOP)
    next_chain = signal("next_chain", D=2)
    gy_used = signal("gy_used", D=1)
    cat_psum = signal("cat_psum", D=8)
    cat_T = signal("cat_T", D=8)
    gate_psum = signal("gate_psum", D=1)
    comb_ready = signal("comb_ready", D=1)
    combT_psum = signal("combT_psum", D=1)
    combT_ready = signal("combT_ready", D=1)
    beta_psum = signal("beta_psum", D=1)
    acc_ready = signal("acc_ready", D=1)
    mu_psum = signal("mu_psum", D=2 * E1)
    mu_act = signal("mu_act", D=2 * E1)
    md_psum = signal("md_psum", D=E1)
    me_stats = signal("me_stats", D=E1)
    me_var = signal("me_var", D=E1)
    me_e = signal("me_e", D=E1)
    me_r = signal("me_r", D=E1)
    me_scale = signal("me_scale", D=E1)
    me_norm = signal("me_norm", D=E1)
    me_g = signal("me_g", D=E1)
    me_acc = signal("me_acc", D=E1)
    stored = signal("stored", D=16)

    due = {}

    def hold(eng, sig, phase, i, n):
        eng.wait_ge(sig.sem, sig.value(phase, i, n))

    def hold_apart(eng, sig, phase, i, n):
        name = str(eng.engine)
        if name not in due:
            due[name] = eng.alloc_register(f"due_{len(due)}")
        eng.reg_mov(due[name], sig.value(phase, i, n))
        eng.wait_ge(ready.sem, 1)
        eng.wait_ge(sig.sem, due[name])

    def bc(ap, axis, shape):
        return ap.unsqueeze(axis).broadcast_to(shape)

    tile = lambda t: slice(t * TOK, (t + 1) * TOK)

    def column(name):
        return T[name].rearrange("(p o) -> p o", o=1)

    loads = [(nat_tok[:, :], T["L0_tok_W"])]
    loads += [(nat[n][:, :], T["L0_attn_" + n]) for n in ("Wq", "Wk", "Wv", "Wo")]
    loads += [(colv[n][:, :], column(n)) for n in colv if n in T]
    loads += [(colv["sub_w"][j * VD0:(j + 1) * VD0, :], column("L0_attn_subln_w")) for j in range(V0)]
    loads += [(colc[n][:, c:c + 1], T[n][c * P:(c + 1) * P].rearrange("(p o) -> p o", o=1))
              for n in colc for c in range(NC_F)]
    loads += [(rowb[n][:, :], T[n].partition_broadcast(TOK)) for n in rowb]
    loads += [
        (mb2_row[:, :], T["L0_attn_mb2"].rearrange("(o d) -> o d", o=1)),
        (nat_m1[:, :, :], T["L0_attn_mW1"].rearrange("(c p) d -> p c d", p=P)),
        (nat_m2[:, :], T["L0_attn_mW2"]),
        (nat_fq[:, :], T["L0_ffn_wq"]), (nat_fk[:, :], T["L0_ffn_wk"]),
        (wv1[:, :], T["L0_ffn_wv"]), (wo1[:, :], T["L0_ffn_wo"]), (wr[:, :], T["L0_ffn_wr"]),
        (nat_b1[:, :], T["L0_ffn_b1"]), (nat_bl[:, :], T["L1_attn_bl"]), (nat_wo1[:, :], T["L1_attn_Wo"]),
        (nat_b11[:, :], T["L1_ffn_b1"]), (wl[:, :, :], T["L1_attn_Wl"].rearrange("h o i -> o h i")),
        (qkv1[:, 0, :, :], T["L1_attn_Wq"].rearrange("h i d -> i h d")),
        (qkv1[:, 1, :, :], T["L1_attn_Wk"].rearrange("h i d -> i h d")),
        (qkv1[:, 2, :, :], T["L1_attn_Wv"].rearrange("h i d -> i h d")),
        (gate_w[:, :], T["L1_ffn_gate_w"]),
        (b2_rows[:, :, :].rearrange("o e d -> o (e d)"), T["L1_ffn_b2"].rearrange("e d -> (e d)").partition_broadcast(SPLIT)),
    ]
    expert_loads = [
        (w1e[:, :, :], T["L1_ffn_w1"].rearrange("e d f -> d e f")),
        (w2e[:, :, :, :].rearrange("p e c d -> p (e c) d"), T["L1_ffn_w2"].rearrange("e (c p) d -> p (e c) d", p=P)),
        (gamma_b[:, :, :].rearrange("p e d -> p (e d)"), T["L1_ffn_gamma"].rearrange("e d -> (e d)").partition_broadcast(TOK)),
        (beta_e[:, :], T["L1_ffn_beta"]),
    ]

    def heads(ap, n, hd):
        return ap.rearrange("p (n d) -> p n d", d=hd)

    turns = [(nat_tok[:, 0:128], w_tok[:, 0, :], None), (nat_tok[:, 128:256], w_tok[:, 1, :], None),
             (nat_tok[:, 256:320], w_tok[0:64, 2, :], None)]
    for n, w in (("Wq", wq0), ("Wk", wk0)):
        turns.append((nat[n][:, :], w[:, :, :].rearrange("p g (j s) -> p (g j) s", s=32)[:, :, 0:HD0], HD0))
    turns += [(nat["Wv"][:, :], wv0[:, :], None), (nat["Wo"][:, :], wo0[:, :], None)]
    for c in range(NC_F):
        turns.append((nat_m1[:, c, :], w1m[:, c * P:(c + 1) * P], None))
        turns.append((nat_m2[:, c * P:(c + 1) * P], w2raw[:, c, :], None))
        turns.append((nat_wo1[:, c * P:(c + 1) * P], wo2[:, c, :], None))
        turns.append((nat_b1[:, c * P:(c + 1) * P], b1t[:, c, :], None))
    turns.append((nat_bl[:, :], blt[:, :], None))
    for c in range(2):
        turns.append((nat_b11[:, c * P:(c + 1) * P], b1e[:, c, :], None))
    RING = 4
    N_TURNS = len(turns)
    STEP_MEAN, STEP_B2, STEP_B2B, STEP_QKV, STEP_QB, STEP_KB, STEP_VB, STEP_VBB = (
        N_TURNS + 1, N_TURNS + 2, N_TURNS + 3, N_TURNS + 4, N_TURNS + 4 + H2, N_TURNS + 5 + H2,
        N_TURNS + 6 + H2, N_TURNS + 7 + H2)

    def take_turned(eng, copy, phase, i, off, m, causal_):
        hold(eng, turned, phase, i, off + m + 1)
        if m >= 2:
            hold(eng, mixed, phase, i, off + m - 1)
        if causal_:
            copy(eng, probT[m % 2][:, 0:SEQ], psT[m % 2][0:TOK, 0:SEQ])
            copy(eng, probT[m % 2][:, SEQ + TOK:2 * SEQ], psT[m % 2][0:TOK, SEQ + TOK:2 * SEQ]).then_inc(taken[m % 2].sem, 1)
        else:
            copy(eng, probT[m % 2][:, :], psT[m % 2][0:TOK, 0:2 * SEQ]).then_inc(taken[m % 2].sem, 1)

    def gates(dve, v, phase, i, link):
        hold(dve, top_exp, phase, i, 1)
        link(phase, i, v.tensor_scalar(den[:, :], ex[:, :], 1.0, None, ALU.add))
        link(phase, i, v.reciprocal(gate[:, :, 0], den[:, :]))
        link(phase, i, v.tensor_tensor(gate[:, :, 1], ex[:, :], gate[:, :, 0], ALU.mult))

    HEAD_FM, HEAD_Q, HEAD_V = 6, 8, 13
    TAIL_X2, TAIL_TOP, TAIL_RANK = 8, 14, 17
    NEXT_NORM, NEXT_Q = 3, 6
    CAT = 18

    def s_ring(phase):
        return 3

    def pv_banks(phase):
        return psPV[:1]

    CONSTS = 3 + 3 + 7 + 1 + 4 + 1
    CLEARS = E0 * CAP // (126 * ZERO_ROWS)

    block = ctx.enter_context(nc.Block())

    @block.sync
    def _(sp):
        for dst, src in loads:
            sp.dma_start(dst, src, allow_slow_non_contiguous=True).then_inc(loaded.sem, 16)
        sp.wait_ge(const_made.sem, CONSTS)
        rows = slot_x.rearrange("(n p r) d -> n p (r d)", p=126, r=ZERO_ROWS)
        for n in range(rows.shape[0]):
            sp.dma_start(rows[n], zero_t[:, :]).then_inc(cleared.sem, 16)
        with sp.Fori(0, ROUNDS) as i:
            hold_apart(sp, win_psum, "A", i, 0)
            for b in range(2):
                for half in range(2):
                    src = bass.AP(T["x"].tensor, (i * 2 + b) * (FRAMES * CH) + half * TOK * CH,
                                  [[CH, TOK], [1, WIN]])
                    sp.dma_start(xw[:, 2 * b + half, :], src).then_inc(win_in.sem, 16)

        sp.wait_ge(scattered.sem, scattered.value("C", 0, 0))
        sp.wait_ge(round_done.sem, round_done.value("C", 0, 0))
        with sp.Fori(0, C_ROUNDS) as i:
            for s in range(N):
                e = i * N + s
                hold_apart(sp, ed_psum[s], "C", i, 0)
                sp.dma_start(xe[s][:, :, :], bass.AP(slot_x.tensor, e * (CAP * D), [[D, TOK], [TOK * D, 2], [1, D]])).then_inc(ew_in[s].sem, 16)
                sp.dma_start(we1[s][:, :], bass.AP(T["L0_ffn_w1"].tensor, e * (D * F0), [[F0, P], [1, F0]])).then_inc(ew_in[s].sem, 16)
                sp.dma_start(we2[s][:, :, :], bass.AP(T["L0_ffn_w2"].tensor, e * (D * F0), [[D, P], [P * D, NC_F], [1, D]])).then_inc(ew_in[s].sem, 16)
                sp.dma_start(be2[s][:, :], bass.AP(T["L0_ffn_b2"].tensor, e * D, [[D, 1], [1, D]])).then_inc(ew_in[s].sem, 16)

        for dst, src in expert_loads:
            sp.dma_start(dst, src, allow_slow_non_contiguous=True).then_inc(loaded_e.sem, 16)

        with sp.Fori(0, ROUNDS) as i:
            hold_apart(sp, me_acc, "D", i, E1)
            sp.dma_start(bass.AP(out.tensor, i * (PAIR * D), [[D, TOK], [TOK * D, TILES], [1, D]]),
                         acc[:, :, :]).then_inc(stored.sem, 16)
        sp.wait_ge(stored.sem, 16 * ROUNDS)

    @block.gpsimd
    def _(pool):
        g = nc.gpsimd
        g.memset(ident[:, :], 0.0).then_inc(const_made.sem, 1)
        g.memset(before[:, :], 1.0).then_inc(const_made.sem, 1)
        g.memset(causal[:, :], 0.0).then_inc(const_made.sem, 1)
        pool.wait_ge(const_made.sem, 3)
        g.affine_select(out=ident[:, :], in_=ident[:, :], compare_op=ALU.not_equal, fill=1.0, base=0,
                        pattern=[[-1, P]], channel_multiplier=1).then_inc(const_made.sem, 1)
        g.affine_select(out=before[:, :], in_=before[:, :], compare_op=ALU.is_gt, fill=0.0, base=0,
                        pattern=[[1, P]], channel_multiplier=-1).then_inc(const_made.sem, 1)
        g.affine_select(out=causal[:, :], in_=causal[:, :], compare_op=ALU.is_ge, fill=MASKED, base=0,
                        pattern=[[-1, TOK]], channel_multiplier=1).then_inc(const_made.sem, 1)
        g.memset(ones[:, :], 1.0).then_inc(const_made.sem, 1)
        g.memset(frac[:, :], 1.0 / MLP).then_inc(const_made.sem, 1)
        g.memset(eps_t[:, :], EPS).then_inc(const_made.sem, 1)
        g.memset(mhalf[:, :], -0.5).then_inc(const_made.sem, 1)
        g.memset(zero_t[:, :], 0.0).then_inc(const_made.sem, 1)
        g.memset(carry[:, :], 0.0).then_inc(const_made.sem, 1)
        g.memset(slots_all[:, ROUNDS * TILES * TOP:], 0).then_inc(const_made.sem, 1)
        g.iota(iota_i[:, :], pattern=[[1, E0]], base=0, channel_multiplier=0).then_inc(const_made.sem, 1)
        for w in (wq0, wk0, wq1, wk1):
            g.memset(w[:, :, :], 0.0).then_inc(const_made.sem, 1)
        g.memset(v17[:, :, :, VD0:VD0 + 1], 1.0).then_inc(const_made.sem, 1)

        pool.wait_ge(bn_link.sem, 1)
        g.tensor_tensor(bn_e[:, :], bn_mv[:, 1:2], eps_t[:, 0:1], ALU.add).then_inc(bn_pool.sem, 1)
        pool.wait_ge(bn_pool.sem, 1)
        g.tensor_tensor(bn_r[:, :], bn_e[:, :], mhalf[:, 0:1], ALU.pow).then_inc(bn_pool.sem, 1)

        def rstd(phase, i, k, n, src, e_sig, mid, r_sig, dst, given):
            hold_apart(pool, given, phase, i, k + 1)
            g.tensor_tensor(mid, src, eps_t[0:TOK, 0:n], ALU.add).then_inc(e_sig.sem, 1)
            hold_apart(pool, e_sig, phase, i, k + 1)
            g.tensor_tensor(dst, mid, mhalf[0:TOK, 0:n], ALU.pow).then_inc(r_sig.sem, 1)

        def norm(phase, i, k):
            rstd(phase, i, k, TILES, ln_mv[:, :, 1], ln_eps, ln_e[:, :], ln_rstd, ln_r[:, :], ln_aggr)

        def norm_again(phase, i, k, j):
            hold_apart(pool, ln_rstd, phase, i, k + 1)
            g.tensor_tensor(again_v[:, :], ln_mv[:, :, 1], ln_r[:, :], ALU.mult).then_inc(again_link.sem, 1)
            hold_apart(pool, again_link, phase, i, 3 * j + 1)
            g.tensor_tensor(again_w[:, :], again_v[:, :], ln_r[:, :], ALU.mult).then_inc(again_link.sem, 1)
            hold_apart(pool, again_link, phase, i, 3 * j + 2)
            g.tensor_tensor(again_e[:, :], again_w[:, :], eps_t[0:TOK, 0:TILES], ALU.add).then_inc(again_link.sem, 1)
            hold_apart(pool, again_link, phase, i, 3 * j + 3)
            g.tensor_tensor(again_r[:, :], again_e[:, :], mhalf[0:TOK, 0:TILES], ALU.pow).then_inc(again_rstd.sem, 1)

        def head_of_round(i):
            norm("B", i, 0)
            norm_again("B", i, 0, 0)

        def tail_of_round(i):
            rstd("B", i, 0, TILES, ln_mv[:, :, 1], tail_eps, ln_e[:, :], tail_rstd, ln_r[:, :], tail_aggr)
            pool.wait_ge(cleared.sem, 16 * CLEARS)
            hold_apart(pool, slots_ready, "B", i, 1)
            for t in range(TILES):
                for k in range(TOP):
                    c = t * TOP + k
                    g.indirect_dma_start(out=slot_x, out_offset=bass.IndirectOffsetOnAxis(ap=slot_u[:, c:c + 1], axis=0),
                                         in_=x2[:, t, :], in_offset=None, bounds_check=E0 * CAP - 1,
                                         oob_is_err=False).then_inc(scattered.sem, 16)

        def round_of_b(i, first, final):
            if not first:
                tail_of_round(i - 1)
            rstd("B", i, 0, TILES * V0, ms1[:, :], diff_e, ms2[:, :], diff_r, ms[:, :], diff_ms)
            norm("B", i, 1)
            norm("B", i, 2)
            rstd("B", i, 0, TILES, mm2[:, :], down_e, ln_e[:, :], down_r, ln_r[:, :], down_var)
            norm("B", i, 3)
            norm_again("B", i, 3, 1)
            if not final:
                head_of_round(i + 1)

        head_of_round(0)
        round_of_b(0, True, False)
        with pool.Fori(1, ROUNDS - 1) as i:
            round_of_b(i, False, False)
        round_of_b(ROUNDS - 1, False, True)
        tail_of_round(ROUNDS - 1)

        with pool.Fori(0, C_ROUNDS) as i:
            for s in range(N):
                p, q = s % 2, s // 2
                hold_apart(pool, ye_ready[p], "C", i, q + 1)
                g.dma_start(bass.AP(slot_y.tensor, (i * N + s) * (CAP * D), [[D, TOK], [TOK * D, 2], [1, D]]),
                            ye[p][:, :, :]).then_inc(ye_out[p].sem, 16)
        for p in range(2):
            pool.wait_ge(ye_out[p].sem, 16 * E0 // 2)

        def gather_rows():
            for c in range(TILES * TOP):
                g.indirect_dma_start(out=gy[:, c, :], out_offset=None, in_=slot_y,
                                     in_offset=bass.IndirectOffsetOnAxis(ap=slot_c[:, c:c + 1], axis=0),
                                     bounds_check=E0 * CAP - 1, oob_is_err=False).then_inc(gathered.sem, 16)

        def gather_next(i):
            hold_apart(pool, idx_ready, "D", i, 1)
            hold_apart(pool, gy_used, "D", i, 1)
            gather_rows()

        def experts_round(i, final):
            norm("D", i, 1)

            def scale(e):
                s = e % 2
                rstd("D", i, e, TILES, e_mv[s][:, :, 1], me_e, e_e[:, :], me_r, e_r[:, :], me_var)
                hold_apart(pool, me_r, "D", i, e + 1)
                g.tensor_tensor(e_s[s][:, :], e_r[:, :], comb[:, :, e], ALU.mult).then_inc(me_scale.sem, 1)

            scale(0)
            for e in range(E1):
                if e + 1 < E1:
                    scale(e + 1)
                hold_apart(pool, me_g, "D", i, e + 1)
                g.tensor_tensor(acc[:, :, :], acc[:, :, :], nrm[e % 2][:, :, :], ALU.add).then_inc(me_acc.sem, 1)
                hold_apart(pool, me_acc, "D", i, e + 1)
                if e == NEXT_NORM - 1 and not final:
                    norm("D", i + 1, 0)
            if not final:
                gather_next(i + 1)

        pool.wait_ge(idx_ready.sem, 1)
        gather_rows()
        norm("D", 0, 0)
        gather_next(0)
        with pool.Fori(0, ROUNDS - 1) as i:
            experts_round(i, False)
        experts_round(ROUNDS - 1, True)
        pool.wait_ge(gathered.sem, 16 * TILES * TOP * (ROUNDS + 1))

    @block.scalar
    def _(act):
        a = nc.scalar
        act.wait_ge(prep_done.sem, STEP_VBB)
        a.activation(lam_e[:, :], lam_s[:, :], ACT.Exp).then_inc(prep_act.sem, 1)
        act.wait_ge(ready.sem, 1)

        with act.Fori(0, ROUNDS) as i:
            hold_apart(act, conv_psum, "A", i, 1)
            a.activation(y_all[:, bass.ds(i * PAIR, PAIR)], psG[:, 0:PAIR], ACT.Relu,
                         bias=colv["L0_tok_b"][:, :]).then_inc(y_ready.sem, 1)

        def feature_major(phase, i, k, weight, bias, turned_=fm_psum, ready_=fm_ready, dst=xT):
            hold(act, turned_, phase, i, k + 1)
            more = {}
            if weight is not None:
                more["scale"] = weight[:, :]
            if bias is not None:
                more["bias"] = bias[:, :]
            a.activation(dst[:, :], psG[:, 0:PAIR], ACT.Identity, **more).then_inc(ready_.sem, 1)

        def query_group(phase, i, k, dst, ps, scale, **more):
            hold(act, q_psum, phase, i, k + 1)
            a.activation(dst, ps[:, 0:PAIR], ACT.Identity, scale=scale, **more).then_inc(q_ready.sem, 1)

        def attention(phase, i, off, steps, causal_, beside=None):
            for m in range(steps + 1):
                if m < steps:
                    hold(act, maxed, phase, i, off + m + 1)
                    if m >= 2:
                        hold(act, turned, phase, i, off + m - 1)
                    for t in range(2):
                        keys = TOK if causal_ and t == 0 else SEQ
                        last = a.activation(prob[m % 2][:, t, 0:keys], psS[m % s_ring(phase)][0:TOK, t * 256:t * 256 + keys],
                                            ACT.Exp, bias=nmax[:, m % 4, t:t + 1])
                    last.then_inc(probs.sem, 1)
                if m >= 1 and (m - 1) % 2 == 1:
                    take(act, phase, i, off, m - 1, causal_)
                if beside is not None:
                    beside(m)

        def take_copy(eng, dst, src):
            return nc.scalar.copy(dst, src) if eng is act else nc.vector.tensor_copy(dst, src)

        def take(eng, phase, i, off, m, causal_):
            take_turned(eng, take_copy, phase, i, off, m, causal_)

        act.wait_ge(bn_ready.sem, 1)

        def head_of_round(i, m):
            if m == 0:
                a.activation(hT[:, :], y_all[:, bass.ds(i * PAIR, PAIR)], ACT.Identity,
                             bias=bn_c[:, :], scale=bn_s[:, :]).then_inc(hT_ready.sem, 1)
            if m == HEAD_FM + 2:
                feature_major("B", i, 0, colv["L0_attn_n1_w"], colv["L0_attn_n1_b"])
            if HEAD_Q < m <= HEAD_Q + 4:
                group = m - HEAD_Q - 1
                query_group("B", i, group, qT[:, group, :], psG, HD0 ** -0.5)

        def tail_of_round(i, m):
            if m == 2:
                feature_major("B", i, 0, None, None, tail_fm_psum, tail_fm_ready)
            if m == TAIL_X2 + 3:
                feature_major("B", i, 1, None, None, tail_fm_psum, tail_fm_ready)
            if m == TAIL_TOP + 2:
                hold(act, top_diff, "B", i, 1)
                a.activation(ex[:, :], dlt[:, :], ACT.Exp).then_inc(top_exp.sem, 1)

        def round_of_b(i, first, final):
            attention("B", i, 0, 2 * H0, False, None if first else lambda m: tail_of_round(i - 1, m))
            feature_major("B", i, 1, colv["sub_w8"], None)
            feature_major("B", i, 2, colv["L0_attn_mln1_w"], colv["L0_attn_mln1_b"])
            for c in range(NC_F):
                hold(act, up_psum, "B", i, c + 1)
                a.activation(big[:, c, :], psS[c][:, 0:PAIR], ACT.Gelu,
                             bias=colc["L0_attn_mb1"][:, c:c + 1]).then_inc(up_act.sem, 1)
            feature_major("B", i, 3, colv["L0_ffn_ln1_g"], colv["L0_ffn_ln1_b"])
            for group in range(2):
                query_group("B", i, 4 + group, q1[:, group, :], psS[group], HD1 ** -0.5)
            attention("B", i, 2 * H0, 2 * H1, False, None if final else lambda m: head_of_round(i + 1, m))

        for m in range(2 * H1 + 1):
            head_of_round(0, m)
        round_of_b(0, True, False)
        with act.Fori(1, ROUNDS - 1) as i:
            round_of_b(i, False, False)
        round_of_b(ROUNDS - 1, False, True)
        for m in range(2 * H0 + 1):
            tail_of_round(ROUNDS - 1, m)

        with act.Fori(0, C_ROUNDS) as i:
            for s in range(N):
                p, q = s % 2, s // 2
                if q:
                    hold(act, ed_psum[s - 2], "C", i, 1)
                else:
                    hold(act, ed_psum[s + N - 2], "C", i, 0)
                for half in range(2):
                    hold_apart(act, eu_psum[p], "C", i, 2 * q + half + 1)
                    for c in (2 * half, 2 * half + 1):
                        last = a.activation(he[p][:, c, :], psS[2 * p + half][:, (c % 2) * 256:(c % 2) * 256 + CAP], ACT.Gelu_apprx_tanh,
                                            bias=b1t[:, c, bass.ds(i * N + s, 1)])
                    last.then_inc(eu_act[p].sem, 1)

        def next_queries(i, e):
            if e == NEXT_NORM + 4:
                feature_major("D", i, 0, None, None, dst=hT)
            if NEXT_Q + 2 <= e < NEXT_Q + 6:
                group = e - NEXT_Q - 2
                query_group("D", i, group, qT[:, group, :], psG, 1.0, bias=qb2[:, group:group + 1])

        def round_of_d(i, final):
            def turned_heads(m):
                if CAT < m <= CAT + 2 * 4 and (m - CAT) % 2 == 0:
                    c = (m - CAT) // 2 - 1
                    hold(act, cat_psum, "D", i, c + 1)
                    a.copy(cat_b[:, c, 0:2 * TOK], psS[3][:, 0:2 * TOK]).then_inc(cat_T.sem, 1)

            attention("D", i, 0, 2 * H2, True, turned_heads)
            for c in range(4):
                hold(act, cat_psum, "D", i, 4 + c + 1)
                a.copy(cat_b[:, c, 2 * TOK:PAIR], psS[c][:, 0:2 * TOK]).then_inc(cat_T.sem, 1)
            feature_major("D", i, 1, None, None)
            hold(act, top_diff, "D", i, 1)
            a.activation(ex[:, :], dlt[:, :], ACT.Exp).then_inc(top_exp.sem, 1)
            for e in range(E1):
                s = e % 2
                if not final:
                    next_queries(i + 1, e)
                for c in range(2):
                    hold(act, mu_psum, "D", i, 2 * e + c + 1)
                    if e >= 2 and c == 0:
                        hold(act, md_psum, "D", i, e - 1)
                    a.activation(hm[s][:, c, :], psS[2 * s + c][:, 0:PAIR], ACT.Gelu,
                                 bias=b1e[:, c, e:e + 1]).then_inc(mu_act.sem, 1)

        for e in range(E1):
            next_queries(0, e)
        with act.Fori(0, ROUNDS - 1) as i:
            round_of_d(i, False)
        round_of_d(ROUNDS - 1, True)

    @block.vector
    def _(dve):
        v = nc.vector
        count = [0]

        def step(ins):
            count[0] += 1
            ins.then_inc(dve_link.sem, 1)
            dve.wait_ge(dve_link.sem, count[0])

        dve.wait_ge(const_made.sem, CONSTS)
        dve.wait_ge(loaded.sem, 16 * len(loads))
        v.tensor_copy(iota_f[:, :], iota_i[:, :])
        v.tensor_reduce(head_rows[:, :], ident[:, :].rearrange("p (j r) -> p j r", j=4), AX.X, ALU.add)
        v.tensor_copy(ident_h[:, :], ident[:, :])
        v.memset(ones_h[:, :], 1.0)
        v.tensor_copy(causal_h[:, :], causal[:, :])
        v.memset(w2m[:, :, D:D + 1], 1.0 / MLP)
        v.tensor_scalar(colv["sub_w8"][:, :], colv["sub_w"][:, :], 1.0 - LAMBDA_INIT, None, ALU.mult)
        for w, src in ((wq1, nat_fq), (wk1, nat_fk)):
            v.tensor_copy(w[:, :, :].rearrange("p g (j s) -> p (g j) s", s=32)[:, :, 0:HD1], heads(src[:, :], H1, HD1))
        for j, (x, y) in enumerate((("lq1", "lk1"), ("lq2", "lk2"))):
            step(v.tensor_tensor(lam_t[:, j, :], rowb["L0_attn_" + x][:, :], rowb["L0_attn_" + y][:, :], ALU.mult))
        v.tensor_reduce(lam_s[:, :], lam_t[:, :, :], AX.X, ALU.add)
        for k, (src, dst, hd) in enumerate(turns):
            dve.wait_ge(prep_psum.sem, k + 1)
            rows, cols = src.shape[1], src.shape[0]
            ps = psS[k % RING][0:rows, 0:cols]
            v.tensor_copy(dst, ps if hd is None else heads(ps, cols // hd, hd)).then_inc(prep_done.sem, 1)
        dve.wait_ge(prep_done.sem, N_TURNS)
        for c in range(NC_F):
            last = v.tensor_scalar(w2w[:, c, :], w2raw[:, c, :], colc["L0_attn_mln2_w"][:, c:c + 1], None, ALU.mult)
        last.then_inc(prep_pool.sem, 1)
        dve.wait_ge(prep_psum.sem, STEP_MEAN)
        dve.wait_ge(prep_pool.sem, 1)
        v.tensor_tensor(w2m[:, :, 0:D], w2w[:, :, :], bc(psS[0][:, 0:D], 1, [P, NC_F, D]), ALU.subtract).then_inc(prep_done.sem, 1)
        dve.wait_ge(prep_psum.sem, STEP_B2)
        v.tensor_tensor(b2m_row[:, :], psS[1][0:1, 0:D], mb2_row[:, :], ALU.add).then_inc(prep_done.sem, 1)
        dve.wait_ge(prep_psum.sem, STEP_B2B)
        v.tensor_copy(b2m[:, :], psS[2][0:TOK, 0:D]).then_inc(prep_done.sem, 1)
        for n in range(H2):
            dve.wait_ge(prep_psum.sem, STEP_QKV + n)
            for x, w in enumerate((wq2, wk2, wv2)):
                last = v.tensor_copy(w[:, n * HD2:(n + 1) * HD2], psS[n % RING][:, x * HD2:(x + 1) * HD2])
            last.then_inc(prep_done.sem, 1)
        for k, dst in ((STEP_QB, qb2), (STEP_KB, kb2)):
            dve.wait_ge(prep_psum.sem, k + 0)
            v.tensor_copy(dst[:, :], psT[0 if dst is qb2 else 1][:, 0:4]).then_inc(prep_done.sem, 1)
        dve.wait_ge(prep_psum.sem, STEP_VB)
        v.tensor_copy(vb_row[:, :], psO[0:1, :]).then_inc(prep_done.sem, 1)
        dve.wait_ge(prep_psum.sem, STEP_VBB)
        v.tensor_copy(vb2[:, :], psG[0:TOK, :]).then_inc(prep_done.sem, 1)
        dve.wait_ge(prep_act.sem, 1)
        step(v.tensor_tensor(lam_s[:, 0:1], lam_e[:, 1:2], lam_e[:, 0:1], ALU.subtract))
        v.tensor_scalar(neg_lam[:, :], lam_s[:, 0:1], -LAMBDA_INIT, None, ALU.add).then_inc(ready.sem, 1)

        with dve.Fori(0, ROUNDS) as i:
            for c in range(3):
                rows = P if c < 2 else WIN - 2 * P
                hold(dve, win_psum, "A", i, c + 1)
                if c == 0:
                    hold(dve, conv_psum, "A", i, 0)
                v.tensor_copy(big[0:rows, c, :], psS[c][0:rows, 0:PAIR]).then_inc(win_T.sem, 1)
            hold_apart(dve, y_ready, "A", i, 1)
            v.bn_stats(y_stats[:, bass.ds(i * 6, 6)], y_all[:, bass.ds(i * PAIR, PAIR)]).then_inc(y_counted.sem, 1)
        dve.wait_ge(y_counted.sem, ROUNDS)
        v.bn_aggr(bn_mv[:, :], y_stats[:, :]).then_inc(bn_link.sem, 1)
        dve.wait_ge(bn_pool.sem, 2)
        v.tensor_tensor(bn_s[:, :], bn_r[:, :], colv["L0_tok_gamma"][:, :], ALU.mult).then_inc(bn_link.sem, 1)
        dve.wait_ge(bn_link.sem, 2)
        v.tensor_tensor(bn_m[:, :], bn_mv[:, 0:1], bn_s[:, :], ALU.mult).then_inc(bn_link.sem, 1)
        dve.wait_ge(bn_link.sem, 3)
        v.tensor_tensor(bn_c[:, :], colv["L0_tok_beta"][:, :], bn_m[:, :], ALU.subtract).then_inc(bn_ready.sem, 1)

        done, tail_done = [0], [0]

        def link(phase, i, ins):
            done[0] += 1
            ins.then_inc(chain.sem, 1)
            hold_apart(dve, chain, phase, i, done[0])

        def tail_link(phase, i, ins):
            tail_done[0] += 1
            ins.then_inc(tail_chain.sem, 1)
            hold_apart(dve, tail_chain, phase, i, tail_done[0])

        def chain_ends(phase, done, chain):
            assert done[0] == chain.growth[phase], (phase, done[0])
            done[0] = 0

        def norm_stats(phase, i, k, src, counted=ln_stats, given=ln_aggr):
            for t in range(TILES):
                last = v.bn_stats(ln_st[:, t, :], src[t])
            last.then_inc(counted.sem, 1)
            hold_apart(dve, counted, phase, i, k + 1)
            for t in range(TILES):
                last = v.bn_aggr(ln_mv[:, t, :], ln_st[:, t, :])
            last.then_inc(given.sem, 1)

        def norm_apply(phase, i, k, src, dst, root=ln_rstd, out_=ln_out):
            hold(dve, root, phase, i, k + 1)
            for t in range(TILES):
                last = v.tensor_scalar(dst[:, t, :], src[t], ln_mv[:, t, 0:1], ln_r[:, t:t + 1], ALU.subtract, ALU.mult)
            last.then_inc(out_.sem, 1)
            hold(dve, out_, phase, i, k + 1)

        def norm(phase, i, k, src, dst):
            norm_stats(phase, i, k, src)
            norm_apply(phase, i, k, src, dst)

        def norm_again(phase, i, j, src, dst):
            hold_apart(dve, again_rstd, phase, i, j + 1)
            v.tensor_tensor(dst[:, :, :], src[:, :, :], bc(again_r[:, :], 2, [TOK, TILES, D]), ALU.mult).then_inc(again_out.sem, 1)

        def tiles(x):
            return [x[:, t, :] for t in range(TILES)]

        def key_group(phase, i, k, dst, ps, bias):
            hold(dve, k_psum, phase, i, k + 1)
            src = ps[:, 0:PAIR]
            ins = v.tensor_copy(dst, src) if bias is None else v.tensor_scalar(dst, src, bias, None, ALU.add)
            ins.then_inc(k_ready.sem, 1)

        def mask(phase, i, off, H, kT, m):
            b, n = m // H, m % H
            if m >= 4:
                hold(dve, scored, phase, i, off + m - 3)
            v.tensor_scalar(k_head[m % 4][:, :], kT[:, n // 4, b * SEQ:(b + 1) * SEQ], head_rows[:, n % 4:n % 4 + 1], None,
                            ALU.mult).then_inc(k_masked.sem, 1)

        def first_masks(phase, i, off, H, kT, k_ready_n):
            hold(dve, k_ready, phase, i, k_ready_n)
            for m in range(4):
                mask(phase, i, off, H, kT, m)

        def attention(phase, i, off, H, vd, kT, o, causal_, beside=None):
            steps = 2 * H
            group0 = off // 4

            def maximum(m):
                hold(dve, scored, phase, i, off + m + 1)
                s = psS[m % s_ring(phase)]
                if causal_:
                    v.tensor_reduce(nmax[:, m % 4, 0:1], s[0:TOK, 0:TOK], AX.X, ALU.max, negate=True)
                    v.tensor_reduce(nmax[:, m % 4, 1:2], s[0:TOK, 256:256 + SEQ], AX.X, ALU.max, negate=True).then_inc(maxed.sem, 1)
                else:
                    v.tensor_reduce(nmax[:, m % 4, :], s[0:TOK, :].rearrange("p (t k) -> p t k", t=2)[:, :, 0:SEQ],
                                    AX.X, ALU.max, negate=True).then_inc(maxed.sem, 1)

            def divide(m):
                gr = m // 4
                hold(dve, mixed, phase, i, off + m + 1)
                banks = pv_banks(phase)
                ps = banks[gr % len(banks)][0:TOK, 0:8 * (vd + 1)].rearrange("p (n t d) -> p n t d", n=4, t=2)
                rd = rden[:, gr % 2, :].rearrange("p (n t) -> p n t", n=4)
                v.reciprocal(rd, ps[:, :, :, vd]).then_inc(recip.sem, 1)
                hold(dve, recip, phase, i, group0 + gr + 1)
                b, n0 = m // H, m % H - 3
                dst = o[:, 2 * b:2 * b + 2, n0 * vd:(n0 + 4) * vd].rearrange("p t (n d) -> p n t d", n=4)
                v.tensor_tensor(dst, ps[:, :, :, 0:vd], bc(rd, 3, [TOK, 4, 2, vd]), ALU.mult).then_inc(normed.sem, 1)

            maximum(0)
            maximum(1)
            for m in range(steps):
                if m + 4 < steps:
                    mask(phase, i, off, H, kT, m + 4)
                if m + 2 < steps:
                    maximum(m + 2)
                if m % 2 == 0:
                    take_turned(dve, lambda eng, dst, src: v.tensor_copy(dst, src), phase, i, off, m, causal_)
                if m >= 1 and (m - 1) % 4 == 3:
                    divide(m - 1)
                if beside is not None:
                    beside(m)
            divide(steps - 1)

        def head_of_round(i, m):
            if m == 2:
                hold(dve, h_psum, "B", i, 1)
                v.tensor_copy(h[:, :, :], psG[0:TOK, :].rearrange("p (t d) -> p t d", t=TILES)).then_inc(h_ready.sem, 1)
                hold_apart(dve, h_ready, "B", i, 1)
                norm_stats("B", i, 0, tiles(h))
            if m == 4:
                norm_apply("B", i, 0, tiles(h), u)
            if m == HEAD_FM - 1:
                norm_again("B", i, 0, u, n_)
            if HEAD_Q < m <= HEAD_Q + 4:
                group = m - HEAD_Q - 1
                key_group("B", i, group, kT[:, group, :], psS[3], None)
            if m == HEAD_V + 1:
                hold(dve, v_psum, "B", i, 1)
                v.tensor_copy(v17[:, :, :, 0:VD0], psG[0:TOK, :].rearrange("p (t n d) -> p t n d", t=TILES, d=VD0)).then_inc(v_ready.sem, 1)

        row = lambda n: bc(rowb[n][:, :], 1, [TOK, TILES, D])
        pairs = [TOK, TILES * TOP, E0]
        ix8 = ixf[:, :, :].rearrange("p t k -> p (t k)")

        def tail_of_round(i, m):
            if m == 0:
                tail_done[0] = 0
            if m == 4:
                hold(dve, tail_proj, "B", i, 1)
                tail_link("B", i, v.tensor_tensor(um_[:, :, :], um_[:, :, :], psG[0:TOK, :].rearrange("p (t d) -> p t d", t=TILES), ALU.add))
                norm_stats("B", i, 0, tiles(um_), tail_stats, tail_aggr)
            if m == 6:
                norm_apply("B", i, 0, tiles(um_), n_, tail_rstd, tail_out)
            if m == 7:
                tail_link("B", i, v.tensor_tensor(n_[:, :, :], n_[:, :, :], row("L0_ffn_ln2_g"), ALU.mult))
            if m == TAIL_X2:
                hold(dve, scattered, "B", i, 0)
                v.tensor_tensor(x2[:, :, :], n_[:, :, :], row("L0_ffn_ln2_b"), ALU.add).then_inc(x2_ready.sem, 1)
                hold_apart(dve, x2_ready, "B", i, 1)
            if m == TAIL_X2 + 1:
                v.tensor_tensor(hx_all[:, bass.ds(i * (TILES * D), TILES * D)], hm_[:, :, :].rearrange("p t d -> p (t d)"),
                                um_[:, :, :].rearrange("p t d -> p (t d)"), ALU.add)
            if m == TAIL_TOP - 1:
                hold(dve, route_psum, "B", i, 1)
                tail_link("B", i, v.tensor_copy(lg[:, :, :], psG[0:TOK, 0:TILES * E0].rearrange("p (t e) -> p t e", t=TILES)))
                for t in range(TILES):
                    last = v.max(mx[:, t, :], lg[:, t, :])
                tail_link("B", i, last)
            if m == TAIL_TOP:
                v.tensor_tensor(dlt[:, :], mx[:, :, 1], mx[:, :, 0], ALU.subtract).then_inc(top_diff.sem, 1)
                for t in range(TILES):
                    last = v.max_index(ix[:, t, :], mx[:, t, :], lg[:, t, :])
                tail_link("B", i, last)
                tail_link("B", i, v.tensor_copy(ixf[:, :, :], ix[:, :, 0:TOP]))
            if m == TAIL_TOP + 1:
                tail_link("B", i, v.tensor_tensor(hot[:, :, :, :].rearrange("p t k e -> p (t k) e"), bc(iota_f[0:TOK, :], 1, pairs), bc(ix8, 2, pairs), ALU.is_equal))
                v.tensor_tensor(hots[:, :, :], hot[:, :, 0, :], hot[:, :, 1, :], ALU.add).then_inc(hot_ready.sem, 1)
            if m == TAIL_RANK:
                gates(dve, v, "B", i, tail_link)
            if m == TAIL_RANK + 1:
                hold(dve, rank_psum, "B", i, 1)
                tail_link("B", i, v.tensor_tensor(pos_e[:, :, :], psG[0:TOK, 0:TILES * E0].rearrange("p (t e) -> p t e", t=TILES),
                                                  bc(carry[0:TOK, :], 1, [TOK, TILES, E0]), ALU.add))
                v.tensor_tensor(carry[:, :], carry[:, :], psG[0:TOK, TILES * E0:(TILES + 1) * E0], ALU.add)
            if m == TAIL_RANK + 2:
                tail_link("B", i, v.tensor_tensor(pos_h[:, :, :, :], hot[:, :, :, :], bc(pos_e[:, :, :], 2, [TOK, TILES, TOP, E0]), ALU.mult))
            if m == TAIL_RANK + 3:
                tail_link("B", i, v.tensor_reduce(pos[:, :], pos_h[:, :, :, :].rearrange("p t k e -> p (t k) e"), AX.X, ALU.add))
            if m == TAIL_RANK + 4:
                v.tensor_scalar(slot_l[:, :], ix8, float(CAP), float(CAP - 1), ALU.mult, ALU.add)
                v.tensor_scalar(keep[:, :], pos[:, :], float(CAP), None, ALU.is_lt)
                tail_link("B", i, v.scalar_tensor_tensor(slot_f[:, :], ix8, float(CAP), pos[:, :], ALU.mult, ALU.add))
                tail_link("B", i, v.tensor_scalar(drop_f[:, :], keep[:, :], -float(DROPPED), float(DROPPED), ALU.mult, ALU.add))
            if m == TAIL_RANK + 5:
                tail_link("B", i, v.tensor_tensor(slot_s[:, :], slot_f[:, :], drop_f[:, :], ALU.add))
                v.tensor_copy(slot_u[:, :], slot_s[:, :]).then_inc(slots_ready.sem, 1)
                tail_link("B", i, v.tensor_tensor(slot_l[:, :], slot_f[:, :], slot_l[:, :], ALU.min))
            if m == TAIL_RANK + 6:
                v.tensor_copy(slots_all[:, bass.ds(i * (TILES * TOP), TILES * TOP)], slot_l[:, :])
                v.tensor_tensor(gates_all[:, bass.ds(i * (TILES * TOP), TILES * TOP)], gate[:, :, :].rearrange("p t k -> p (t k)"),
                                keep[:, :], ALU.mult).then_inc(round_done.sem, 1)
                chain_ends("B", tail_done, tail_chain)

        def round_of_b(i, first, final):
            first_masks("B", i, 0, H0, kT, 4)
            attention("B", i, 0, H0, VD0, kT, o_all, False, None if first else lambda m: tail_of_round(i - 1, m))
            hold(dve, normed, "B", i, 2 * H0 // 4)
            for t in range(TILES):
                pair = o_all[:, t, 0:H0 * VD0].rearrange("p (n two d) -> p n two d", two=2, d=VD0)
                last = v.scalar_tensor_tensor(oc[:, t * V0:(t + 1) * V0, :], pair[:, :, 1, :], neg_lam[:, :], pair[:, :, 0, :], ALU.mult, ALU.add)
            link("B", i, last)
            link("B", i, v.tensor_tensor(ocs[:, :, :], oc[:, :, :], oc[:, :, :], ALU.mult))
            link("B", i, v.tensor_reduce(ms[:, :], ocs[:, :, :], AX.X, ALU.add))
            v.tensor_scalar(ms1[:, :], ms[:, :], 1.0 / VD0, None, ALU.mult).then_inc(diff_ms.sem, 1)
            hold(dve, diff_r, "B", i, 1)
            v.tensor_tensor(n_[:, :, :].rearrange("p t (n d) -> p (t n) d", d=VD0), oc[:, :, :], bc(ms[:, :], 2, [TOK, TILES * V0, VD0]),
                            ALU.mult).then_inc(diff_out.sem, 1)
            hold(dve, proj_psum, "B", i, 1)
            norm("B", i, 1, [psS[0][0:TOK, t * D:(t + 1) * D] for t in range(TILES)], n_)
            link("B", i, v.tensor_tensor(n_[:, :, :], n_[:, :, :], row("L0_attn_n2_w"), ALU.mult))
            link("B", i, v.tensor_tensor(n_[:, :, :], n_[:, :, :], row("L0_attn_n2_b"), ALU.add))
            link("B", i, v.tensor_tensor(h1[:, :, :], n_[:, :, :], u[:, :, :], ALU.add))
            norm("B", i, 2, tiles(h1), n_)
            link("B", i, v.tensor_tensor(h[:, :, :], h[:, :, :], h1[:, :, :], ALU.add))
            link("B", i, v.tensor_tensor(h[:, :, :], h[:, :, :], bc(b2m[:, :], 1, [TOK, TILES, D]), ALU.add))
            for c in range(NC_F):
                hold(dve, up_act, "B", i, c + 1)
                v.tensor_tensor(sq[:, c, :], big[:, c, :], big[:, c, :], ALU.mult).then_inc(up_sq.sem, 1)
            hold(dve, down_psum, "B", i, 1)
            for j in range(2):
                last = v.tensor_copy(mm[:, 2 * j:2 * j + 2, :], psT[j][0:TOK, 0:2 * (D + 2)].rearrange("p (t d) -> p t d", t=2)[:, :, D:D + 2])
            link("B", i, last)
            link("B", i, v.tensor_tensor(mm2[:, :], mm[:, :, 0], mm[:, :, 0], ALU.mult))
            v.tensor_tensor(mm2[:, :], mm[:, :, 1], mm2[:, :], ALU.subtract).then_inc(down_var.sem, 1)
            hold(dve, down_r, "B", i, 1)
            for t in range(TILES):
                at = (t % 2) * (D + 2)
                last = v.scalar_tensor_tensor(hm_[:, t, :], psT[t // 2][0:TOK, at:at + D], ln_r[:, t:t + 1], h[:, t, :], ALU.mult, ALU.add)
            link("B", i, last)
            chain_ends("B", done, chain)
            norm("B", i, 3, tiles(hm_), um_)
            norm_again("B", i, 1, um_, n_)
            for group in range(2):
                key_group("B", i, 4 + group, k1[:, group, :], psS[group], None)
            first_masks("B", i, 2 * H0, H1, k1, 6)
            hold(dve, v_psum, "B", i, 2)
            v.tensor_copy(v17m[:, :, :, 0:HD1], psG[0:TOK, :].rearrange("p (t n d) -> p t n d", t=TILES, d=HD1)).then_inc(v_ready.sem, 1)
            attention("B", i, 2 * H0, H1, HD1, k1, om, False, None if final else lambda m: head_of_round(i + 1, m))

        v.memset(v17m[:, :, :, HD1:HD1 + 1], 1.0)
        for m in range(2 * H1 + 1):
            head_of_round(0, m)
        round_of_b(0, True, False)
        with dve.Fori(1, ROUNDS - 1) as i:
            round_of_b(i, False, False)
        round_of_b(ROUNDS - 1, False, True)
        for m in range(2 * H0 + 1):
            tail_of_round(ROUNDS - 1, m)

        def rows_turned(i, s):
            p, q = s % 2, s // 2
            hold(dve, xe_psum[p], "C", i, q + 1)
            v.tensor_copy(xeT[p][:, :], (psG, psO)[p][:, 0:CAP]).then_inc(xe_T[p].sem, 1)

        def expert_steps(i, ahead):
            for s in range(N):
                if s + 2 < N or ahead:
                    rows_turned(i, s + 2)
                p, q = s % 2, s // 2
                hold(dve, ed_psum[s], "C", i, 1)
                hold(dve, ye_out[p], "C", i, 16 * q)
                v.tensor_copy(ye[p][:, :, :], psT[p][0:TOK, 0:2 * D].rearrange("p (t d) -> p t d", t=2)).then_inc(ye_ready[p].sem, 1)

        links = [0]

        def split_link(ins):
            links[0] += 1
            ins.then_inc(b2_link.sem, 1)
            dve.wait_ge(b2_link.sem, links[0])

        left, sum_ = b2_left
        for half in range(2):
            es = slice(half * E1 // 2, (half + 1) * E1 // 2)
            b, high = b2_rows[:, es, :], b2_split[:, es, :]
            split_link(v.tensor_copy(high, b))
            split_link(v.tensor_tensor(left, b, high, ALU.subtract))
            split_link(v.tensor_copy(b2_part[:, :, :], left))
            split_link(v.tensor_tensor(left, left, b2_part[:, :, :], ALU.subtract))
            split_link(v.tensor_scalar(left, left, ident[0:SPLIT, 2:3], None, ALU.mult))
            split_link(v.scalar_tensor_tensor(sum_, b2_part[:, :, :], ident[0:SPLIT, 1:2], left, ALU.mult, ALU.add))
            split_link(v.scalar_tensor_tensor(high, high, ident[0:SPLIT, 0:1], sum_, ALU.mult, ALU.add))

        rows_turned(0, 0)
        rows_turned(0, 1)
        with dve.Fori(0, C_ROUNDS - 1) as i:
            expert_steps(i, True)
        expert_steps(C_ROUNDS - 1, False)

        v.memset(v33[:, :, :, HD2:HD2 + 1], 1.0)
        v.tensor_copy(slot_c[:, :], slots_all[:, 0:TILES * TOP]).then_inc(idx_ready.sem, 1)

        def next_head(i, e):
            if e == 0:
                v.tensor_copy(gate_c[:, :], gates_all[:, bass.ds(i * (TILES * TOP), TILES * TOP)])
                v.tensor_copy(h[:, :, :].rearrange("p t d -> p (t d)"), hx_all[:, bass.ds(i * (TILES * D), TILES * D)]).then_inc(next_chain.sem, 1)
                hold_apart(dve, gathered, "D", i, 0)
                v.tensor_copy(slot_c[:, :], slots_all[:, bass.ds((i + 1) * (TILES * TOP), TILES * TOP)]).then_inc(idx_ready.sem, 1)
                hold_apart(dve, next_chain, "D", i, 1)
            if e in (0, 1):
                for t in range(TILES):
                    c = t * TOP + e
                    last = v.scalar_tensor_tensor(h[:, t, :], gy[:, c, :], gate_c[:, c:c + 1], h[:, t, :], ALU.mult, ALU.add)
                if e == 0:
                    last.then_inc(next_chain.sem, 1)
                    hold_apart(dve, next_chain, "D", i, 2)
                else:
                    last.then_inc(gy_used.sem, 1)
                    hold_apart(dve, gy_used, "D", i, 1)
            if e == NEXT_NORM - 1:
                norm_stats("D", i, 0, tiles(h))
            if e == NEXT_NORM:
                norm_apply("D", i, 0, tiles(h), u)

            if e == E1 - 2:
                first_masks("D", i, 0, H2, kT, 4)

        def next_keys(i, e):
            if NEXT_Q <= e < NEXT_Q + 4:
                group = e - NEXT_Q
                key_group("D", i, group, kT[:, group, :], psG, kb2[:, group:group + 1])
            if NEXT_Q + 4 <= e < NEXT_Q + 8:
                t = e - NEXT_Q - 4
                hold(dve, v_psum, "D", i, t + 1)
                v.tensor_tensor(v33[:, t, :, 0:HD2], psG[0:TOK, :].rearrange("p (n d) -> p n d", d=HD2),
                                vb2[:, :].rearrange("p (n d) -> p n d", d=HD2), ALU.add).then_inc(v_ready.sem, 1)

        def round_of_d(i, final):
            def beside_attention(m):
                if m == 1:
                    link("D", i, v.tensor_tensor(h[:, :, :], h[:, :, :], bc(rowb["L1_attn_bo"][:, :], 1, [TOK, TILES, D]), ALU.add))

            attention("D", i, 0, H2, HD2, kT, o_all, True, beside_attention)
            hold(dve, proj_psum, "D", i, 1)
            link("D", i, v.tensor_tensor(h[:, :, :], h[:, :, :], psG[0:TOK, :].rearrange("p (t d) -> p t d", t=TILES), ALU.add))
            norm("D", i, 1, tiles(h), u)
            hold(dve, gate_psum, "D", i, 1)
            link("D", i, v.tensor_tensor(s16[:, :, :], psG[0:TOK, 0:TILES * E1].rearrange("p (t e) -> p t e", t=TILES),
                                         bc(rowb["L1_ffn_gate_b"][:, :], 1, [TOK, TILES, E1]), ALU.add))
            for t in range(TILES):
                last = v.max(mx[:, t, :], s16[:, t, :])
            link("D", i, last)
            v.tensor_tensor(dlt[:, :], mx[:, :, 1], mx[:, :, 0], ALU.subtract).then_inc(top_diff.sem, 1)
            for t in range(TILES):
                last = v.max_index(ix[:, t, :], mx[:, t, :], s16[:, t, :])
            link("D", i, last)
            link("D", i, v.tensor_copy(ixf[:, :, :], ix[:, :, 0:TOP]))
            pairs = [TOK, TILES * TOP, E1]
            link("D", i, v.tensor_tensor(hot1[:, :, :, :].rearrange("p t k e -> p (t k) e"), bc(iota_f[0:TOK, 0:E1], 1, pairs),
                                         bc(ixf[:, :, :].rearrange("p t k -> p (t k)"), 2, pairs), ALU.is_equal))
            gates(dve, v, "D", i, link)
            link("D", i, v.tensor_tensor(comb2[:, :, :, :].rearrange("p t k e -> p (t k) e"), hot1[:, :, :, :].rearrange("p t k e -> p (t k) e"),
                                         bc(gate[:, :, :].rearrange("p t k -> p (t k)"), 2, pairs), ALU.mult))
            v.tensor_tensor(comb[:, :, :], comb2[:, :, 0, :], comb2[:, :, 1, :], ALU.add).then_inc(comb_ready.sem, 1)
            hold(dve, combT_psum, "D", i, 1)
            v.tensor_copy(combT[:, :], psG[0:E1, 0:PAIR]).then_inc(combT_ready.sem, 1)
            hold(dve, beta_psum, "D", i, 1)
            hold(dve, stored, "D", i, 0)
            v.tensor_tensor(acc[:, :, :], h[:, :, :], psG[0:TOK, :].rearrange("p (t d) -> p t d", t=TILES), ALU.add).then_inc(acc_ready.sem, 1)

            def stats(e):
                s = e % 2
                if e >= 2:
                    hold(dve, me_scale, "D", i, e - 1)
                hold(dve, md_psum, "D", i, e + 1)
                for t in range(TILES):
                    last = v.bn_stats(e_st[s][:, t, :], ps_down[e % 3][0:TOK, t * D:(t + 1) * D])
                last.then_inc(me_stats.sem, 1)
                hold_apart(dve, me_stats, "D", i, e + 1)
                for t in range(TILES):
                    last = v.bn_aggr(e_mv[s][:, t, :], e_st[s][:, t, :])
                last.then_inc(me_var.sem, 1)

            stats(0)
            for e in range(E1):
                s = e % 2
                if not final:
                    next_keys(i + 1, e + 1)
                if e + 1 < E1:
                    stats(e + 1)
                hold(dve, me_scale, "D", i, e + 1)
                hold(dve, me_acc, "D", i, max(e - 1, 0))
                for t in range(TILES):
                    last = v.tensor_scalar(nrm[s][:, t, :], ps_down[e % 3][0:TOK, t * D:(t + 1) * D], e_mv[s][:, t, 0:1], e_s[s][:, t:t + 1],
                                           ALU.subtract, ALU.mult)
                last.then_inc(me_norm.sem, 1)
                hold(dve, me_norm, "D", i, e + 1)
                v.tensor_tensor(nrm[s][:, :, :], nrm[s][:, :, :], bc(gamma_b[:, e, :], 1, [TOK, TILES, D]), ALU.mult).then_inc(me_g.sem, 1)
                if not final:
                    next_head(i + 1, e)
            chain_ends("D", done, chain)

        for e in range(E1):
            next_head(0, e)
            next_keys(0, e + 1)
        with dve.Fori(0, ROUNDS - 1) as i:
            round_of_d(i, False)
        round_of_d(ROUNDS - 1, True)

    @block.tensor
    def _(pe):
        mmul = nc.tensor.matmul
        pe.wait_ge(const_made.sem, CONSTS)
        pe.wait_ge(loaded.sem, 16 * len(loads))
        for k, (src, dst, hd) in enumerate(turns):
            rows, cols = src.shape[1], src.shape[0]
            if k >= RING:
                pe.wait_ge(prep_done.sem, k - RING + 1)
            nc.tensor.transpose(psS[k % RING][0:rows, 0:cols], src, ident[0:cols, 0:cols]).then_inc(prep_psum.sem, 1)
        pe.wait_ge(prep_done.sem, N_TURNS)
        pe.wait_ge(prep_pool.sem, 1)
        for c in range(NC_F):
            last = mmul(psS[0][:, 0:D], frac[:, :], w2w[:, c, :], start=c == 0, stop=c == NC_F - 1)
        last.then_inc(prep_psum.sem, 1)
        for c in range(NC_F):
            last = mmul(psS[1][0:1, 0:D], colc["L0_attn_mln2_b"][:, c:c + 1], w2raw[:, c, :], start=c == 0, stop=c == NC_F - 1)
        last.then_inc(prep_psum.sem, 1)
        pe.wait_ge(prep_done.sem, STEP_B2)
        mmul(psS[2][0:TOK, 0:D], ones[0:1, 0:TOK], b2m_row[:, :], start=True, stop=True).then_inc(prep_psum.sem, 1)
        for n in range(H2):
            pe.wait_ge(prep_done.sem, max(STEP_B2B, STEP_QKV + n - RING))
            for x in range(3):
                last = mmul(psS[n % RING][:, x * HD2:(x + 1) * HD2], wl[:, n, :], qkv1[:, x, n, :], start=True, stop=True)
            last.then_inc(prep_psum.sem, 1)
        for x, ps in ((0, psT[0]), (1, psT[1])):
            for n in range(H2):
                j, g = n % 4, n // 4
                last = mmul(ps[32 * j:32 * j + 32, g:g + 1], qkv1[:, x, n, :], blt[:, n:n + 1], start=True, stop=True)
            last.then_inc(prep_psum.sem, 1)
        for n in range(H2):
            last = mmul(psO[0:1, n * HD2:(n + 1) * HD2], blt[:, n:n + 1], qkv1[:, 2, n, :], start=True, stop=True)
        last.then_inc(prep_psum.sem, 1)
        pe.wait_ge(prep_done.sem, STEP_VB)
        mmul(psG[0:TOK, :], ones[0:1, 0:TOK], vb_row[:, :], start=True, stop=True).then_inc(prep_psum.sem, 1)
        pe.wait_ge(ready.sem, 1)

        with pe.Fori(0, ROUNDS) as i:
            hold(pe, win_in, "A", i, 16 * TILES)
            hold(pe, win_T, "A", i, 0)
            for c in range(3):
                cols = P if c < 2 else WIN - 2 * P
                for t in range(TILES):
                    last = nc.tensor.transpose(psS[c][0:cols, tile(t)], xw[:, t, c * P:c * P + cols], ident[0:TOK, 0:TOK])
                last.then_inc(win_psum.sem, 1)
            hold(pe, win_T, "A", i, 3)
            hold(pe, y_ready, "A", i, 0)
            for c in range(3):
                rows = P if c < 2 else WIN - 2 * P
                last = mmul(psG[:, 0:PAIR], w_tok[0:rows, c, :], big[0:rows, c, :], start=c == 0, stop=c == 2)
            last.then_inc(conv_psum.sem, 1)

        def turn_to_features(phase, i, src, turned_=fm_psum):
            for t in range(TILES):
                last = nc.tensor.transpose(psG[:, tile(t)], src[:, t, :], ident[0:TOK, 0:TOK])
            last.then_inc(turned_.sem, 1)

        def attention(phase, i, off, H, hd, vd, qT, v_of, causal_, heads_a_value, beside=None):
            steps = 2 * H
            ring = s_ring(phase)
            banks = pv_banks(phase)

            def scores(m):
                b, n = m // H, m % H
                g = n // 4
                hold(pe, k_masked, phase, i, off + m + 1)
                if m >= ring:
                    hold(pe, probs, phase, i, off + m - ring + 1)
                bank = psS[m % ring]
                for t in range(2):
                    keys = TOK if causal_ and t == 0 else SEQ
                    at = t * 256
                    last = mmul(bank[0:TOK, at:at + keys], qT[:, g, tile(2 * b + t)], k_head[m % 4][:, 0:keys],
                                start=True, stop=not causal_)
                    if causal_:
                        last = mmul(bank[0:TOK, at + t * TOK:at + (t + 1) * TOK], ident_h[0:TOK, 0:TOK], causal_h[:, :], start=False, stop=True)
                last.then_inc(scored.sem, 1)

            def turn(m):
                hold(pe, probs, phase, i, off + m + 1)
                if m >= 2:
                    hold(pe, taken[m % 2], phase, i, (off + m) // 2)
                for c in range(2):
                    for t in range(2):
                        if causal_ and t < c:
                            continue
                        last = nc.tensor.transpose(psT[m % 2][0:TOK, c * SEQ + t * TOK:c * SEQ + (t + 1) * TOK],
                                                   prob[m % 2][:, t, c * TOK:(c + 1) * TOK], ident[0:TOK, 0:TOK])
                last.then_inc(turned.sem, 1)

            def mix(m):
                b, n = m // H, m % H
                hold(pe, taken[m % 2], phase, i, (off + m) // 2 + 1)
                if m % 4 == 0 and m >= 4 * len(banks):
                    hold(pe, normed, phase, i, (off + m) // 4 - len(banks) + 1)
                for t in range(2):
                    last_c = 0 if causal_ and t == 0 else 1
                    at = ((n % 4) * 2 + t) * (vd + 1)
                    for c in range(last_c + 1):
                        last = mmul(banks[(m // 4) % len(banks)][0:TOK, at:at + vd + 1], probT[m % 2][:, c * SEQ + t * TOK:c * SEQ + (t + 1) * TOK],
                                    v_of(2 * b + c, n // heads_a_value), start=c == 0, stop=c == last_c)
                last.then_inc(mixed.sem, 1)

            for m in range(ring - 1):
                scores(m)
            for m in range(steps):
                if m + ring - 1 < steps:
                    scores(m + ring - 1)
                turn(m)
                if m:
                    mix(m - 1)
                if beside is not None:
                    beside(m)
            mix(steps - 1)

        def v_small(phase, i, k, w):
            for t in range(TILES):
                last = mmul(psG[0:TOK, t * D:(t + 1) * D], xT[:, tile(t)], w[:, :], start=True, stop=True)
            last.then_inc(v_psum.sem, 1)

        def out_projection(ps, w, made):
            for t in range(TILES):
                last = mmul(ps[0:TOK, t * D:(t + 1) * D], xT[:, tile(t)], w[:, :], start=True, stop=True)
            last.then_inc(made.sem, 1)

        def head_of_round(i, m):
            if m == 1:
                hold(pe, hT_ready, "B", i, 1)
                for t in range(TILES):
                    last = nc.tensor.transpose(psG[0:TOK, t * D:(t + 1) * D], hT[:, tile(t)], ident[:, :])
                last.then_inc(h_psum.sem, 1)
            if m == HEAD_FM:
                hold(pe, again_out, "B", i, 1)
                turn_to_features("B", i, n_)
            if HEAD_Q <= m < HEAD_Q + 4:
                group = m - HEAD_Q
                if group == 0:
                    hold(pe, fm_ready, "B", i, 1)
                hold(pe, q_ready, "B", i, group)
                mmul(psG[:, 0:PAIR], wq0[:, group, :], xT[:, :], start=True, stop=True).then_inc(q_psum.sem, 1)
                hold(pe, k_ready, "B", i, group)
                mmul(psS[3][:, 0:PAIR], wk0[:, group, :], xT[:, :], start=True, stop=True).then_inc(k_psum.sem, 1)
            if m == HEAD_V:
                hold(pe, q_ready, "B", i, 4)
                v_small("B", i, 1, wv0)

        def tail_of_round(i, m):
            if m == 0:
                hold(pe, normed, "B", i, HEADS_B // 4)
                turn_to_features("B", i, om, tail_fm_psum)
            if m == 3:
                hold(pe, tail_fm_ready, "B", i, 1)
                out_projection(psG, wo1, tail_proj)
            if m == TAIL_X2 + 1:
                hold(pe, x2_ready, "B", i, 1)
                turn_to_features("B", i, x2, tail_fm_psum)
            if m == TAIL_X2 + 4:
                hold(pe, tail_fm_ready, "B", i, 2)
                for t in range(TILES):
                    last = mmul(psG[0:TOK, t * E0:(t + 1) * E0], xT[:, tile(t)], wr[:, :], start=True, stop=True)
                last.then_inc(route_psum.sem, 1)
            if m == TAIL_RANK:
                hold(pe, hot_ready, "B", i, 1)
                for t in range(TILES):
                    for t2 in range(t + 1):
                        lhs = before if t2 == t else ones
                        mmul(psG[0:TOK, t * E0:(t + 1) * E0], lhs[0:TOK, 0:TOK], hots[:, t2, :], start=t2 == 0, stop=t2 == t)
                for t in range(TILES):
                    last = mmul(psG[0:TOK, TILES * E0:(TILES + 1) * E0], ones[0:TOK, 0:TOK], hots[:, t, :], start=t == 0, stop=t == TILES - 1)
                last.then_inc(rank_psum.sem, 1)

        def round_of_b(i, first, final):
            hold(pe, k_ready, "B", i, 4)
            hold(pe, v_ready, "B", i, 1)
            if not first:
                hold(pe, normed, "B", i - 1, HEADS_B // 4)
            attention("B", i, 0, H0, HD0, VD0, qT, lambda t, n: v17[:, t, n, :], False, H0 // V0,
                      None if first else lambda m: tail_of_round(i - 1, m))
            hold(pe, diff_out, "B", i, 1)
            turn_to_features("B", i, n_)
            hold(pe, fm_ready, "B", i, 2)
            out_projection(psS[0], wo0, proj_psum)
            hold(pe, ln_out, "B", i, 3)
            turn_to_features("B", i, n_)
            hold(pe, fm_ready, "B", i, 3)
            for c in range(NC_F):
                mmul(psS[c][:, 0:PAIR], w1m[:, c * P:(c + 1) * P], xT[:, :], start=True, stop=True).then_inc(up_psum.sem, 1)
            hold(pe, up_act, "B", i, NC_F)
            for t in range(TILES):
                at = (t % 2) * (D + 2)
                for c in range(NC_F):
                    mmul(psT[t // 2][0:TOK, at:at + D + 1], big[:, c, tile(t)], w2m[:, c, :], start=c == 0, stop=c == NC_F - 1)
                if t == 0:
                    hold(pe, up_sq, "B", i, NC_F)
                for c in range(NC_F):
                    last = mmul(psT[t // 2][0:TOK, at + D + 1:at + D + 2], sq[:, c, tile(t)], frac[:, 0:1], start=c == 0, stop=c == NC_F - 1)
            last.then_inc(down_psum.sem, 1)
            hold(pe, again_out, "B", i, 2)
            turn_to_features("B", i, n_)
            hold(pe, fm_ready, "B", i, 4)
            for group in range(2):
                mmul(psS[group][:, 0:PAIR], wq1[:, group, :], xT[:, :], start=True, stop=True).then_inc(q_psum.sem, 1)
            v_small("B", i, 2, wv1)
            for group in range(2):
                hold(pe, q_ready, "B", i, 4 + group + 1)
                mmul(psS[group][:, 0:PAIR], wk1[:, group, :], xT[:, :], start=True, stop=True).then_inc(k_psum.sem, 1)
            hold(pe, k_ready, "B", i, 6)
            hold(pe, v_ready, "B", i, 2)
            attention("B", i, 2 * H0, H1, HD1, HD1, q1, lambda t, n: v17m[:, t, n, :], False, 1,
                      None if final else lambda m: head_of_round(i + 1, m))

        for m in range(2 * H1 + 1):
            head_of_round(0, m)
        round_of_b(0, True, False)
        with pe.Fori(1, ROUNDS - 1) as i:
            round_of_b(i, False, False)
        round_of_b(ROUNDS - 1, False, True)
        for m in range(2 * H0 + 1):
            tail_of_round(ROUNDS - 1, m)

        pe.wait_ge(round_done.sem, round_done.value("C", 0, 0))

        def rows_to_features(i, s):
            p, q = s % 2, s // 2
            if s < N:
                hold(pe, ew_in[s], "C", i, 16 * 4)
            else:
                hold(pe, ew_in[s - N], "C", i, 2 * 16 * 4)
            hold(pe, xe_T[p], "C", i, q)
            for t in range(2):
                last = nc.tensor.transpose((psG, psO)[p][:, tile(t)], xe[s % N][:, t, :], ident[0:TOK, 0:TOK])
            last.then_inc(xe_psum[p].sem, 1)

        def expert_up(i, s):
            p, q = s % 2, s // 2
            hold(pe, xe_T[p], "C", i, q + 1)
            for half in range(2):
                hold(pe, eu_act[p], "C", i, 2 * q)
                for c in (2 * half, 2 * half + 1):
                    last = mmul(psS[2 * p + half][:, (c % 2) * 256:(c % 2) * 256 + CAP], we1[s % N][:, c * P:(c + 1) * P], xeT[p][:, :],
                                start=True, stop=True)
                last.then_inc(eu_psum[p].sem, 1)

        def expert_down(i, s):
            p, q = s % 2, s // 2
            hold(pe, eu_act[p], "C", i, 2 * q + 2)
            hold(pe, ye_ready[p], "C", i, q)
            for t in range(2):
                for c in range(NC_F):
                    mmul(psT[p][0:TOK, t * D:(t + 1) * D], he[p][:, c, tile(t)], we2[s][:, c, :], start=c == 0, stop=False)
                last = mmul(psT[p][0:TOK, t * D:(t + 1) * D], ones[0:1, 0:TOK], be2[s][:, :], start=False, stop=True)
            last.then_inc(ed_psum[s].sem, 1)

        def expert_round(i, ahead):
            for s in range(N):
                if s + 2 < N or ahead:
                    rows_to_features(i, s + 2)
                if s + 1 < N or ahead:
                    expert_up(i, s + 1)
                expert_down(i, s)

        rows_to_features(0, 0)
        rows_to_features(0, 1)
        expert_up(0, 0)
        with pe.Fori(0, C_ROUNDS - 1) as i:
            expert_round(i, True)
        expert_round(C_ROUNDS - 1, False)

        def next_before(i, e):
            if NEXT_Q <= e < NEXT_Q + 4:
                group = e - NEXT_Q
                if group == 0:
                    hold(pe, fm_ready, "D", i, 1)
                else:
                    hold(pe, q_ready, "D", i, group)
                mmul(psG[:, 0:PAIR], wk2[:, group * P:(group + 1) * P], hT[:, :], start=True, stop=True).then_inc(k_psum.sem, 1)
            if NEXT_Q + 4 <= e < NEXT_Q + 8:
                t = e - NEXT_Q - 4
                if t == 0:
                    hold(pe, q_ready, "D", i, 4)
                else:
                    hold(pe, v_ready, "D", i, t)
                mmul(psG[0:TOK, :], hT[:, tile(t)], wv2[:, :], start=True, stop=True).then_inc(v_psum.sem, 1)

        def next_behind(i, e):
            if e == NEXT_NORM + 2:
                hold(pe, ln_out, "D", i, 1)
                turn_to_features("D", i, u)
            if NEXT_Q <= e < NEXT_Q + 4:
                group = e - NEXT_Q
                hold(pe, k_ready, "D", i, group + 1)
                mmul(psG[:, 0:PAIR], wq2[:, group * P:(group + 1) * P], hT[:, :], start=True, stop=True).then_inc(q_psum.sem, 1)

        def round_of_d(i, final):
            hold(pe, k_ready, "D", i, 4)
            hold(pe, v_ready, "D", i, 4)
            def turn_heads(m):
                if CAT <= m < CAT + 2 * 4 and (m - CAT) % 2 == 0:
                    c = (m - CAT) // 2
                    if c == 0:
                        hold(pe, normed, "D", i, HEADS_D // 8)
                    else:
                        hold(pe, cat_T, "D", i, c)
                    for t in range(2):
                        last = nc.tensor.transpose(psS[3][:, tile(t)], o_all[:, t, c * P:(c + 1) * P], ident[0:TOK, 0:TOK])
                    last.then_inc(cat_psum.sem, 1)
                if m in (CAT + 10, CAT + 12):
                    if m == CAT + 10:
                        hold(pe, cat_T, "D", i, 4)
                    project_heads((m - CAT - 10) // 2)

            def project_heads(t):
                for c in range(4):
                    last = mmul(psG[0:TOK, t * D:(t + 1) * D], cat_b[:, c, tile(t)], wo2[:, c, :], start=c == 0, stop=c == 3)
                return last

            attention("D", i, 0, H2, HD2, HD2, qT, lambda t, n: v33[:, t, n, :], True, 1, turn_heads)
            hold(pe, normed, "D", i, HEADS_D // 4)
            for c in range(4):
                for t in range(2, TILES):
                    last = nc.tensor.transpose(psS[c][:, tile(t - 2)], o_all[:, t, c * P:(c + 1) * P], ident[0:TOK, 0:TOK])
                last.then_inc(cat_psum.sem, 1)
            hold(pe, cat_T, "D", i, 8)
            for t in range(2, TILES):
                last = project_heads(t)
            last.then_inc(proj_psum.sem, 1)
            hold(pe, ln_out, "D", i, 2)
            turn_to_features("D", i, u)
            hold(pe, fm_ready, "D", i, 2)
            for t in range(TILES):
                last = mmul(psG[0:TOK, t * E1:(t + 1) * E1], xT[:, tile(t)], gate_w[:, :], start=True, stop=True)
            last.then_inc(gate_psum.sem, 1)

            def up(e):
                s = e % 2
                for c in range(2):
                    if e >= 2:
                        hold(pe, mu_act, "D", i, 2 * (e - 2) + c + 1)
                    mmul(psS[2 * s + c][:, 0:PAIR], w1e[:, e, c * P:(c + 1) * P], xT[:, :], start=True, stop=True).then_inc(mu_psum.sem, 1)

            def down(e):
                s = e % 2
                hold(pe, mu_act, "D", i, 2 * e + 2)
                ps = ps_down[e % 3]
                if e >= 3:
                    hold(pe, me_norm, "D", i, e - 2)
                for t in range(TILES):
                    for c in range(2):
                        mmul(ps[0:TOK, t * D:(t + 1) * D], hm[s][:, c, tile(t)], w2e[:, e, c, :], start=c == 0, stop=False)
                    last = mmul(ps[0:TOK, t * D:(t + 1) * D], ones_h[:, :], b2_split[:, e, :], start=False, stop=True)
                last.then_inc(md_psum.sem, 1)

            pe.wait_ge(loaded_e.sem, 16 * len(expert_loads))
            up(0)
            up(1)
            down(0)
            hold(pe, comb_ready, "D", i, 1)
            for t in range(TILES):
                last = nc.tensor.transpose(psG[0:E1, tile(t)], comb[:, t, :], ident[0:TOK, 0:TOK])
            last.then_inc(combT_psum.sem, 1)
            hold(pe, combT_ready, "D", i, 1)
            for t in range(TILES):
                last = mmul(psG[0:TOK, t * D:(t + 1) * D], combT[:, tile(t)], beta_e[:, :], start=True, stop=True)
            last.then_inc(beta_psum.sem, 1)
            for e in range(E1):
                if 1 <= e and e + 1 < E1:
                    up(e + 1)
                if not final:
                    next_before(i + 1, e)
                if e:
                    down(e)
                if not final:
                    next_behind(i + 1, e)

        for e in range(E1):
            next_before(0, e)
            next_behind(0, e)
        with pe.Fori(0, ROUNDS - 1) as i:
            round_of_d(i, False)
        round_of_d(ROUNDS - 1, True)


_OUT = (BATCH, SEQ, D)


def kernel(**inputs):
    import numpy as _np
    import concourse.bacc as _bacc
    from concourse import mybir as _mybir
    from concourse.bass_utils import run_bass_kernel_spmd as _run

    nc = _bacc.Bacc("TRN2", target_bir_lowering=False, num_devices=1)
    arrays, handles = {}, {}
    for name, value in inputs.items():
        a = _np.ascontiguousarray(value)
        arrays["in_" + name] = a
        handles[name] = nc.dram_tensor("in_" + name, a.shape, _mybir.dt.from_np(a.dtype), kind="ExternalInput").ap()
    result = nc.dram_tensor("result", _OUT, _mybir.dt.float32, kind="ExternalOutput").ap()
    build(nc, handles, result)
    r = _run(nc, [arrays], core_ids=[0])
    return r.results[0]["result"]
```

```python
import numpy as np
import concourse.bass as bass
from concourse import mybir
from contextlib import ExitStack

F32 = mybir.dt.float32
BF16 = mybir.dt.bfloat16
U32 = mybir.dt.uint32
F32R = mybir.dt.float32r
I32 = mybir.dt.int32
ALU = mybir.AluOpType
ACT = mybir.ActivationFunctionType
AX = mybir.AxisListType

P = 128
BATCH, FRAMES, CH = 16, 256, 64
CONTEXT = 5
SEQ = FRAMES - (CONTEXT - 1)
WIN = CONTEXT * CH
D = 128
TOK = SEQ // 2
TILES = 4
PAIR = TILES * TOK
ROUNDS = BATCH // 2
N_TOKENS = BATCH * SEQ
EPS = 1e-5
H0, HD0 = 16, 8
V0, VD0 = 8, 16
LAMBDA_INIT = 0.8 - 0.6 * float(np.exp(-0.3 * 0))
MLP = 512
H1, HD1 = 8, 16
E0, F0 = 64, 512
TOP = 2
CAP = 2 * (N_TOKENS * TOP // E0)
H2, HD2 = 16, 32
E1, F1 = 16, 256
EXPERTS_A_ROUND = 4
CHAIN_B, SQUARED = 19, 16
PIECES = ((0, 0, V0), (1, 0, V0 // 2), (1, V0 // 2, V0))
TAIL_LINKS = 16
C_ROUNDS = E0 // EXPERTS_A_ROUND
DROPPED = 1 << 15
MASKED = -1e30
NC_F = MLP // P
SPLIT = 3
ZERO_ROWS = 16

assert CAP == SEQ and LAMBDA_INIT > 0

PHASE_ROUNDS = {"S": 1, "A": ROUNDS, "B": ROUNDS, "C": C_ROUNDS, "P": 1, "D": ROUNDS}


class Signal:

    def __init__(self, sem, growth):
        self.sem, self.growth, self.start = sem, growth, {}
        total = 0
        for phase, rounds in PHASE_ROUNDS.items():
            self.start[phase] = total
            total += rounds * growth.get(phase, 0)

    def value(self, phase, i, n):
        base = self.start[phase] + n
        return i * self.growth.get(phase, 0) + base


def build(nc, T, out):
    with ExitStack() as ctx:
        build_in(nc, T, out, ctx)


def build_in(nc, T, out, ctx):
    def sb(name, shape, dt=F32):
        return ctx.enter_context(nc.sbuf_tensor(name, shape, dt))

    def part(of, at, shape):
        size = int(np.prod(shape[1:]))
        ap = of[0:shape[0], at:at + size]
        if len(shape) == 2:
            return ap
        names = "abc"[:len(shape) - 1]
        return ap.rearrange(f"p ({' '.join(names)}) -> p {' '.join(names)}", **dict(zip(names, shape[1:])))

    def parts(of, at, *shapes):
        found = []
        for shape in shapes:
            found.append(part(of, at, shape))
            at += int(np.prod(shape[1:]))
        assert at <= of.shape[1], at
        return found

    def signal(name, **growth):
        return Signal(ctx.enter_context(nc.semaphore(name)), growth)

    slot_x = nc.dram_tensor("slot_x", [E0 * CAP, D], F32, kind="Internal").ap()
    slot_y = nc.dram_tensor("slot_y", [E0 * CAP, D], F32, kind="Internal").ap()

    psS = [ctx.enter_context(nc.psum_tensor(f"psS{j}", [P, 512], F32)) for j in range(4)]
    psT = [ctx.enter_context(nc.psum_tensor(f"psT{j}", [P, 512], F32)) for j in range(2)]
    psO = ctx.enter_context(nc.psum_tensor("psO", [P, 512], F32))
    psG = ctx.enter_context(nc.psum_tensor("psG", [P, 512], F32))
    ps_down = [psT[0], psT[1], psO]

    LATE = 7232
    with ExitStack() as phase_b:
        def sb_b(name, shape, dt=F32):
            return phase_b.enter_context(nc.sbuf_tensor(name, shape, dt))

        sb_b("zeros_before", [126, ZERO_ROWS * D])
        qs1 = sb_b("qs1", [P, 4, PAIR], F32R)
        ks1 = sb_b("ks1", [P, 4, PAIR], F32R)
        high_of = [sb_b(f"high{p}", [P, PAIR], F32R) for p in range(2)]
        v17m = sb_b("v17m", [TOK, TILES, 8, 17])
        hm_ = sb_b("hm_", [TOK, TILES, D])
        um_ = sb_b("um_", [TOK, TILES, D])
        om = sb_b("om", [TOK, TILES, D])
    arena = sb("arena", [P, LATE + 2 * E1 * D])
    y_all = sb("y_all", [P, E1 * F1])
    ident = sb("ident", [P, P])
    before = sb("before", [P, P])
    before_h = sb("before_h", [TOK, TOK], BF16)
    all_h = sb("all_h", [TOK, TOK], BF16)
    ones = sb("ones", [P, P])
    frac = sb("frac", [P, P])
    causal = sb("causal", [TOK, TOK])
    causal_h = sb("causal_h", [TOK, TOK], BF16)
    ident_h = sb("ident_h", [P, P], BF16)
    eps_t = sb("eps_t", [P, 32])
    mhalf = sb("mhalf", [P, 32])
    iota_i = sb("iota_i", [P, E0], I32)
    iota_f = sb("iota_f", [P, E0])

    colv = {n: sb("c_" + n, [P, 1]) for n in
            ("L0_tok_b", "L0_tok_gamma", "L0_tok_beta", "L0_attn_n1_w", "L0_attn_n1_b", "L0_attn_mln1_w",
             "L0_attn_mln1_b", "L0_ffn_ln1_g", "L0_ffn_ln1_b", "sub_w", "sub_w8")}
    colc = {n: sb("k_" + n, [P, NC_F]) for n in ("L0_attn_mb1", "L0_attn_mln2_w", "L0_attn_mln2_b")}
    rowb = {n: sb("r_" + n, [TOK, T[n].shape[0]]) for n in
            ("L0_attn_n2_w", "L0_attn_n2_b", "L0_ffn_ln2_g", "L0_ffn_ln2_b", "L1_attn_bo", "L1_ffn_gate_b",
             "L0_attn_lq1", "L0_attn_lk1", "L0_attn_lq2", "L0_attn_lk2")}
    beta_e = sb("beta_e", [E1, D])

    zero_t, nat_tok, nat_q, nat_k, nat_v, nat_o, nat_m1, nat_m2, nat_fq, nat_fk, nat_b1, nat_bl, nat_wo1, nat_b11, \
        w2raw, w2w, b2m_row, mb2_row, qkv1 = parts(
            arena, 0, [126, ZERO_ROWS * D], [P, WIN], [P, P], [P, P], [P, P], [P, P], [P, NC_F, P], [P, MLP], [P, D],
            [P, D], [E0, F0], [H2, D], [P, H2 * HD2], [E1, F1], [P, NC_F, D], [P, NC_F, D], [1, D], [1, D],
            [P, 3, H2, HD2])
    nat = {"Wq": nat_q, "Wk": nat_k, "Wv": nat_v, "Wo": nat_o}
    wl = part(y_all, 0, [P, H2, D])
    gamma_b, b2_rows = parts(arena, LATE, [TOK, E1, D], [SPLIT, E1, D])

    w_tok = sb("w_tok", [P, 3, D])
    wq0 = sb("wq0", [P, 4, P])
    wk0 = sb("wk0", [P, 4, P])
    wv0 = sb("wv0", [P, D])
    wo0 = sb("wo0", [P, D])
    w1m = sb("w1m", [P, MLP])
    w2m = sb("w2m", [P, NC_F, D + 1])
    b2m = sb("b2m", [TOK, D])
    neg_lam = sb("neg_lam", [TOK, 1])
    table = sb("table", [TOK, 4])
    lam_t = sb("lam_t", [TOK, 2, HD0])
    lam_s = sb("lam_s", [TOK, 2])
    lam_e = sb("lam_e", [TOK, 2])
    wq1 = sb("wq1", [P, 4, P])
    wk1 = sb("wk1", [P, 4, P])
    low_rows = sb("low_rows", [P, 4])
    wv1 = sb("wv1", [P, D])
    wo1 = sb("wo1", [P, D])
    wr = sb("wr", [P, E0])
    b1t = sb("b1t", [P, NC_F, E0])
    blt = sb("blt", [P, H2])
    wq2 = sb("wq2", [P, H2 * HD2])
    wk2 = sb("wk2", [P, H2 * HD2])
    wv2 = sb("wv2", [P, H2 * HD2])
    qb2 = sb("qb2", [P, 4])
    kb2 = sb("kb2", [P, 4])
    vb_row = sb("vb_row", [1, H2 * HD2])
    vb2 = sb("vb2", [TOK, H2 * HD2])
    wo2 = sb("wo2", [P, 4, D])
    gate_w = sb("gate_w", [P, E1])
    b1e = sb("b1e", [P, 2, E1])
    w1e = part(y_all, 0, [P, E1, F1])
    w2e = sb("w2e", [P, E1, 2, D])

    ones_h = sb("ones_h", [SPLIT, TOK], BF16)
    b2_split = sb("b2_split", [SPLIT, E1, D], BF16)
    b2_part = sb("b2_part", [SPLIT, E1 // 2, D], BF16)

    y_stats = sb("y_stats", [P, ROUNDS * 6])
    bn_mv = sb("bn_mv", [P, 2])
    bn_e = sb("bn_e", [P, 1])
    bn_r = sb("bn_r", [P, 1])
    bn_s = sb("bn_s", [P, 1])
    bn_m = sb("bn_m", [P, 1])
    bn_c = sb("bn_c", [P, 1])
    hx_all = sb("hx_all", [TOK, ROUNDS * TILES * D])
    gates_all = sb("gates_all", [TOK, ROUNDS * TILES * TOP])
    slots_all = sb("slots_all", [TOK, (ROUNDS + 1) * TILES * TOP], U32)

    hT = sb("hT", [P, PAIR])
    h = sb("h", [TOK, TILES, D])
    u = sb("u", [TOK, TILES, D])
    n_ = sb("n_", [TOK, TILES, D])
    h1 = sb("h1", [TOK, TILES, D])
    xT = sb("xT", [P, PAIR])
    with ExitStack() as phase_b:
        qs0 = sb_b("qs0", [P, 4, PAIR], F32R)
        ks0 = sb_b("ks0", [P, 4, PAIR], F32R)
    qT = sb("qT", [P, 4, PAIR])
    kT = sb("kT", [P, 4, PAIR])
    b2_left = [x[0:SPLIT, :, :].rearrange("p a b -> p (a b)")[:, 0:E1 // 2 * D].rearrange("p (e d) -> p e d", d=D) for x in (qT, kT)]
    big, sq = qT, kT
    v17 = sb("v17", [TOK, TILES, 8, 17])
    head_rows = sb("head_rows", [P, 4])
    k_head = [sb(f"k_head{j}", [P, SEQ]) for j in range(4)]
    nmax = sb("nmax", [TOK, 4, 2])
    sumsT = [k_head[j] for j in range(2)]
    prob = [sb(f"prob{j}", [TOK, 2, SEQ]) for j in range(2)]
    probT = [sb(f"probT{j}", [TOK, 2 * SEQ]) for j in range(2)]
    rden = sb("rden", [TOK, 2, 8])
    o_all = sb("o_all", [TOK, TILES, H2 * HD2])
    xw = (o_all[:, :, 0:WIN], hx_all[:, 0:TILES * WIN].rearrange("p (t k) -> p t k", t=TILES))
    oc = sb("oc", [TOK, TILES * V0, VD0])
    ocs = sb("ocs", [TOK, TILES * V0, VD0])
    ms = sb("ms", [TOK, TILES * V0])
    ms1 = sb("ms1", [TOK, TILES * V0])
    ms2 = sb("ms2", [TOK, TILES * V0])
    again_v = sb("again_v", [TOK, TILES])
    again_w = sb("again_w", [TOK, TILES])
    again_e = sb("again_e", [TOK, TILES])
    again_r = sb("again_r", [TOK, TILES])
    ln_st = sb("ln_st", [TOK, TILES, 6])
    ln_mv = sb("ln_mv", [TOK, TILES, 2])
    ln_e = sb("ln_e", [TOK, TILES])
    ln_r = sb("ln_r", [TOK, TILES])
    mm = sb("mm", [TOK, TILES, 2])
    mm2 = sb("mm2", [TOK, TILES])
    lg = sb("lg", [TOK, TILES, E0])
    mx = sb("mx", [TOK, TILES, 8])
    ix = sb("ix", [TOK, TILES, 8], U32)
    ixf = sb("ixf", [TOK, TILES, TOP])
    dlt = sb("dlt", [TOK, TILES])
    ex = sb("ex", [TOK, TILES])
    den = sb("den", [TOK, TILES])
    gate = sb("gate", [TOK, TILES, TOP])
    hot = sb("hot", [TOK, TILES, TOP, E0])
    hots = sb("hots", [TOK, TILES, E0], BF16)
    pos_e = sb("pos_e", [TOK, TILES, E0])
    carry = sb("carry", [TOK, E0])
    pos_h = sb("pos_h", [TOK, TILES, TOP, E0])
    pos = sb("pos", [TOK, TILES * TOP])
    keep = sb("keep", [TOK, TILES * TOP])
    slot_f = sb("slot_f", [TOK, TILES * TOP])
    drop_f = sb("drop_f", [TOK, TILES * TOP])
    slot_s = sb("slot_s", [TOK, TILES * TOP])
    slot_l = sb("slot_l", [TOK, TILES * TOP])
    slot_u = sb("slot_u", [TOK, TILES * TOP], U32)
    x2 = sb("x2", [TOK, TILES, D])
    SETS = EXPERTS_A_ROUND
    SET = 2 * F0 + D + 2 * D
    loads_in_flight = [parts(arena, s * SET, [P, F0], [P, NC_F, D], [1, D], [TOK, 2, D]) for s in range(SETS)]
    we1, we2, be2, xe = zip(*loads_in_flight)
    xeT0, xeT1, ye0, ye1 = parts(arena, SETS * SET, [P, CAP], [P, CAP], [TOK, 2, D], [TOK, 2, D])
    xeT, ye = (xeT0, xeT1), (ye0, ye1)
    he = [x[:, :, 0:CAP] for x in (qT, kT)]
    v33, gy, hm_both, nrm0, nrm1, acc = parts(
        arena, 0, [TOK, TILES, H2, HD2 + 1], [TOK, TILES * TOP, D], [P, 4, PAIR], [TOK, TILES, D],
        [TOK, TILES, D], [TOK, TILES, D])
    cat_b = hm_both
    hm, nrm = (hm_both[:, 0:2, :], hm_both[:, 2:4, :]), (nrm0, nrm1)
    slot_c = sb("slot_c", [TOK, TILES * TOP], U32)
    gate_c = sb("gate_c", [TOK, TILES * TOP])
    hot1 = sb("hot1", [TOK, TILES, TOP, E1])
    comb2 = sb("comb2", [TOK, TILES, TOP, E1])
    comb = sb("comb", [TOK, TILES, E1])
    combT = sb("combT", [E1, PAIR])
    s16 = sb("s16", [TOK, TILES, E1])
    e_st = [sb(f"e_st{s}", [TOK, TILES, 6]) for s in range(2)]
    e_mv = [sb(f"e_mv{s}", [TOK, TILES, 2]) for s in range(2)]
    e_e = sb("e_e", [TOK, TILES])
    e_r = sb("e_r", [TOK, TILES])
    e_s = [sb(f"e_s{s}", [TOK, TILES]) for s in range(2)]

    LN_B, LN_D = 4, 2
    FM_B, FM_D = 4, 2
    HEADS_B, HEADS_D = 2 * (H0 + H1), 2 * H2
    loaded = signal("loaded", S=0)
    loaded_e = signal("loaded_e", S=0)
    const_made = signal("const_made", S=0)
    prep_psum = signal("prep_psum", S=0)
    prep_done = signal("prep_done", S=0)
    prep_pool = signal("prep_pool", S=0)
    prep_act = signal("prep_act", S=0)
    cleared = signal("cleared", S=0)
    dve_link = signal("dve_link", S=0)
    ready = signal("ready", S=0)

    win_in = [signal(f"win_in{r}", A=16 * TILES // 2) for r in range(2)]
    win_psum = signal("win_psum", A=3)
    win_T = signal("win_T", A=3)
    conv_psum = signal("conv_psum", A=1)
    y_ready = signal("y_ready", A=1)
    y_counted = signal("y_counted", A=1)
    bn_link = signal("bn_link")
    bn_pool = signal("bn_pool")
    bn_ready = signal("bn_ready")

    round_done = signal("round_done", B=1)
    hT_ready = signal("hT_ready", B=1)
    h_psum = signal("h_psum", B=1)
    h_ready = signal("h_ready", B=1)
    ln_stats = signal("ln_stats", B=LN_B, D=LN_D)
    ln_aggr = signal("ln_aggr", B=LN_B, D=LN_D)
    ln_eps = signal("ln_eps", B=LN_B, D=LN_D)
    ln_rstd = signal("ln_rstd", B=LN_B, D=LN_D)
    ln_out = signal("ln_out", B=LN_B, D=LN_D)
    again_link = signal("again_link", B=2 * 3)
    again_rstd = signal("again_rstd", B=2)
    again_out = signal("again_out", B=2)
    fm_psum = signal("fm_psum", B=FM_B, D=FM_D)
    fm_ready = signal("fm_ready", B=FM_B, D=FM_D)
    q_psum = signal("q_psum", B=4 + 4, D=4)
    qs_ready = signal("qs_ready", B=4 + 4)
    q_ready = signal("q_ready", D=4)
    high_ready = [signal(f"high_ready{p}", B=4 + 4) for p in range(2)]
    k_psum = signal("k_psum", B=4 + 4, D=4)
    k_ready = signal("k_ready", B=4 + 4, D=4)
    v_psum = signal("v_psum", B=2, D=4)
    v_ready = signal("v_ready", B=2, D=4)
    scored = signal("scored", B=HEADS_B, D=HEADS_D)
    k_masked = signal("k_masked", D=HEADS_D)
    maxed = signal("maxed", B=HEADS_B, D=HEADS_D)
    probs = signal("probs", B=HEADS_B, D=HEADS_D)
    turned = signal("turned", B=HEADS_B, D=HEADS_D)
    taken_odd = signal("taken_odd", B=HEADS_B // 2, D=HEADS_D // 2)
    taken_even = signal("taken_even", B=H1, D=HEADS_D // 2)
    taken_first = signal("taken_first", B=H0)
    mixed = signal("mixed", B=HEADS_B, D=HEADS_D)
    sums_out = signal("sums_out", B=HEADS_B // 4)
    sums_back = signal("sums_back", B=HEADS_B // 4)
    recip = signal("recip", B=HEADS_B // 4, D=HEADS_D // 4)
    normed = signal("normed", B=HEADS_B // 4, D=HEADS_D // 4)
    chain = signal("chain", B=CHAIN_B, D=11)
    diff_ms = signal("diff_ms", B=len(PIECES))
    diff_e = signal("diff_e", B=len(PIECES))
    diff_r = signal("diff_r", B=len(PIECES))
    diff_out = signal("diff_out", B=1)
    proj_psum = signal("proj_psum", B=1, D=1)
    up_psum = signal("up_psum", B=4)
    up_act = signal("up_act", B=4)
    up_sq = signal("up_sq", B=4)
    down_psum = signal("down_psum", B=1)
    down_var = signal("down_var", B=1)
    down_e = signal("down_e", B=1)
    down_r = signal("down_r", B=1)
    x2_ready = signal("x2_ready", B=1)
    tail_fm_psum = signal("tail_fm_psum", B=2)
    tail_fm_ready = signal("tail_fm_ready", B=2)
    tail_proj = signal("tail_proj", B=1)
    tail_chain = signal("tail_chain", B=TAIL_LINKS)
    tail_stats = signal("tail_stats", B=1)
    tail_aggr = signal("tail_aggr", B=1)
    tail_eps = signal("tail_eps", B=1)
    tail_rstd = signal("tail_rstd", B=1)
    tail_out = signal("tail_out", B=1)
    route_psum = signal("route_psum", B=1)
    top_diff = signal("top_diff", B=1, D=1)
    top_exp = signal("top_exp", B=1, D=1)
    hot_ready = signal("hot_ready", B=1)
    rank_psum = signal("rank_psum", B=1)
    slots_ready = signal("slots_ready", B=1)
    scattered = signal("scattered", B=16 * TILES * TOP)

    N = EXPERTS_A_ROUND
    ew_in = [signal(f"ew_in{s}", C=16 * 4) for s in range(N)]
    xe_psum = [signal(f"xe_psum{s}", C=N // 2) for s in range(2)]
    xe_T = [signal(f"xe_T{s}", C=N // 2) for s in range(2)]
    eu_psum = [signal(f"eu_psum{s}", C=N) for s in range(2)]
    eu_act = [signal(f"eu_act{s}", C=N) for s in range(2)]
    ed_psum = [signal(f"ed_psum{s}", C=1) for s in range(N)]
    ye_ready = [signal(f"ye_ready{s}", C=N // 2) for s in range(2)]
    ye_out = [signal(f"ye_out{s}", C=16 * N // 2) for s in range(2)]

    b2_link = signal("b2_link")
    idx_ready = signal("idx_ready", P=1, D=1)
    gathered = signal("gathered", P=16 * TILES * TOP, D=16 * TILES * TOP)
    next_chain = signal("next_chain", D=2)
    gy_used = signal("gy_used", D=1)
    cat_psum = signal("cat_psum", D=8)
    cat_T = signal("cat_T", D=8)
    gate_psum = signal("gate_psum", D=1)
    comb_ready = signal("comb_ready", D=1)
    combT_psum = signal("combT_psum", D=1)
    combT_ready = signal("combT_ready", D=1)
    beta_psum = signal("beta_psum", D=1)
    acc_ready = signal("acc_ready", D=1)
    mu_psum = signal("mu_psum", D=2 * E1)
    mu_act = signal("mu_act", D=2 * E1)
    md_psum = signal("md_psum", D=E1)
    me_stats = signal("me_stats", D=E1)
    me_var = signal("me_var", D=E1)
    me_e = signal("me_e", D=E1)
    me_r = signal("me_r", D=E1)
    me_scale = signal("me_scale", D=E1)
    me_norm = signal("me_norm", D=E1)
    me_g = signal("me_g", D=E1)
    me_acc = signal("me_acc", D=E1)
    stored = signal("stored", D=16)

    due = {}

    def hold(eng, sig, phase, i, n):
        if isinstance(i, int) and sig.value(phase, i, n) <= 0:
            return
        eng.wait_ge(sig.sem, sig.value(phase, i, n))

    def hold_apart(eng, sig, phase, i, n):
        if isinstance(i, int) and sig.value(phase, i, n) <= 0:
            return
        name = str(eng.engine)
        if name not in due:
            due[name] = eng.alloc_register(f"due_{len(due)}")
        eng.reg_mov(due[name], sig.value(phase, i, n))
        eng.wait_ge(ready.sem, 1)
        eng.wait_ge(sig.sem, due[name])

    def bc(ap, axis, shape):
        return ap.unsqueeze(axis).broadcast_to(shape)

    tile = lambda t: slice(t * TOK, (t + 1) * TOK)

    def column(name):
        return T[name].rearrange("(p o) -> p o", o=1)

    loads = [(nat_tok[:, :], T["L0_tok_W"])]
    loads += [(nat[n][:, :], T["L0_attn_" + n]) for n in ("Wq", "Wk", "Wv", "Wo")]
    loads += [(colv[n][:, :], column(n)) for n in colv if n in T]
    loads += [(colv["sub_w"][j * VD0:(j + 1) * VD0, :], column("L0_attn_subln_w")) for j in range(V0)]
    loads += [(colc[n][:, c:c + 1], T[n][c * P:(c + 1) * P].rearrange("(p o) -> p o", o=1))
              for n in colc for c in range(NC_F)]
    loads += [(rowb[n][:, :], T[n].partition_broadcast(TOK)) for n in rowb]
    loads += [
        (mb2_row[:, :], T["L0_attn_mb2"].rearrange("(o d) -> o d", o=1)),
        (nat_m1[:, :, :], T["L0_attn_mW1"].rearrange("(c p) d -> p c d", p=P)),
        (nat_m2[:, :], T["L0_attn_mW2"]),
        (nat_fq[:, :], T["L0_ffn_wq"]), (nat_fk[:, :], T["L0_ffn_wk"]),
        (wv1[:, :], T["L0_ffn_wv"]), (wo1[:, :], T["L0_ffn_wo"]), (wr[:, :], T["L0_ffn_wr"]),
        (nat_b1[:, :], T["L0_ffn_b1"]), (nat_bl[:, :], T["L1_attn_bl"]), (nat_wo1[:, :], T["L1_attn_Wo"]),
        (nat_b11[:, :], T["L1_ffn_b1"]), (wl[:, :, :], T["L1_attn_Wl"].rearrange("h o i -> o h i")),
        (qkv1[:, 0, :, :], T["L1_attn_Wq"].rearrange("h i d -> i h d")),
        (qkv1[:, 1, :, :], T["L1_attn_Wk"].rearrange("h i d -> i h d")),
        (qkv1[:, 2, :, :], T["L1_attn_Wv"].rearrange("h i d -> i h d")),
        (gate_w[:, :], T["L1_ffn_gate_w"]),
        (b2_rows[:, :, :].rearrange("o e d -> o (e d)"), T["L1_ffn_b2"].rearrange("e d -> (e d)").partition_broadcast(SPLIT)),
    ]
    expert_loads = [
        (w1e[:, :, :], T["L1_ffn_w1"].rearrange("e d f -> d e f")),
        (w2e[:, :, :, :].rearrange("p e c d -> p (e c) d"), T["L1_ffn_w2"].rearrange("e (c p) d -> p (e c) d", p=P)),
        (gamma_b[:, :, :].rearrange("p e d -> p (e d)"), T["L1_ffn_gamma"].rearrange("e d -> (e d)").partition_broadcast(TOK)),
        (beta_e[:, :], T["L1_ffn_beta"]),
    ]

    def heads(ap, n, hd):
        return ap.rearrange("p (n d) -> p n d", d=hd)

    turns = [(nat_tok[:, 0:128], w_tok[:, 0, :], None), (nat_tok[:, 128:256], w_tok[:, 1, :], None),
             (nat_tok[:, 256:320], w_tok[0:64, 2, :], None)]
    def thirds(w, hd):
        return w[:, :, :].rearrange("p g (j s) -> p (g j) s", s=4 * hd)[:, :, 0:3 * hd].rearrange("p n (r d) -> p n r d", r=3)

    for n, w in (("Wq", wq0), ("Wk", wk0)):
        turns.append((nat[n][:, :], thirds(w, HD0), HD0))
    turns += [(nat["Wv"][:, :], wv0[:, :], None), (nat["Wo"][:, :], wo0[:, :], None)]
    for c in range(NC_F):
        turns.append((nat_m1[:, c, :], w1m[:, c * P:(c + 1) * P], None))
        turns.append((nat_m2[:, c * P:(c + 1) * P], w2raw[:, c, :], None))
        turns.append((nat_wo1[:, c * P:(c + 1) * P], wo2[:, c, :], None))
        turns.append((nat_b1.rearrange("p (f c) -> p c f", c=NC_F)[:, c, :], b1t[:, c, :], None))
    turns.append((nat_bl[:, :], blt[:, :], None))
    for c in range(2):
        turns.append((nat_b11[:, c * P:(c + 1) * P], b1e[:, c, :], None))
    win_banks = ((psS[0], psS[1], psS[2]), (psS[3], psT[0], psT[1]))
    win_turned = (qT, kT)
    RING = 4
    N_TURNS = len(turns)
    STEP_MEAN, STEP_B2, STEP_B2B, STEP_QKV, STEP_QB, STEP_KB, STEP_VB, STEP_VBB = (
        N_TURNS + 1, N_TURNS + 2, N_TURNS + 3, N_TURNS + 4, N_TURNS + 4 + H2, N_TURNS + 5 + H2,
        N_TURNS + 6 + H2, N_TURNS + 7 + H2)

    def taken(phase, off, m):
        if m % 2:
            return taken_odd, (off + m) // 2
        return (taken_first if phase == "B" and off == 0 else taken_even), m // 2

    def take_turned(eng, copy, phase, i, off, m, causal_):
        hold(eng, turned, phase, i, off + m + 1)
        if m >= 2:
            hold(eng, mixed, phase, i, off + m - 1)
        if causal_:
            copy(eng, probT[m % 2][:, 0:SEQ], psT[m % 2][0:TOK, 0:SEQ])
            copy(eng, probT[m % 2][:, SEQ + TOK:2 * SEQ], psT[m % 2][0:TOK, SEQ + TOK:2 * SEQ]).then_inc(taken(phase, off, m)[0].sem, 1)
        else:
            copy(eng, probT[m % 2][:, :], psT[m % 2][0:TOK, 0:2 * SEQ]).then_inc(taken(phase, off, m)[0].sem, 1)

    def gates(dve, v, phase, i, link):
        hold(dve, top_exp, phase, i, 1)
        link(phase, i, v.tensor_scalar(den[:, :], ex[:, :], 1.0, None, ALU.add))
        link(phase, i, v.reciprocal(gate[:, :, 0], den[:, :]))
        link(phase, i, v.tensor_tensor(gate[:, :, 1], ex[:, :], gate[:, :, 0], ALU.mult))

    HEAD_FM, HEAD_Q, HEAD_V = 2, 4, 13
    TAIL_X2, TAIL_TOP, TAIL_RANK = 7, 14, 17
    NEXT_NORM, NEXT_Q = 5, 8
    CAT = 18

    S_RING = 3

    CONSTS = 3 + 3 + 7 + 1 + 4 + 1
    CLEARS = E0 * CAP // (126 * ZERO_ROWS)

    block = ctx.enter_context(nc.Block())

    @block.sync
    def _(sp):
        for dst, src in loads:
            sp.dma_start(dst, src, allow_slow_non_contiguous=True).then_inc(loaded.sem, 16)
        sp.wait_ge(const_made.sem, CONSTS)
        rows = slot_x.rearrange("(n p r) d -> n p (r d)", p=126, r=ZERO_ROWS)
        for n in range(rows.shape[0]):
            sp.dma_start(rows[n], zero_t[:, :]).then_inc(cleared.sem, 16)
        def windows(i):
            for r in range(2):
                hold_apart(sp, win_psum, "A", 2 * i + r - 2, 3)
                for b in range(2):
                    for half in range(2):
                        src = bass.AP(T["x"].tensor, ((2 * i + r) * 2 + b) * (FRAMES * CH) + half * TOK * CH,
                                      [[CH, TOK], [1, WIN]])
                        sp.dma_start(xw[r][:, 2 * b + half, :], src).then_inc(win_in[r].sem, 16)

        windows(0)
        with sp.Fori(1, ROUNDS // 2) as i:
            windows(i)

        sp.wait_ge(scattered.sem, scattered.value("C", 0, 0))
        sp.wait_ge(round_done.sem, round_done.value("C", 0, 0))
        def experts_in(i):
            for s in range(N):
                e = i * N + s
                hold_apart(sp, ed_psum[s], "C", i, 0)
                sp.dma_start(xe[s][:, :, :], bass.AP(slot_x.tensor, e * (CAP * D), [[D, TOK], [TOK * D, 2], [1, D]])).then_inc(ew_in[s].sem, 16)
                sp.dma_start(we1[s][:, :], bass.AP(T["L0_ffn_w1"].tensor, e * (D * F0), [[F0, P], [1, F0]])).then_inc(ew_in[s].sem, 16)
                sp.dma_start(we2[s][:, :, :], bass.AP(T["L0_ffn_w2"].tensor, e * (D * F0), [[NC_F * D, P], [D, NC_F], [1, D]])).then_inc(ew_in[s].sem, 16)
                sp.dma_start(be2[s][:, :], bass.AP(T["L0_ffn_b2"].tensor, e * D, [[D, 1], [1, D]])).then_inc(ew_in[s].sem, 16)

        experts_in(0)
        with sp.Fori(1, C_ROUNDS) as i:
            experts_in(i)

        for dst, src in expert_loads:
            sp.dma_start(dst, src, allow_slow_non_contiguous=True).then_inc(loaded_e.sem, 16)

        with sp.Fori(0, ROUNDS) as i:
            hold_apart(sp, me_acc, "D", i, E1)
            sp.dma_start(bass.AP(out.tensor, i * (PAIR * D), [[D, TOK], [TOK * D, TILES], [1, D]]),
                         acc[:, :, :]).then_inc(stored.sem, 16)
        sp.wait_ge(stored.sem, 16 * ROUNDS)

    @block.gpsimd
    def _(pool):
        g = nc.gpsimd
        g.memset(ident[:, :], 0.0).then_inc(const_made.sem, 1)
        g.memset(before[:, :], 1.0).then_inc(const_made.sem, 1)
        g.memset(causal[:, :], 0.0).then_inc(const_made.sem, 1)
        pool.wait_ge(const_made.sem, 3)
        g.affine_select(out=ident[:, :], in_=ident[:, :], compare_op=ALU.not_equal, fill=1.0, base=0,
                        pattern=[[-1, P]], channel_multiplier=1).then_inc(const_made.sem, 1)
        g.affine_select(out=before[:, :], in_=before[:, :], compare_op=ALU.is_gt, fill=0.0, base=0,
                        pattern=[[1, P]], channel_multiplier=-1).then_inc(const_made.sem, 1)
        g.affine_select(out=causal[:, :], in_=causal[:, :], compare_op=ALU.is_ge, fill=MASKED, base=0,
                        pattern=[[-1, TOK]], channel_multiplier=1).then_inc(const_made.sem, 1)
        g.memset(ones[:, :], 1.0).then_inc(const_made.sem, 1)
        g.memset(frac[:, :], 1.0 / MLP).then_inc(const_made.sem, 1)
        g.memset(eps_t[:, :], EPS).then_inc(const_made.sem, 1)
        g.memset(mhalf[:, :], -0.5).then_inc(const_made.sem, 1)
        g.memset(zero_t[:, :], 0.0).then_inc(const_made.sem, 1)
        g.memset(carry[:, :], 0.0).then_inc(const_made.sem, 1)
        g.memset(slots_all[:, ROUNDS * TILES * TOP:], 0).then_inc(const_made.sem, 1)
        g.iota(iota_i[:, :], pattern=[[1, E0]], base=0, channel_multiplier=0).then_inc(const_made.sem, 1)
        for w in (wq0, wk0, wq1, wk1):
            g.memset(w[:, :, :], 0.0).then_inc(const_made.sem, 1)
        g.memset(v17[:, :, :, VD0:VD0 + 1], 1.0).then_inc(const_made.sem, 1)

        pool.wait_ge(bn_link.sem, 1)
        g.tensor_tensor(bn_e[:, :], bn_mv[:, 1:2], eps_t[:, 0:1], ALU.add).then_inc(bn_pool.sem, 1)
        pool.wait_ge(bn_pool.sem, 1)
        g.tensor_tensor(bn_r[:, :], bn_e[:, :], mhalf[:, 0:1], ALU.pow).then_inc(bn_pool.sem, 1)

        def rstd(phase, i, k, n, src, e_sig, mid, r_sig, dst, given):
            hold_apart(pool, given, phase, i, k + 1)
            g.tensor_tensor(mid, src, eps_t[0:TOK, 0:n], ALU.add).then_inc(e_sig.sem, 1)
            hold_apart(pool, e_sig, phase, i, k + 1)
            g.tensor_tensor(dst, mid, mhalf[0:TOK, 0:n], ALU.pow).then_inc(r_sig.sem, 1)

        def norm(phase, i, k):
            rstd(phase, i, k, TILES, ln_mv[:, :, 1], ln_eps, ln_e[:, :], ln_rstd, ln_r[:, :], ln_aggr)

        def norm_again(phase, i, k, j):
            hold_apart(pool, ln_rstd, phase, i, k + 1)
            g.tensor_tensor(again_v[:, :], ln_mv[:, :, 1], ln_r[:, :], ALU.mult).then_inc(again_link.sem, 1)
            hold_apart(pool, again_link, phase, i, 3 * j + 1)
            g.tensor_tensor(again_w[:, :], again_v[:, :], ln_r[:, :], ALU.mult).then_inc(again_link.sem, 1)
            hold_apart(pool, again_link, phase, i, 3 * j + 2)
            g.tensor_tensor(again_e[:, :], again_w[:, :], eps_t[0:TOK, 0:TILES], ALU.add).then_inc(again_link.sem, 1)
            hold_apart(pool, again_link, phase, i, 3 * j + 3)
            g.tensor_tensor(again_r[:, :], again_e[:, :], mhalf[0:TOK, 0:TILES], ALU.pow).then_inc(again_rstd.sem, 1)

        def head_of_round(i):
            norm("B", i, 0)
            norm_again("B", i, 0, 0)

        def piece_rstd(i, j):
            b, v0, v1 = PIECES[j]
            hold_apart(pool, diff_ms, "B", i, j + 1)
            n = 2 * (v1 - v0)
            pick = lambda x: x[:, 2 * b * V0:(2 * b + 2) * V0].rearrange("p (t n) -> p t n", t=2)[:, :, v0:v1]
            flat = lambda x: x[0:TOK, 0:n].rearrange("p (t n) -> p t n", t=2)
            g.tensor_tensor(pick(ms2), pick(ms1), flat(eps_t), ALU.add).then_inc(diff_e.sem, 1)
            hold_apart(pool, diff_e, "B", i, j + 1)
            g.tensor_tensor(pick(ms), pick(ms2), flat(mhalf), ALU.pow).then_inc(diff_r.sem, 1)

        def tail_of_round(i, final):
            rstd("B", i, 0, TILES, ln_mv[:, :, 1], tail_eps, ln_e[:, :], tail_rstd, ln_r[:, :], tail_aggr)
            if not final:
                piece_rstd(i + 1, 0)
            pool.wait_ge(cleared.sem, 16 * CLEARS)
            hold_apart(pool, slots_ready, "B", i, 1)
            for t in range(TILES):
                for k in range(TOP):
                    c = t * TOP + k
                    g.indirect_dma_start(out=slot_x, out_offset=bass.IndirectOffsetOnAxis(ap=slot_u[:, c:c + 1], axis=0),
                                         in_=x2[:, t, :], in_offset=None, bounds_check=E0 * CAP - 1,
                                         oob_is_err=False).then_inc(scattered.sem, 16)

        def round_of_b(i, first, final):
            if not first:
                tail_of_round(i - 1, False)
            else:
                piece_rstd(i, 0)
            piece_rstd(i, 1)
            piece_rstd(i, 2)
            norm("B", i, 1)
            norm("B", i, 2)
            rstd("B", i, 0, TILES, mm2[:, :], down_e, ln_e[:, :], down_r, ln_r[:, :], down_var)
            norm("B", i, 3)
            norm_again("B", i, 3, 1)
            if not final:
                head_of_round(i + 1)

        head_of_round(0)
        round_of_b(0, True, False)
        with pool.Fori(1, ROUNDS - 1) as i:
            round_of_b(i, False, False)
        round_of_b(ROUNDS - 1, False, True)
        tail_of_round(ROUNDS - 1, True)

        with pool.Fori(0, C_ROUNDS) as i:
            for s in range(N):
                p, q = s % 2, s // 2
                hold_apart(pool, ye_ready[p], "C", i, q + 1)
                g.dma_start(bass.AP(slot_y.tensor, (i * N + s) * (CAP * D), [[D, TOK], [TOK * D, 2], [1, D]]),
                            ye[p][:, :, :]).then_inc(ye_out[p].sem, 16)
        for p in range(2):
            pool.wait_ge(ye_out[p].sem, 16 * E0 // 2)

        def gather_rows():
            for c in range(TILES * TOP):
                g.indirect_dma_start(out=gy[:, c, :], out_offset=None, in_=slot_y,
                                     in_offset=bass.IndirectOffsetOnAxis(ap=slot_c[:, c:c + 1], axis=0),
                                     bounds_check=E0 * CAP - 1, oob_is_err=False).then_inc(gathered.sem, 16)

        def gather_next(i):
            hold_apart(pool, idx_ready, "D", i, 1)
            hold_apart(pool, gy_used, "D", i, 1)
            gather_rows()

        def experts_round(i, final):
            norm("D", i, 1)

            def scale(e):
                s = e % 2
                rstd("D", i, e, TILES, e_mv[s][:, :, 1], me_e, e_e[:, :], me_r, e_r[:, :], me_var)
                hold_apart(pool, me_r, "D", i, e + 1)
                g.tensor_tensor(e_s[s][:, :], e_r[:, :], comb[:, :, e], ALU.mult).then_inc(me_scale.sem, 1)

            scale(0)
            for e in range(E1):
                if e + 1 < E1:
                    scale(e + 1)
                hold_apart(pool, me_g, "D", i, e + 1)
                g.tensor_tensor(acc[:, :, :], acc[:, :, :], nrm[e % 2][:, :, :], ALU.add).then_inc(me_acc.sem, 1)
                hold_apart(pool, me_acc, "D", i, e + 1)
                if e == NEXT_NORM - 1 and not final:
                    norm("D", i + 1, 0)
            if not final:
                gather_next(i + 1)

        pool.wait_ge(idx_ready.sem, 1)
        gather_rows()
        norm("D", 0, 0)
        gather_next(0)
        with pool.Fori(0, ROUNDS - 1) as i:
            experts_round(i, False)
        experts_round(ROUNDS - 1, True)
        pool.wait_ge(gathered.sem, 16 * TILES * TOP * (ROUNDS + 1))

    @block.scalar
    def _(act):
        a = nc.scalar
        act.wait_ge(prep_done.sem, STEP_VBB)
        a.activation(lam_e[:, :], lam_s[:, :], ACT.Exp).then_inc(prep_act.sem, 1)
        act.wait_ge(ready.sem, 1)

        with act.Fori(0, ROUNDS) as i:
            hold_apart(act, conv_psum, "A", i, 1)
            a.activation(y_all[:, bass.ds(i * PAIR, PAIR)], psG[:, 0:PAIR], ACT.Relu,
                         bias=colv["L0_tok_b"][:, :]).then_inc(y_ready.sem, 1)

        def feature_major(phase, i, k, weight, bias, turned_=fm_psum, ready_=fm_ready, dst=xT):
            hold(act, turned_, phase, i, k + 1)
            more = {}
            if weight is not None:
                more["scale"] = weight[:, :]
            if bias is not None:
                more["bias"] = bias[:, :]
            a.activation(dst[:, :], psG[:, 0:PAIR], ACT.Identity, **more).then_inc(ready_.sem, 1)

        def high_parts(i, k, p, ps):
            hold(act, (q_psum, k_psum)[p], "B", i, k + 1)
            if k:
                hold(act, (qs_ready, k_ready)[p], "B", i, k)
            a.activation(high_of[p][:, :], ps[:, 0:PAIR], ACT.Identity).then_inc(high_ready[p].sem, 1)

        def query_group(phase, i, k, dst, ps, scale, **more):
            hold(act, q_psum, phase, i, k + 1)
            a.activation(dst, ps[:, 0:PAIR], ACT.Identity, scale=scale, **more).then_inc(q_ready.sem, 1)

        def copy_sums(i, off, gr):
            hold(act, mixed, "B", i, off + 4 * gr + 4)
            last_back = off // 4 + gr - 1
            if last_back > 0:
                hold(act, sums_back, "B", i, last_back)
            a.copy(sumsT[gr % 2][:, :], psO[:, 0:SEQ]).then_inc(sums_out.sem, 1)

        def attention(phase, i, off, steps, causal_, beside=None):
            for m in range(steps + 1):
                if m < steps:
                    hold(act, maxed, phase, i, off + m + 1)
                    if m >= 2:
                        hold(act, turned, phase, i, off + m - 1)
                    for t in range(2):
                        keys = TOK if causal_ and t == 0 else SEQ
                        last = a.activation(prob[m % 2][:, t, 0:keys], psS[m % S_RING][0:TOK, t * 256:t * 256 + keys],
                                            ACT.Exp, bias=nmax[:, m % 4, t:t + 1])
                    last.then_inc(probs.sem, 1)
                if m >= 1 and ((m - 1) % 2 == 1 or phase == "B" and off == 0):
                    take(act, phase, i, off, m - 1, causal_)
                if phase == "B" and m >= 5 and m % 4 == 1 and m < steps:
                    copy_sums(i, off, (m - 5) // 4)
                if beside is not None:
                    beside(m)
            if phase == "B":
                copy_sums(i, off, steps // 4 - 1)

        def take_copy(eng, dst, src):
            return nc.scalar.copy(dst, src) if eng is act else nc.vector.tensor_copy(dst, src)

        def take(eng, phase, i, off, m, causal_):
            take_turned(eng, take_copy, phase, i, off, m, causal_)

        act.wait_ge(bn_ready.sem, 1)

        def before_head(i):
            a.activation(hT[:, :], y_all[:, bass.ds(i * PAIR, PAIR)], ACT.Identity,
                         bias=bn_c[:, :], scale=bn_s[:, :]).then_inc(hT_ready.sem, 1)

        def head_of_round(i, m):
            if m == HEAD_FM + 2:
                feature_major("B", i, 0, colv["L0_attn_n1_w"], colv["L0_attn_n1_b"])
            if m - HEAD_Q - 1 in range(8):
                group, p = divmod(m - HEAD_Q - 1, 2)
                high_parts(i, group, p, (psG, psS[3])[p])

        def tail_of_round(i, m):
            if m == 2:
                feature_major("B", i, 0, None, None, tail_fm_psum, tail_fm_ready)
            if m == TAIL_X2 + 3:
                feature_major("B", i, 1, None, None, tail_fm_psum, tail_fm_ready)
            if m == TAIL_TOP + 2:
                hold(act, top_diff, "B", i, 1)
                a.activation(ex[:, :], dlt[:, :], ACT.Exp).then_inc(top_exp.sem, 1)

        def round_of_b(i, first, final):
            attention("B", i, 0, 2 * H0, False, None if first else lambda m: tail_of_round(i - 1, m))
            feature_major("B", i, 1, colv["sub_w8"], None)
            a.activation(table[:, 0:1], neg_lam[:, :], ACT.Gelu)
            if not final:
                before_head(i + 1)
            feature_major("B", i, 2, colv["L0_attn_mln1_w"], colv["L0_attn_mln1_b"])
            for c in range(NC_F):
                hold(act, up_psum, "B", i, c + 1)
                a.activation(big[:, c, :], psS[c][:, 0:PAIR], ACT.Gelu,
                             bias=colc["L0_attn_mb1"][:, c:c + 1]).then_inc(up_act.sem, 1)
            a.activation(table[:, 1:2], neg_lam[:, :], ACT.Exp)
            feature_major("B", i, 3, colv["L0_ffn_ln1_g"], colv["L0_ffn_ln1_b"])
            for group in range(4):
                high_parts(i, 4 + group, 0, psS[2 * (group % 2)])
                high_parts(i, 4 + group, 1, psS[2 * (group % 2) + 1])
            attention("B", i, 2 * H0, 2 * H1, False, None if final else lambda m: head_of_round(i + 1, m))

        before_head(0)
        for m in range(2 * H1 + 1):
            head_of_round(0, m)
        round_of_b(0, True, False)
        with act.Fori(1, ROUNDS - 1) as i:
            round_of_b(i, False, False)
        round_of_b(ROUNDS - 1, False, True)
        for m in range(2 * H0 + 1):
            tail_of_round(ROUNDS - 1, m)

        def hidden_layers(i):
            for s in range(N):
                p, q = s % 2, s // 2
                if q:
                    hold(act, ed_psum[s - 2], "C", i, 1)
                else:
                    hold(act, ed_psum[s + N - 2], "C", i, 0)
                for half in range(2):
                    hold_apart(act, eu_psum[p], "C", i, 2 * q + half + 1)
                    for c in (2 * half, 2 * half + 1):
                        last = a.activation(he[p][:, c, :], psS[2 * p + half][:, (c % 2) * 256:(c % 2) * 256 + CAP], ACT.Gelu_apprx_tanh,
                                            bias=b1t[:, c, bass.ds(i * N + s, 1)])
                    last.then_inc(eu_act[p].sem, 1)

        hidden_layers(0)
        with act.Fori(1, C_ROUNDS) as i:
            hidden_layers(i)

        def next_queries(i, e):
            if e == NEXT_NORM + 4:
                feature_major("D", i, 0, None, None, dst=hT)
            if NEXT_Q + 2 <= e < NEXT_Q + 6:
                group = e - NEXT_Q - 2
                query_group("D", i, group, qT[:, group, :], psG, 1.0, bias=qb2[:, group:group + 1])

        def round_of_d(i, final):
            def turned_heads(m):
                if CAT < m <= CAT + 2 * 4 and (m - CAT) % 2 == 0:
                    c = (m - CAT) // 2 - 1
                    hold(act, cat_psum, "D", i, c + 1)
                    a.copy(cat_b[:, c, 0:2 * TOK], psS[3][:, 0:2 * TOK]).then_inc(cat_T.sem, 1)

            attention("D", i, 0, 2 * H2, True, turned_heads)
            for c in range(4):
                hold(act, cat_psum, "D", i, 4 + c + 1)
                a.copy(cat_b[:, c, 2 * TOK:PAIR], psS[c][:, 0:2 * TOK]).then_inc(cat_T.sem, 1)
            feature_major("D", i, 1, None, None)
            hold(act, top_diff, "D", i, 1)
            a.activation(ex[:, :], dlt[:, :], ACT.Exp).then_inc(top_exp.sem, 1)
            for e in range(E1):
                s = e % 2
                if not final:
                    next_queries(i + 1, e)
                if e == 0:
                    a.activation(table[:, 2:3], neg_lam[:, :], ACT.Gelu)
                for c in range(2):
                    hold(act, mu_psum, "D", i, 2 * e + c + 1)
                    if e >= 2 and c == 0:
                        hold(act, md_psum, "D", i, e - 1)
                    a.activation(hm[s][:, c, :], psS[2 * s + c][:, 0:PAIR], ACT.Gelu,
                                 bias=b1e[:, c, e:e + 1]).then_inc(mu_act.sem, 1)
            a.activation(table[:, 3:4], neg_lam[:, :], ACT.Exp)

        for e in range(E1):
            next_queries(0, e)
        round_of_d(0, False)
        with act.Fori(1, ROUNDS - 1) as i:
            round_of_d(i, False)
        round_of_d(ROUNDS - 1, True)

    @block.vector
    def _(dve):
        v = nc.vector
        count = [0]

        def step(ins):
            count[0] += 1
            ins.then_inc(dve_link.sem, 1)
            dve.wait_ge(dve_link.sem, count[0])

        dve.wait_ge(const_made.sem, CONSTS)
        dve.wait_ge(loaded.sem, 16 * len(loads))
        v.tensor_copy(iota_f[:, :], iota_i[:, :])
        v.tensor_reduce(head_rows[:, :], ident[:, :].rearrange("p (j r) -> p j r", j=4), AX.X, ALU.add)
        v.tensor_copy(ident_h[:, :], ident[:, :])
        v.memset(ones_h[:, :], 1.0)
        v.memset(all_h[:, :], 1.0)
        v.tensor_copy(before_h[:, :], before[0:TOK, 0:TOK])
        v.tensor_copy(causal_h[:, :], causal[:, :])
        v.memset(w2m[:, :, D:D + 1], 1.0 / MLP)
        v.tensor_scalar(colv["sub_w8"][:, :], colv["sub_w"][:, :], 1.0 - LAMBDA_INIT, None, ALU.mult)
        def scaled_heads(dst, src, hd, scaled):
            n = src.shape[1]
            return v.tensor_scalar(dst, bc(src, 2, [P, n, 3, hd]), hd ** -0.5 if scaled else 1.0, None, ALU.mult)

        for k, (hd, r) in enumerate(((HD0, 2), (HD0, 1), (HD1, 2), (HD1, 1))):
            rows = ident[:, :].rearrange("p (n s) -> p n s", s=4 * hd)[:, :, r * hd:(r + 1) * hd]
            step(v.tensor_reduce(low_rows[:, k:k + 1], rows, AX.XY, ALU.add))
        step(v.tensor_scalar(low_rows[:, :], low_rows[:, :], -1.0, None, ALU.mult))
        for w, src in ((wq1, nat_fq), (wk1, nat_fk)):
            scaled_heads(thirds(w, HD1), heads(src[:, :], H1, HD1), HD1, w is wq1)
        for j, (x, y) in enumerate((("lq1", "lk1"), ("lq2", "lk2"))):
            step(v.tensor_tensor(lam_t[:, j, :], rowb["L0_attn_" + x][:, :], rowb["L0_attn_" + y][:, :], ALU.mult))
        v.tensor_reduce(lam_s[:, :], lam_t[:, :, :], AX.X, ALU.add)
        for k, (src, dst, hd) in enumerate(turns):
            dve.wait_ge(prep_psum.sem, k + 1)
            rows, cols = src.shape[1], src.shape[0]
            ps = psS[k % RING][0:rows, 0:cols]
            ins = v.tensor_copy(dst, ps) if hd is None else scaled_heads(dst, heads(ps, cols // hd, hd), hd, src is turns[3][0])
            ins.then_inc(prep_done.sem, 1)
        dve.wait_ge(prep_done.sem, N_TURNS)
        for c in range(NC_F):
            last = v.tensor_scalar(w2w[:, c, :], w2raw[:, c, :], colc["L0_attn_mln2_w"][:, c:c + 1], None, ALU.mult)
        last.then_inc(prep_pool.sem, 1)
        dve.wait_ge(prep_psum.sem, STEP_MEAN)
        dve.wait_ge(prep_pool.sem, 1)
        v.tensor_tensor(w2m[:, :, 0:D], w2w[:, :, :], bc(psS[0][:, 0:D], 1, [P, NC_F, D]), ALU.subtract).then_inc(prep_done.sem, 1)
        dve.wait_ge(prep_psum.sem, STEP_B2)
        v.tensor_tensor(b2m_row[:, :], psS[1][0:1, 0:D], mb2_row[:, :], ALU.add).then_inc(prep_done.sem, 1)
        dve.wait_ge(prep_psum.sem, STEP_B2B)
        v.tensor_copy(b2m[:, :], psS[2][0:TOK, 0:D]).then_inc(prep_done.sem, 1)
        for n in range(H2):
            dve.wait_ge(prep_psum.sem, STEP_QKV + n)
            for x, w in enumerate((wq2, wk2, wv2)):
                last = v.tensor_copy(w[:, n * HD2:(n + 1) * HD2], psS[n % RING][:, x * HD2:(x + 1) * HD2])
            last.then_inc(prep_done.sem, 1)
        for k, dst in ((STEP_QB, qb2), (STEP_KB, kb2)):
            dve.wait_ge(prep_psum.sem, k + 0)
            v.tensor_copy(dst[:, :], psT[0 if dst is qb2 else 1][:, 0:4]).then_inc(prep_done.sem, 1)
        dve.wait_ge(prep_psum.sem, STEP_VB)
        v.tensor_copy(vb_row[:, :], psO[0:1, :]).then_inc(prep_done.sem, 1)
        dve.wait_ge(prep_psum.sem, STEP_VBB)
        v.tensor_copy(vb2[:, :], psG[0:TOK, :]).then_inc(prep_done.sem, 1)
        dve.wait_ge(prep_act.sem, 1)
        step(v.tensor_tensor(lam_s[:, 0:1], lam_e[:, 1:2], lam_e[:, 0:1], ALU.subtract))
        v.tensor_scalar(neg_lam[:, :], lam_s[:, 0:1], -LAMBDA_INIT, None, ALU.add).then_inc(ready.sem, 1)

        def windows_out(i, r):
            hold(dve, conv_psum, "A", i - 2, 1)
            for c in range(3):
                rows = P if c < 2 else WIN - 2 * P
                hold(dve, win_psum, "A", i, c + 1)
                v.tensor_copy(win_turned[r][0:rows, c, :], win_banks[r][c][0:rows, 0:PAIR]).then_inc(win_T.sem, 1)

        def count(i):
            hold_apart(dve, y_ready, "A", i, 1)
            v.bn_stats(y_stats[:, bass.ds(i * 6, 6)], y_all[:, bass.ds(i * PAIR, PAIR)]).then_inc(y_counted.sem, 1)

        windows_out(0, 0)
        windows_out(1, 1)
        count(0)
        with dve.Fori(1, ROUNDS // 2) as i:
            windows_out(2 * i, 0)
            count(2 * i - 1)
            windows_out(2 * i + 1, 1)
            count(2 * i)
        count(ROUNDS - 1)
        dve.wait_ge(y_counted.sem, ROUNDS)
        v.bn_aggr(bn_mv[:, :], y_stats[:, :]).then_inc(bn_link.sem, 1)
        dve.wait_ge(bn_pool.sem, 2)
        v.tensor_tensor(bn_s[:, :], bn_r[:, :], colv["L0_tok_gamma"][:, :], ALU.mult).then_inc(bn_link.sem, 1)
        dve.wait_ge(bn_link.sem, 2)
        v.tensor_tensor(bn_m[:, :], bn_mv[:, 0:1], bn_s[:, :], ALU.mult).then_inc(bn_link.sem, 1)
        dve.wait_ge(bn_link.sem, 3)
        v.tensor_tensor(bn_c[:, :], colv["L0_tok_beta"][:, :], bn_m[:, :], ALU.subtract).then_inc(bn_ready.sem, 1)

        done, tail_done = [0], [0]

        def link(phase, i, ins):
            done[0] += 1
            ins.then_inc(chain.sem, 1)
            hold_apart(dve, chain, phase, i, done[0])

        def tail_link(phase, i, ins):
            tail_done[0] += 1
            ins.then_inc(tail_chain.sem, 1)
            hold_apart(dve, tail_chain, phase, i, tail_done[0])

        def chain_ends(phase, done, chain):
            assert done[0] == chain.growth[phase], (phase, done[0])
            done[0] = 0

        def norm_stats(phase, i, k, src, counted=ln_stats, given=ln_aggr):
            for t in range(TILES):
                last = v.bn_stats(ln_st[:, t, :], src[t])
            last.then_inc(counted.sem, 1)
            hold_apart(dve, counted, phase, i, k + 1)
            for t in range(TILES):
                last = v.bn_aggr(ln_mv[:, t, :], ln_st[:, t, :])
            last.then_inc(given.sem, 1)

        def norm_apply(phase, i, k, src, dst, root=ln_rstd, out_=ln_out):
            hold(dve, root, phase, i, k + 1)
            for t in range(TILES):
                last = v.tensor_scalar(dst[:, t, :], src[t], ln_mv[:, t, 0:1], ln_r[:, t:t + 1], ALU.subtract, ALU.mult)
            last.then_inc(out_.sem, 1)
            hold(dve, out_, phase, i, k + 1)

        def norm_weighted(phase, i, k, src, weight, dst, given, out_):
            hold_apart(dve, given, phase, i, k + 1)
            for t in range(TILES):
                last = v.scalar_tensor_tensor(dst[:, t, :], src[t], ln_mv[:, t, 0:1], weight[:, :], ALU.subtract, ALU.mult)
            last.then_inc(out_.sem, 1)
            hold_apart(dve, out_, phase, i, k + 1)

        def norm(phase, i, k, src, dst):
            norm_stats(phase, i, k, src)
            norm_apply(phase, i, k, src, dst)

        def norm_again(phase, i, j, src, dst):
            hold_apart(dve, again_rstd, phase, i, j + 1)
            v.tensor_tensor(dst[:, :, :], src[:, :, :], bc(again_r[:, :], 2, [TOK, TILES, D]), ALU.mult).then_inc(again_out.sem, 1)

        def tiles(x):
            return [x[:, t, :] for t in range(TILES)]

        def key_group(phase, i, k, dst, ps, bias):
            hold(dve, k_psum, phase, i, k + 1)
            src = ps[:, 0:PAIR]
            ins = v.tensor_copy(dst, src) if bias is None else v.tensor_scalar(dst, src, bias, None, ALU.add)
            ins.then_inc(k_ready.sem, 1)

        def split_group(i, k, p, dst, ps, rows):
            hold(dve, high_ready[p], "B", i, k + 1)
            v.scalar_tensor_tensor(dst, high_of[p][:, :], low_rows[:, rows:rows + 1], ps[:, 0:PAIR], ALU.mult, ALU.add).then_inc(
                (qs_ready, k_ready)[p].sem, 1)

        def mask(phase, i, off, H, kT, m):
            b, n = m // H, m % H
            if m >= 4:
                hold(dve, scored, phase, i, off + m - 3)
            v.tensor_scalar(k_head[m % 4][:, :], kT[:, n // 4, b * SEQ:(b + 1) * SEQ], head_rows[:, n % 4:n % 4 + 1], None,
                            ALU.mult).then_inc(k_masked.sem, 1)

        def first_masks(phase, i, off, H, kT, k_ready_n):
            hold(dve, k_ready, phase, i, k_ready_n)
            for m in range(4):
                mask(phase, i, off, H, kT, m)

        def attention(phase, i, off, H, vd, kT, o, causal_, beside=None):
            steps = 2 * H
            group0 = off // 4

            def maximum(m):
                hold(dve, scored, phase, i, off + m + 1)
                s = psS[m % S_RING]
                if causal_:
                    v.tensor_reduce(nmax[:, m % 4, 0:1], s[0:TOK, 0:TOK], AX.X, ALU.max, negate=True)
                    v.tensor_reduce(nmax[:, m % 4, 1:2], s[0:TOK, 256:256 + SEQ], AX.X, ALU.max, negate=True).then_inc(maxed.sem, 1)
                else:
                    v.tensor_reduce(nmax[:, m % 4, :], s[0:TOK, :].rearrange("p (t k) -> p t k", t=2)[:, :, 0:SEQ],
                                    AX.X, ALU.max, negate=True).then_inc(maxed.sem, 1)

            def divide(m):
                gr = m // 4
                if phase == "B":
                    hold(dve, sums_back, phase, i, group0 + gr + 1)
                    ps = psT[0][0:TOK, 0:2 * P].rearrange("p (t n d) -> p n t d", n=4, t=2)
                else:
                    hold(dve, mixed, phase, i, off + m + 1)
                    ps = psO[0:TOK, 0:8 * (vd + 1)].rearrange("p (n t d) -> p n t d", n=4, t=2)
                rd = rden[:, gr % 2, :].rearrange("p (n t) -> p n t", n=4)
                v.reciprocal(rd, ps[:, :, :, vd]).then_inc(recip.sem, 1)
                hold(dve, recip, phase, i, group0 + gr + 1)
                b, n0 = m // H, m % H - 3
                dst = o[:, 2 * b:2 * b + 2, n0 * vd:(n0 + 4) * vd].rearrange("p t (n d) -> p n t d", n=4)
                v.tensor_tensor(dst, ps[:, :, :, 0:vd], bc(rd, 3, [TOK, 4, 2, vd]), ALU.mult).then_inc(normed.sem, 1)

            maximum(0)
            maximum(1)
            for m in range(steps):
                if m + 4 < steps and kT is not None:
                    mask(phase, i, off, H, kT, m + 4)
                if m + 2 < steps:
                    maximum(m + 2)
                if m % 2 == 0 and not (phase == "B" and off == 0):
                    take_turned(dve, lambda eng, dst, src: v.tensor_copy(dst, src), phase, i, off, m, causal_)
                if phase == "B":
                    if m >= 5 and m % 4 == 1:
                        divide(m - 2)
                elif m >= 1 and (m - 1) % 4 == 3:
                    divide(m - 1)
                if beside is not None:
                    beside(m)
            divide(steps - 1)

        def before_head(i):
            hold(dve, h_psum, "B", i, 1)
            v.tensor_copy(h[:, :, :], psO[0:TOK, :].rearrange("p (t d) -> p t d", t=TILES)).then_inc(h_ready.sem, 1)
            hold_apart(dve, h_ready, "B", i, 1)
            norm_stats("B", i, 0, tiles(h))

        def head_of_round(i, m):
            if m == 0:
                norm_apply("B", i, 0, tiles(h), u)
            if m == HEAD_FM - 1:
                norm_again("B", i, 0, u, n_)
            if m - HEAD_Q - 1 in range(8):
                group, p = divmod(m - HEAD_Q - 1, 2)
                split_group(i, group, p, (qs0, ks0)[p][:, group, :], (psG, psS[3])[p], p)
            if m == HEAD_V + 1:
                hold(dve, v_psum, "B", i, 1)
                v.tensor_copy(v17[:, :, :, 0:VD0], psG[0:TOK, :].rearrange("p (t n d) -> p t n d", t=TILES, d=VD0)).then_inc(v_ready.sem, 1)

        row = lambda n: bc(rowb[n][:, :], 1, [TOK, TILES, D])
        pairs = [TOK, TILES * TOP, E0]
        ix8 = ixf[:, :, :].rearrange("p t k -> p (t k)")

        def tail_of_round(i, m):
            if m == 0:
                tail_done[0] = 0
            if m == 4:
                hold(dve, tail_proj, "B", i, 1)
                tail_link("B", i, v.tensor_tensor(um_[:, :, :], um_[:, :, :], psG[0:TOK, :].rearrange("p (t d) -> p t d", t=TILES), ALU.add))
                norm_stats("B", i, 0, tiles(um_), tail_stats, tail_aggr)
            if m == 5:
                norm_weighted("B", i, 0, tiles(um_), rowb["L0_ffn_ln2_g"], n_, tail_aggr, tail_out)
            if m == TAIL_X2:
                hold(dve, tail_rstd, "B", i, 1)
                for t in range(TILES):
                    last = v.scalar_tensor_tensor(x2[:, t, :], n_[:, t, :], ln_r[:, t:t + 1], rowb["L0_ffn_ln2_b"][:, :], ALU.mult, ALU.add)
                last.then_inc(x2_ready.sem, 1)
                hold_apart(dve, x2_ready, "B", i, 1)
            if m == TAIL_X2 + 1:
                v.tensor_tensor(hx_all[:, bass.ds(i * (TILES * D), TILES * D)], hm_[:, :, :].rearrange("p t d -> p (t d)"),
                                um_[:, :, :].rearrange("p t d -> p (t d)"), ALU.add)
            if m == TAIL_TOP - 1:
                hold(dve, route_psum, "B", i, 1)
                tail_link("B", i, v.tensor_copy(lg[:, :, :], psG[0:TOK, 0:TILES * E0].rearrange("p (t e) -> p t e", t=TILES)))
                for t in range(TILES):
                    last = v.max(mx[:, t, :], lg[:, t, :])
                tail_link("B", i, last)
            if m == TAIL_TOP:
                v.tensor_tensor(dlt[:, :], mx[:, :, 1], mx[:, :, 0], ALU.subtract).then_inc(top_diff.sem, 1)
                for t in range(TILES):
                    last = v.max_index(ix[:, t, :], mx[:, t, :], lg[:, t, :])
                tail_link("B", i, last)
                tail_link("B", i, v.tensor_copy(ixf[:, :, :], ix[:, :, 0:TOP]))
            if m == TAIL_TOP + 1:
                tail_link("B", i, v.tensor_tensor(hot[:, :, :, :].rearrange("p t k e -> p (t k) e"), bc(iota_f[0:TOK, :], 1, pairs), bc(ix8, 2, pairs), ALU.is_equal))
                v.tensor_tensor(hots[:, :, :], hot[:, :, 0, :], hot[:, :, 1, :], ALU.add).then_inc(hot_ready.sem, 1)
            if m == TAIL_RANK:
                gates(dve, v, "B", i, tail_link)
            if m == TAIL_RANK + 1:
                hold(dve, rank_psum, "B", i, 1)
                tail_link("B", i, v.tensor_tensor(pos_e[:, :, :], psG[0:TOK, 0:TILES * E0].rearrange("p (t e) -> p t e", t=TILES),
                                                  bc(carry[0:TOK, :], 1, [TOK, TILES, E0]), ALU.add))
                v.tensor_tensor(carry[:, :], carry[:, :], psG[0:TOK, TILES * E0:(TILES + 1) * E0], ALU.add)
            if m == TAIL_RANK + 2:
                tail_link("B", i, v.tensor_tensor(pos_h[:, :, :, :], hot[:, :, :, :], bc(pos_e[:, :, :], 2, [TOK, TILES, TOP, E0]), ALU.mult))
            if m == TAIL_RANK + 3:
                tail_link("B", i, v.tensor_reduce(pos[:, :], pos_h[:, :, :, :].rearrange("p t k e -> p (t k) e"), AX.X, ALU.add))
            if m == TAIL_RANK + 4:
                v.tensor_scalar(slot_l[:, :], ix8, float(CAP), float(CAP - 1), ALU.mult, ALU.add)
                v.tensor_scalar(keep[:, :], pos[:, :], float(CAP), None, ALU.is_lt)
                tail_link("B", i, v.scalar_tensor_tensor(slot_f[:, :], ix8, float(CAP), pos[:, :], ALU.mult, ALU.add))
                tail_link("B", i, v.tensor_scalar(drop_f[:, :], keep[:, :], -float(DROPPED), float(DROPPED), ALU.mult, ALU.add))
            if m == TAIL_RANK + 5:
                tail_link("B", i, v.tensor_tensor(slot_s[:, :], slot_f[:, :], drop_f[:, :], ALU.add))
                v.tensor_copy(slot_u[:, :], slot_s[:, :]).then_inc(slots_ready.sem, 1)
                tail_link("B", i, v.tensor_tensor(slot_l[:, :], slot_f[:, :], slot_l[:, :], ALU.min))
            if m == TAIL_RANK + 6:
                v.tensor_copy(slots_all[:, bass.ds(i * (TILES * TOP), TILES * TOP)], slot_l[:, :])
                v.tensor_tensor(gates_all[:, bass.ds(i * (TILES * TOP), TILES * TOP)], gate[:, :, :].rearrange("p t k -> p (t k)"),
                                keep[:, :], ALU.mult).then_inc(round_done.sem, 1)
                chain_ends("B", tail_done, tail_chain)

        def piece_of_difference(i, j):
            b, v0, v1 = PIECES[j]
            four = [TOK, 2, v1 - v0, VD0]
            pick = lambda x: x.rearrange("p (t n) d -> p t n d", t=2)[:, :, v0:v1]
            rows = slice(2 * b * V0, (2 * b + 2) * V0)
            hold(dve, normed, "B", i, H0 * b // 4 + 2 * v1 // 4)
            for t in (2 * b, 2 * b + 1):
                pair = o_all[:, t, 2 * v0 * VD0:2 * v1 * VD0].rearrange("p (n two d) -> p n two d", two=2, d=VD0)
                last = v.scalar_tensor_tensor(oc[:, t * V0 + v0:t * V0 + v1, :], pair[:, :, 1, :], neg_lam[:, :], pair[:, :, 0, :], ALU.mult, ALU.add)
            link("B", i, last)
            link("B", i, v.tensor_tensor(pick(ocs[:, rows, :]), pick(oc[:, rows, :]), pick(oc[:, rows, :]), ALU.mult))
            one = lambda x: x[:, rows].rearrange("p (t n) -> p t n", t=2)[:, :, v0:v1]
            link("B", i, v.tensor_reduce(one(ms), pick(ocs[:, rows, :]), AX.X, ALU.add))
            v.tensor_scalar(one(ms1), one(ms), 1.0 / VD0, None, ALU.mult).then_inc(diff_ms.sem, 1)

        def piece_scaled(i, j):
            b, v0, v1 = PIECES[j]
            hold(dve, diff_r, "B", i, j + 1)
            return v.tensor_tensor(n_[:, 2 * b:2 * b + 2, v0 * VD0:v1 * VD0].rearrange("p t (n d) -> p t n d", d=VD0),
                                   oc[:, 2 * b * V0:(2 * b + 2) * V0, :].rearrange("p (t n) d -> p t n d", t=2)[:, :, v0:v1],
                                   bc(ms[:, 2 * b * V0:(2 * b + 2) * V0].rearrange("p (t n) -> p t n", t=2)[:, :, v0:v1], 3,
                                      [TOK, 2, v1 - v0, VD0]), ALU.mult)

        def round_of_b(i, first, final):
            def beside(m):
                if not first:
                    tail_of_round(i - 1, m)
                if m == 2:
                    link("B", i, v.tensor_tensor(u[:, :, :], u[:, :, :], row("L0_attn_n2_b"), ALU.add))
                if m == 19:
                    piece_of_difference(i, 0)
                if m == 26:
                    piece_of_difference(i, 1)
                if m == 29:
                    piece_scaled(i, 0)
                if m == 31:
                    piece_scaled(i, 1)

            attention("B", i, 0, H0, VD0, None, o_all, False, beside)
            piece_of_difference(i, 2)
            piece_scaled(i, 2).then_inc(diff_out.sem, 1)
            hold(dve, proj_psum, "B", i, 1)
            a_out = [psS[0][0:TOK, t * D:(t + 1) * D] for t in range(TILES)]
            norm_stats("B", i, 1, a_out)
            norm_weighted("B", i, 1, a_out, rowb["L0_attn_n2_w"], n_, ln_aggr, ln_out)
            hold(dve, ln_rstd, "B", i, 2)
            for t in range(TILES):
                last = v.scalar_tensor_tensor(h1[:, t, :], n_[:, t, :], ln_r[:, t:t + 1], u[:, t, :], ALU.mult, ALU.add)
            link("B", i, last)
            norm("B", i, 2, tiles(h1), n_)
            link("B", i, v.tensor_tensor(h[:, :, :], h[:, :, :], h1[:, :, :], ALU.add))
            link("B", i, v.tensor_tensor(h[:, :, :], h[:, :, :], bc(b2m[:, :], 1, [TOK, TILES, D]), ALU.add))
            for c in range(NC_F):
                hold(dve, up_act, "B", i, c + 1)
                v.tensor_tensor(sq[:, c, :], big[:, c, :], big[:, c, :], ALU.mult).then_inc(up_sq.sem, 1)
                if c:
                    hold(dve, up_sq, "B", i, c + 1)
                    link("B", i, v.tensor_tensor(sq[:, 0, :], sq[:, 0, :], sq[:, c, :], ALU.add))
            hold(dve, down_psum, "B", i, 1)
            for j in range(2):
                last = v.tensor_copy(mm[:, 2 * j:2 * j + 2, :], psT[j][0:TOK, 0:2 * (D + 2)].rearrange("p (t d) -> p t d", t=2)[:, :, D:D + 2])
            link("B", i, last)
            link("B", i, v.tensor_tensor(mm2[:, :], mm[:, :, 0], mm[:, :, 0], ALU.mult))
            v.tensor_tensor(mm2[:, :], mm[:, :, 1], mm2[:, :], ALU.subtract).then_inc(down_var.sem, 1)
            hold(dve, down_r, "B", i, 1)
            for t in range(TILES):
                at = (t % 2) * (D + 2)
                last = v.scalar_tensor_tensor(hm_[:, t, :], psT[t // 2][0:TOK, at:at + D], ln_r[:, t:t + 1], h[:, t, :], ALU.mult, ALU.add)
            link("B", i, last)
            chain_ends("B", done, chain)
            norm("B", i, 3, tiles(hm_), um_)
            norm_again("B", i, 1, um_, n_)
            if not final:
                before_head(i + 1)
            for group in range(4):
                split_group(i, 4 + group, 0, qs1[:, group, :], psS[2 * (group % 2)], 2)
                split_group(i, 4 + group, 1, ks1[:, group, :], psS[2 * (group % 2) + 1], 3)
            hold(dve, v_psum, "B", i, 2)
            v.tensor_copy(v17m[:, :, :, 0:HD1], psG[0:TOK, :].rearrange("p (t n d) -> p t n d", t=TILES, d=HD1)).then_inc(v_ready.sem, 1)
            if not first:
                hold(dve, scattered, "B", i - 1, 16 * TILES * TOP)
            attention("B", i, 2 * H0, H1, HD1, None, om, False, None if final else lambda m: head_of_round(i + 1, m))

        v.memset(v17m[:, :, :, HD1:HD1 + 1], 1.0)
        before_head(0)
        for m in range(2 * H1 + 1):
            head_of_round(0, m)
        round_of_b(0, True, False)
        with dve.Fori(1, ROUNDS - 1) as i:
            round_of_b(i, False, False)
        round_of_b(ROUNDS - 1, False, True)
        for m in range(2 * H0 + 1):
            tail_of_round(ROUNDS - 1, m)

        def rows_turned(i, s):
            p, q = s % 2, s // 2
            hold(dve, xe_psum[p], "C", i, q + 1)
            v.tensor_copy(xeT[p][:, :], (psG, psO)[p][:, 0:CAP]).then_inc(xe_T[p].sem, 1)

        def expert_steps(i, ahead):
            for s in range(N):
                if s + 2 < N or ahead:
                    rows_turned(i, s + 2)
                p, q = s % 2, s // 2
                hold(dve, ed_psum[s], "C", i, 1)
                hold(dve, ye_out[p], "C", i, 16 * q)
                v.tensor_copy(ye[p][:, :, :], psT[p][0:TOK, 0:2 * D].rearrange("p (t d) -> p t d", t=2)).then_inc(ye_ready[p].sem, 1)

        links = [0]

        def split_link(ins):
            links[0] += 1
            ins.then_inc(b2_link.sem, 1)
            dve.wait_ge(b2_link.sem, links[0])

        left, sum_ = b2_left
        for half in range(2):
            es = slice(half * E1 // 2, (half + 1) * E1 // 2)
            b, high = b2_rows[:, es, :], b2_split[:, es, :]
            split_link(v.tensor_copy(high, b))
            split_link(v.tensor_tensor(left, b, high, ALU.subtract))
            split_link(v.tensor_copy(b2_part[:, :, :], left))
            split_link(v.tensor_tensor(left, left, b2_part[:, :, :], ALU.subtract))
            split_link(v.tensor_scalar(left, left, ident[0:SPLIT, 2:3], None, ALU.mult))
            split_link(v.scalar_tensor_tensor(sum_, b2_part[:, :, :], ident[0:SPLIT, 1:2], left, ALU.mult, ALU.add))
            split_link(v.scalar_tensor_tensor(high, high, ident[0:SPLIT, 0:1], sum_, ALU.mult, ALU.add))

        rows_turned(0, 0)
        rows_turned(0, 1)
        expert_steps(0, True)
        with dve.Fori(1, C_ROUNDS - 1) as i:
            expert_steps(i, True)
        expert_steps(C_ROUNDS - 1, False)

        v.memset(v33[:, :, :, HD2:HD2 + 1], 1.0)
        v.tensor_copy(slot_c[:, :], slots_all[:, 0:TILES * TOP]).then_inc(idx_ready.sem, 1)

        def next_head(i, e):
            if e == 0:
                v.tensor_copy(gate_c[:, :], gates_all[:, bass.ds(i * (TILES * TOP), TILES * TOP)])
                v.tensor_copy(h[:, :, :].rearrange("p t d -> p (t d)"), hx_all[:, bass.ds(i * (TILES * D), TILES * D)]).then_inc(next_chain.sem, 1)
                hold_apart(dve, gathered, "D", i, 0)
                v.tensor_copy(slot_c[:, :], slots_all[:, bass.ds((i + 1) * (TILES * TOP), TILES * TOP)]).then_inc(idx_ready.sem, 1)
                hold_apart(dve, next_chain, "D", i, 1)
            if e in (0, 1):
                for t in range(TILES):
                    c = t * TOP + e
                    last = v.scalar_tensor_tensor(h[:, t, :], gy[:, c, :], gate_c[:, c:c + 1], h[:, t, :], ALU.mult, ALU.add)
                if e == 0:
                    last.then_inc(next_chain.sem, 1)
                    hold_apart(dve, next_chain, "D", i, 2)
                else:
                    last.then_inc(gy_used.sem, 1)
                    hold_apart(dve, gy_used, "D", i, 1)
            if e == NEXT_NORM - 1:
                norm_stats("D", i, 0, tiles(h))
            if e == NEXT_NORM:
                norm_apply("D", i, 0, tiles(h), u)

            if e == E1 - 2:
                first_masks("D", i, 0, H2, kT, 4)

        def next_keys(i, e):
            if NEXT_Q <= e < NEXT_Q + 4:
                group = e - NEXT_Q
                key_group("D", i, group, kT[:, group, :], psG, kb2[:, group:group + 1])
            if NEXT_Q + 4 <= e < NEXT_Q + 8:
                t = e - NEXT_Q - 4
                hold(dve, v_psum, "D", i, t + 1)
                v.tensor_tensor(v33[:, t, :, 0:HD2], psG[0:TOK, :].rearrange("p (n d) -> p n d", d=HD2),
                                vb2[:, :].rearrange("p (n d) -> p n d", d=HD2), ALU.add).then_inc(v_ready.sem, 1)

        def round_of_d(i, final):
            def beside_attention(m):
                if m == 1:
                    link("D", i, v.tensor_tensor(h[:, :, :], h[:, :, :], bc(rowb["L1_attn_bo"][:, :], 1, [TOK, TILES, D]), ALU.add))

            attention("D", i, 0, H2, HD2, kT, o_all, True, beside_attention)
            hold(dve, proj_psum, "D", i, 1)
            link("D", i, v.tensor_tensor(h[:, :, :], h[:, :, :], psG[0:TOK, :].rearrange("p (t d) -> p t d", t=TILES), ALU.add))
            norm("D", i, 1, tiles(h), u)
            hold(dve, gate_psum, "D", i, 1)
            link("D", i, v.tensor_tensor(s16[:, :, :], psG[0:TOK, 0:TILES * E1].rearrange("p (t e) -> p t e", t=TILES),
                                         bc(rowb["L1_ffn_gate_b"][:, :], 1, [TOK, TILES, E1]), ALU.add))
            for t in range(TILES):
                last = v.max(mx[:, t, :], s16[:, t, :])
            link("D", i, last)
            v.tensor_tensor(dlt[:, :], mx[:, :, 1], mx[:, :, 0], ALU.subtract).then_inc(top_diff.sem, 1)
            for t in range(TILES):
                last = v.max_index(ix[:, t, :], mx[:, t, :], s16[:, t, :])
            link("D", i, last)
            link("D", i, v.tensor_copy(ixf[:, :, :], ix[:, :, 0:TOP]))
            pairs = [TOK, TILES * TOP, E1]
            link("D", i, v.tensor_tensor(hot1[:, :, :, :].rearrange("p t k e -> p (t k) e"), bc(iota_f[0:TOK, 0:E1], 1, pairs),
                                         bc(ixf[:, :, :].rearrange("p t k -> p (t k)"), 2, pairs), ALU.is_equal))
            gates(dve, v, "D", i, link)
            link("D", i, v.tensor_tensor(comb2[:, :, :, :].rearrange("p t k e -> p (t k) e"), hot1[:, :, :, :].rearrange("p t k e -> p (t k) e"),
                                         bc(gate[:, :, :].rearrange("p t k -> p (t k)"), 2, pairs), ALU.mult))
            v.tensor_tensor(comb[:, :, :], comb2[:, :, 0, :], comb2[:, :, 1, :], ALU.add).then_inc(comb_ready.sem, 1)
            hold(dve, combT_psum, "D", i, 1)
            v.tensor_copy(combT[:, :], psG[0:E1, 0:PAIR]).then_inc(combT_ready.sem, 1)
            hold(dve, beta_psum, "D", i, 1)
            hold(dve, stored, "D", i, 0)
            v.tensor_tensor(acc[:, :, :], h[:, :, :], psG[0:TOK, :].rearrange("p (t d) -> p t d", t=TILES), ALU.add).then_inc(acc_ready.sem, 1)

            def stats(e):
                s = e % 2
                if e >= 2:
                    hold(dve, me_scale, "D", i, e - 1)
                hold(dve, md_psum, "D", i, e + 1)
                for t in range(TILES):
                    last = v.bn_stats(e_st[s][:, t, :], ps_down[e % 3][0:TOK, t * D:(t + 1) * D])
                last.then_inc(me_stats.sem, 1)
                hold_apart(dve, me_stats, "D", i, e + 1)
                for t in range(TILES):
                    last = v.bn_aggr(e_mv[s][:, t, :], e_st[s][:, t, :])
                last.then_inc(me_var.sem, 1)

            stats(0)
            for e in range(E1):
                s = e % 2
                if not final:
                    next_keys(i + 1, e + 1)
                if e + 1 < E1:
                    stats(e + 1)
                hold(dve, me_scale, "D", i, e + 1)
                hold(dve, me_acc, "D", i, max(e - 1, 0))
                for t in range(TILES):
                    last = v.tensor_scalar(nrm[s][:, t, :], ps_down[e % 3][0:TOK, t * D:(t + 1) * D], e_mv[s][:, t, 0:1], e_s[s][:, t:t + 1],
                                           ALU.subtract, ALU.mult)
                last.then_inc(me_norm.sem, 1)
                hold(dve, me_norm, "D", i, e + 1)
                v.tensor_tensor(nrm[s][:, :, :], nrm[s][:, :, :], bc(gamma_b[:, e, :], 1, [TOK, TILES, D]), ALU.mult).then_inc(me_g.sem, 1)
                if not final:
                    next_head(i + 1, e)
            chain_ends("D", done, chain)

        for e in range(E1):
            next_head(0, e)
            next_keys(0, e + 1)
        round_of_d(0, False)
        with dve.Fori(1, ROUNDS - 1) as i:
            round_of_d(i, False)
        round_of_d(ROUNDS - 1, True)

    @block.tensor
    def _(pe):
        mmul = nc.tensor.matmul
        pe.wait_ge(const_made.sem, CONSTS)
        pe.wait_ge(loaded.sem, 16 * len(loads))
        for k, (src, dst, hd) in enumerate(turns):
            rows, cols = src.shape[1], src.shape[0]
            if k >= RING:
                pe.wait_ge(prep_done.sem, k - RING + 1)
            nc.tensor.transpose(psS[k % RING][0:rows, 0:cols], src, ident[0:cols, 0:cols]).then_inc(prep_psum.sem, 1)
        pe.wait_ge(prep_done.sem, N_TURNS)
        pe.wait_ge(prep_pool.sem, 1)
        for c in range(NC_F):
            last = mmul(psS[0][:, 0:D], frac[:, :], w2w[:, c, :], start=c == 0, stop=c == NC_F - 1)
        last.then_inc(prep_psum.sem, 1)
        for c in range(NC_F):
            last = mmul(psS[1][0:1, 0:D], colc["L0_attn_mln2_b"][:, c:c + 1], w2raw[:, c, :], start=c == 0, stop=c == NC_F - 1)
        last.then_inc(prep_psum.sem, 1)
        pe.wait_ge(prep_done.sem, STEP_B2)
        mmul(psS[2][0:TOK, 0:D], ones[0:1, 0:TOK], b2m_row[:, :], start=True, stop=True).then_inc(prep_psum.sem, 1)
        for n in range(H2):
            pe.wait_ge(prep_done.sem, max(STEP_B2B, STEP_QKV + n - RING))
            for x in range(3):
                last = mmul(psS[n % RING][:, x * HD2:(x + 1) * HD2], wl[:, n, :], qkv1[:, x, n, :], start=True, stop=True)
            last.then_inc(prep_psum.sem, 1)
        for x, ps in ((0, psT[0]), (1, psT[1])):
            for n in range(H2):
                j, g = n % 4, n // 4
                last = mmul(ps[32 * j:32 * j + 32, g:g + 1], qkv1[:, x, n, :], blt[:, n:n + 1], start=True, stop=True)
            last.then_inc(prep_psum.sem, 1)
        for n in range(H2):
            last = mmul(psO[0:1, n * HD2:(n + 1) * HD2], blt[:, n:n + 1], qkv1[:, 2, n, :], start=True, stop=True)
        last.then_inc(prep_psum.sem, 1)
        pe.wait_ge(prep_done.sem, STEP_VB)
        mmul(psG[0:TOK, :], ones[0:1, 0:TOK], vb_row[:, :], start=True, stop=True).then_inc(prep_psum.sem, 1)
        pe.wait_ge(ready.sem, 1)

        def turn_windows(i, r):
            hold(pe, win_in[r], "A", i - r, 16 * TILES)
            hold(pe, win_T, "A", i - 2, 3)
            for c in range(3):
                cols = P if c < 2 else WIN - 2 * P
                for t in range(TILES):
                    last = nc.tensor.transpose(win_banks[r][c][0:cols, tile(t)], xw[r][:, t, c * P:c * P + cols], ident[0:TOK, 0:TOK])
                last.then_inc(win_psum.sem, 1)

        def convolve(i, r):
            hold(pe, win_T, "A", i, 3)
            hold(pe, y_ready, "A", i, 0)
            for c in range(3):
                rows = P if c < 2 else WIN - 2 * P
                last = mmul(psG[:, 0:PAIR], w_tok[0:rows, c, :], win_turned[r][0:rows, c, :], start=c == 0, stop=c == 2)
            last.then_inc(conv_psum.sem, 1)

        turn_windows(0, 0)
        turn_windows(1, 1)
        convolve(0, 0)
        with pe.Fori(1, ROUNDS // 2) as i:
            turn_windows(2 * i, 0)
            convolve(2 * i - 1, 1)
            turn_windows(2 * i + 1, 1)
            convolve(2 * i, 0)
        convolve(ROUNDS - 1, 1)

        def turn_to_features(phase, i, src, turned_=fm_psum):
            for t in range(TILES):
                last = nc.tensor.transpose(psG[:, tile(t)], src[:, t, :], ident[0:TOK, 0:TOK])
            last.then_inc(turned_.sem, 1)

        def attention(phase, i, off, H, hd, vd, q, k, v_of, causal_, heads_a_value, beside=None):
            steps = 2 * H
            ring = S_RING

            def scores(m):
                b, n = m // H, m % H
                g = n // 4
                if k is None:
                    hold(pe, k_masked, phase, i, off + m + 1)
                if m >= ring:
                    hold(pe, probs, phase, i, off + m - ring + 1)
                bank = psS[m % ring]
                for t in range(2):
                    keys = TOK if causal_ and t == 0 else SEQ
                    at = t * 256
                    if k is None:
                        last = mmul(bank[0:TOK, at:at + keys], q[:, g, tile(2 * b + t)], k_head[m % 4][:, 0:keys], start=True, stop=False)
                    else:
                        g, j = n * 4 * hd // P, n * 4 * hd % P
                        last = mmul(bank[0:TOK, at:at + keys], q[j:j + 3 * hd, g, tile(2 * b + t)],
                                    k[j:j + 3 * hd, g, b * SEQ:(b + 1) * SEQ], start=True, stop=True)
                    if causal_:
                        last = mmul(bank[0:TOK, at + t * TOK:at + (t + 1) * TOK], ident_h[0:TOK, 0:TOK], causal_h[:, :], start=False, stop=True)
                last.then_inc(scored.sem, 1)

            def turn(m):
                hold(pe, probs, phase, i, off + m + 1)
                if m >= 2:
                    out_, before_ = taken(phase, off, m)
                    hold(pe, out_, phase, i, before_)
                if phase == "B" and m >= 6 and m % 4 == 2:
                    hold(pe, normed, phase, i, off // 4 + (m - 6) // 4 + 1)
                for c in range(2):
                    for t in range(2):
                        if causal_ and t < c:
                            continue
                        last = nc.tensor.transpose(psT[m % 2][0:TOK, c * SEQ + t * TOK:c * SEQ + (t + 1) * TOK],
                                                   prob[m % 2][:, t, c * TOK:(c + 1) * TOK], ident[0:TOK, 0:TOK])
                last.then_inc(turned.sem, 1)

            def mix(m):
                b, n = m // H, m % H
                out_, before_ = taken(phase, off, m)
                hold(pe, out_, phase, i, before_ + 1)
                if phase == "B":
                    if m % 4 == 0 and m >= 4:
                        hold(pe, sums_out, phase, i, (off + m) // 4)
                    j = 32 * (n % 4)
                    for c in range(2):
                        last = mmul(psO[j:j + vd + 1, 0:SEQ], v_of(2 * b + c, n // heads_a_value), probT[m % 2][:, c * SEQ:(c + 1) * SEQ],
                                    start=c == 0, stop=c == 1)
                    last.then_inc(mixed.sem, 1)
                    return
                if m % 4 == 0 and m >= 4:
                    hold(pe, normed, phase, i, (off + m) // 4)
                for t in range(2):
                    last_c = 0 if causal_ and t == 0 else 1
                    at = ((n % 4) * 2 + t) * (vd + 1)
                    for c in range(last_c + 1):
                        last = mmul(psO[0:TOK, at:at + vd + 1], probT[m % 2][:, c * SEQ + t * TOK:c * SEQ + (t + 1) * TOK],
                                    v_of(2 * b + c, n // heads_a_value), start=c == 0, stop=c == last_c)
                last.then_inc(mixed.sem, 1)

            def sums_to_tokens(gr):
                hold(pe, sums_out, phase, i, off // 4 + gr + 1)
                for t in range(2):
                    last = nc.tensor.transpose(psT[0][0:TOK, t * P:(t + 1) * P], sumsT[gr % 2][:, t * TOK:(t + 1) * TOK], ident[:, :])
                last.then_inc(sums_back.sem, 1)

            for m in range(ring - 1):
                scores(m)
            for m in range(steps):
                if m + ring - 1 < steps:
                    scores(m + ring - 1)
                turn(m)
                if m:
                    mix(m - 1)
                if phase == "B" and m >= 5 and m % 4 == 1:
                    sums_to_tokens((m - 5) // 4)
                if beside is not None:
                    beside(m)
            mix(steps - 1)
            if phase == "B":
                sums_to_tokens(steps // 4 - 1)

        def v_small(phase, i, k, w):
            for t in range(TILES):
                last = mmul(psG[0:TOK, t * D:(t + 1) * D], xT[:, tile(t)], w[:, :], start=True, stop=True)
            last.then_inc(v_psum.sem, 1)

        def out_projection(ps, w, made):
            for t in range(TILES):
                last = mmul(ps[0:TOK, t * D:(t + 1) * D], xT[:, tile(t)], w[:, :], start=True, stop=True)
            last.then_inc(made.sem, 1)

        def before_head(i):
            hold(pe, hT_ready, "B", i, 1)
            for t in range(TILES):
                last = nc.tensor.transpose(psO[0:TOK, t * D:(t + 1) * D], hT[:, tile(t)], ident[:, :])
            last.then_inc(h_psum.sem, 1)

        def head_of_round(i, m):
            if m == HEAD_FM:
                hold(pe, again_out, "B", i, 1)
                turn_to_features("B", i, n_)
            if m - HEAD_Q in range(8):
                group, p = divmod(m - HEAD_Q, 2)
                if m == HEAD_Q:
                    hold(pe, fm_ready, "B", i, 1)
                if p == 0:
                    hold(pe, qs_ready, "B", i, group)
                    mmul(psG[:, 0:PAIR], wq0[:, group, :], xT[:, :], start=True, stop=True).then_inc(q_psum.sem, 1)
                else:
                    hold(pe, k_ready, "B", i, group)
                    mmul(psS[3][:, 0:PAIR], wk0[:, group, :], xT[:, :], start=True, stop=True).then_inc(k_psum.sem, 1)
            if m == HEAD_V:
                hold(pe, qs_ready, "B", i, 4)
                v_small("B", i, 1, wv0)

        def tail_of_round(i, m):
            if m == 0:
                hold(pe, normed, "B", i, HEADS_B // 4)
                turn_to_features("B", i, om, tail_fm_psum)
            if m == 3:
                hold(pe, tail_fm_ready, "B", i, 1)
                out_projection(psG, wo1, tail_proj)
            if m == TAIL_X2 + 1:
                hold(pe, x2_ready, "B", i, 1)
                turn_to_features("B", i, x2, tail_fm_psum)
            if m == TAIL_X2 + 4:
                hold(pe, tail_fm_ready, "B", i, 2)
                for t in range(TILES):
                    last = mmul(psG[0:TOK, t * E0:(t + 1) * E0], xT[:, tile(t)], wr[:, :], start=True, stop=True)
                last.then_inc(route_psum.sem, 1)
            if m == TAIL_RANK:
                hold(pe, hot_ready, "B", i, 1)
                for t in range(TILES):
                    for t2 in range(t + 1):
                        lhs = before_h if t2 == t else all_h
                        mmul(psG[0:TOK, t * E0:(t + 1) * E0], lhs[:, :], hots[:, t2, :], start=t2 == 0, stop=t2 == t)
                for t in range(TILES):
                    last = mmul(psG[0:TOK, TILES * E0:(TILES + 1) * E0], all_h[:, :], hots[:, t, :], start=t == 0, stop=t == TILES - 1)
                last.then_inc(rank_psum.sem, 1)

        def round_of_b(i, first, final):
            hold(pe, qs_ready, "B", i, 4)
            hold(pe, k_ready, "B", i, 4)
            hold(pe, v_ready, "B", i, 1)
            if not first:
                hold(pe, normed, "B", i - 1, HEADS_B // 4)
            attention("B", i, 0, H0, HD0, VD0, qs0, ks0, lambda t, n: v17[:, t, n, :], False, H0 // V0,
                      None if first else lambda m: tail_of_round(i - 1, m))
            hold(pe, diff_out, "B", i, 1)
            turn_to_features("B", i, n_)
            hold(pe, fm_ready, "B", i, 2)
            out_projection(psS[0], wo0, proj_psum)
            hold(pe, ln_out, "B", i, 3)
            turn_to_features("B", i, n_)
            hold(pe, fm_ready, "B", i, 3)
            for c in range(NC_F):
                mmul(psS[c][:, 0:PAIR], w1m[:, c * P:(c + 1) * P], xT[:, :], start=True, stop=True).then_inc(up_psum.sem, 1)
            if not final:
                before_head(i + 1)
            hold(pe, up_act, "B", i, NC_F)
            for t in range(TILES):
                at = (t % 2) * (D + 2)
                for c in range(NC_F):
                    mmul(psT[t // 2][0:TOK, at:at + D + 1], big[:, c, tile(t)], w2m[:, c, :], start=c == 0, stop=c == NC_F - 1)
            hold(pe, chain, "B", i, SQUARED)
            for t in range(TILES):
                at = (t % 2) * (D + 2)
                last = mmul(psT[t // 2][0:TOK, at + D + 1:at + D + 2], sq[:, 0, tile(t)], frac[:, 0:1], start=True, stop=True)
            last.then_inc(down_psum.sem, 1)
            hold(pe, again_out, "B", i, 2)
            turn_to_features("B", i, n_)
            hold(pe, fm_ready, "B", i, 4)
            v_small("B", i, 2, wv1)
            for group in range(4):
                if group >= 2:
                    hold(pe, qs_ready, "B", i, 4 + group - 1)
                    hold(pe, k_ready, "B", i, 4 + group - 1)
                mmul(psS[2 * (group % 2)][:, 0:PAIR], wq1[:, group, :], xT[:, :], start=True, stop=True).then_inc(q_psum.sem, 1)
                mmul(psS[2 * (group % 2) + 1][:, 0:PAIR], wk1[:, group, :], xT[:, :], start=True, stop=True).then_inc(k_psum.sem, 1)
            hold(pe, qs_ready, "B", i, 8)
            hold(pe, k_ready, "B", i, 8)
            hold(pe, v_ready, "B", i, 2)
            attention("B", i, 2 * H0, H1, HD1, HD1, qs1, ks1, lambda t, n: v17m[:, t, n, :], False, 1,
                      None if final else lambda m: head_of_round(i + 1, m))

        for half in range(2):
            mmul(psO[:, half * P:(half + 1) * P], ident[:, :], ones[:, :], start=True, stop=True)
        before_head(0)
        for m in range(2 * H1 + 1):
            head_of_round(0, m)
        round_of_b(0, True, False)
        with pe.Fori(1, ROUNDS - 1) as i:
            round_of_b(i, False, False)
        round_of_b(ROUNDS - 1, False, True)
        for m in range(2 * H0 + 1):
            tail_of_round(ROUNDS - 1, m)

        pe.wait_ge(round_done.sem, round_done.value("C", 0, 0))

        def rows_to_features(i, s):
            p, q = s % 2, s // 2
            if s < N:
                hold(pe, ew_in[s], "C", i, 16 * 4)
            else:
                hold(pe, ew_in[s - N], "C", i, 2 * 16 * 4)
            hold(pe, xe_T[p], "C", i, q)
            for t in range(2):
                last = nc.tensor.transpose((psG, psO)[p][:, tile(t)], xe[s % N][:, t, :], ident[0:TOK, 0:TOK])
            last.then_inc(xe_psum[p].sem, 1)

        def expert_up(i, s):
            p, q = s % 2, s // 2
            hold(pe, xe_T[p], "C", i, q + 1)
            for half in range(2):
                hold(pe, eu_act[p], "C", i, 2 * q)
                for c in (2 * half, 2 * half + 1):
                    last = mmul(psS[2 * p + half][:, (c % 2) * 256:(c % 2) * 256 + CAP], we1[s % N].rearrange("p (f c) -> p c f", c=NC_F)[:, c, :], xeT[p][:, :],
                                start=True, stop=True)
                last.then_inc(eu_psum[p].sem, 1)

        def expert_down(i, s):
            p, q = s % 2, s // 2
            hold(pe, eu_act[p], "C", i, 2 * q + 2)
            hold(pe, ye_ready[p], "C", i, q)
            for t in range(2):
                for c in range(NC_F):
                    mmul(psT[p][0:TOK, t * D:(t + 1) * D], he[p][:, c, tile(t)], we2[s][:, c, :], start=c == 0, stop=False)
                last = mmul(psT[p][0:TOK, t * D:(t + 1) * D], ones[0:1, 0:TOK], be2[s][:, :], start=False, stop=True)
            last.then_inc(ed_psum[s].sem, 1)

        def expert_round(i, ahead):
            for s in range(N):
                if s + 2 < N or ahead:
                    rows_to_features(i, s + 2)
                if s + 1 < N or ahead:
                    expert_up(i, s + 1)
                expert_down(i, s)

        rows_to_features(0, 0)
        rows_to_features(0, 1)
        expert_up(0, 0)
        expert_round(0, True)
        with pe.Fori(1, C_ROUNDS - 1) as i:
            expert_round(i, True)
        expert_round(C_ROUNDS - 1, False)

        def next_before(i, e):
            if NEXT_Q <= e < NEXT_Q + 4:
                group = e - NEXT_Q
                if group == 0:
                    hold(pe, fm_ready, "D", i, 1)
                else:
                    hold(pe, q_ready, "D", i, group)
                mmul(psG[:, 0:PAIR], wk2[:, group * P:(group + 1) * P], hT[:, :], start=True, stop=True).then_inc(k_psum.sem, 1)
            if NEXT_Q + 4 <= e < NEXT_Q + 8:
                t = e - NEXT_Q - 4
                if t == 0:
                    hold(pe, q_ready, "D", i, 4)
                else:
                    hold(pe, v_ready, "D", i, t)
                mmul(psG[0:TOK, :], hT[:, tile(t)], wv2[:, :], start=True, stop=True).then_inc(v_psum.sem, 1)

        def next_behind(i, e):
            if e == NEXT_NORM + 2:
                hold(pe, ln_out, "D", i, 1)
                turn_to_features("D", i, u)
            if NEXT_Q <= e < NEXT_Q + 4:
                group = e - NEXT_Q
                hold(pe, k_ready, "D", i, group + 1)
                mmul(psG[:, 0:PAIR], wq2[:, group * P:(group + 1) * P], hT[:, :], start=True, stop=True).then_inc(q_psum.sem, 1)

        def round_of_d(i, final):
            hold(pe, k_ready, "D", i, 4)
            hold(pe, v_ready, "D", i, 4)
            def turn_heads(m):
                if CAT <= m < CAT + 2 * 4 and (m - CAT) % 2 == 0:
                    c = (m - CAT) // 2
                    if c == 0:
                        hold(pe, normed, "D", i, HEADS_D // 8)
                    else:
                        hold(pe, cat_T, "D", i, c)
                    for t in range(2):
                        last = nc.tensor.transpose(psS[3][:, tile(t)], o_all[:, t, c * P:(c + 1) * P], ident[0:TOK, 0:TOK])
                    last.then_inc(cat_psum.sem, 1)
                if m in (CAT + 10, CAT + 12):
                    if m == CAT + 10:
                        hold(pe, cat_T, "D", i, 4)
                    project_heads((m - CAT - 10) // 2)

            def project_heads(t):
                for c in range(4):
                    last = mmul(psG[0:TOK, t * D:(t + 1) * D], cat_b[:, c, tile(t)], wo2[:, c, :], start=c == 0, stop=c == 3)
                return last

            attention("D", i, 0, H2, HD2, HD2, qT, None, lambda t, n: v33[:, t, n, :], True, 1, turn_heads)
            hold(pe, normed, "D", i, HEADS_D // 4)
            for c in range(4):
                for t in range(2, TILES):
                    last = nc.tensor.transpose(psS[c][:, tile(t - 2)], o_all[:, t, c * P:(c + 1) * P], ident[0:TOK, 0:TOK])
                last.then_inc(cat_psum.sem, 1)
            hold(pe, cat_T, "D", i, 8)
            for t in range(2, TILES):
                last = project_heads(t)
            last.then_inc(proj_psum.sem, 1)
            hold(pe, ln_out, "D", i, 2)
            turn_to_features("D", i, u)
            hold(pe, fm_ready, "D", i, 2)
            for t in range(TILES):
                last = mmul(psG[0:TOK, t * E1:(t + 1) * E1], xT[:, tile(t)], gate_w[:, :], start=True, stop=True)
            last.then_inc(gate_psum.sem, 1)

            def up(e):
                s = e % 2
                for c in range(2):
                    if e >= 2:
                        hold(pe, mu_act, "D", i, 2 * (e - 2) + c + 1)
                    mmul(psS[2 * s + c][:, 0:PAIR], w1e[:, e, c * P:(c + 1) * P], xT[:, :], start=True, stop=True).then_inc(mu_psum.sem, 1)

            def down(e):
                s = e % 2
                hold(pe, mu_act, "D", i, 2 * e + 2)
                ps = ps_down[e % 3]
                if e >= 3:
                    hold(pe, me_norm, "D", i, e - 2)
                for t in range(TILES):
                    for c in range(2):
                        mmul(ps[0:TOK, t * D:(t + 1) * D], hm[s][:, c, tile(t)], w2e[:, e, c, :], start=c == 0, stop=False)
                    last = mmul(ps[0:TOK, t * D:(t + 1) * D], ones_h[:, :], b2_split[:, e, :], start=False, stop=True)
                last.then_inc(md_psum.sem, 1)

            pe.wait_ge(loaded_e.sem, 16 * len(expert_loads))
            up(0)
            up(1)
            down(0)
            hold(pe, comb_ready, "D", i, 1)
            for t in range(TILES):
                last = nc.tensor.transpose(psG[0:E1, tile(t)], comb[:, t, :], ident[0:TOK, 0:TOK])
            last.then_inc(combT_psum.sem, 1)
            hold(pe, combT_ready, "D", i, 1)
            for t in range(TILES):
                last = mmul(psG[0:TOK, t * D:(t + 1) * D], combT[:, tile(t)], beta_e[:, :], start=True, stop=True)
            last.then_inc(beta_psum.sem, 1)
            for e in range(E1):
                if 1 <= e and e + 1 < E1:
                    up(e + 1)
                if not final:
                    next_before(i + 1, e)
                if e:
                    down(e)
                if not final:
                    next_behind(i + 1, e)

        for e in range(E1):
            next_before(0, e)
            next_behind(0, e)
        round_of_d(0, False)
        with pe.Fori(1, ROUNDS - 1) as i:
            round_of_d(i, False)
        round_of_d(ROUNDS - 1, True)


_OUT = (BATCH, SEQ, D)


def kernel(**inputs):
    import numpy as _np
    import concourse.bacc as _bacc
    from concourse import mybir as _mybir
    from concourse.bass_utils import run_bass_kernel_spmd as _run

    nc = _bacc.Bacc("TRN2", target_bir_lowering=False, num_devices=1)
    arrays, handles = {}, {}
    for name, value in inputs.items():
        a = _np.ascontiguousarray(value)
        arrays["in_" + name] = a
        handles[name] = nc.dram_tensor("in_" + name, a.shape, _mybir.dt.from_np(a.dtype), kind="ExternalInput").ap()
    result = nc.dram_tensor("result", _OUT, _mybir.dt.float32, kind="ExternalOutput").ap()
    build(nc, handles, result)
    r = _run(nc, [arrays], core_ids=[0])
    return r.results[0]["result"]
```
